# Optimizing a Trainium2 kernel written in Bass

```python
import numpy as np
import jax
import jax.numpy as jnp

def _softmax(x, axis=-1):
    return jax.nn.softmax(x, axis=axis)

def _gelu(x):
    return jax.nn.gelu(x, approximate=True)

def _silu(x):
    return jax.nn.silu(x)

def _sigmoid(x):
    return jax.nn.sigmoid(x)

def _layernorm(x, axis=-1, eps=1e-05):
    m = jnp.mean(x, axis=axis, keepdims=True)
    v = jnp.var(x, axis=axis, keepdims=True)
    return (x - m) / jnp.sqrt(v + eps)

def _scatter_add(tgt, idx, src, axis=0):
    return tgt.at[idx].add(src)

def _segment_sum(src, seg, n):
    return jax.ops.segment_sum(src, seg, n)
kernel_name = 'mk_xattn_seq_d1_seqx_r8_bf12a1'

def setup_inputs(seed: int=0):
    np.random.seed(seed)
    _w = jnp.asarray

    def _rec_inputs():
        import jax
        import jax.numpy as jnp
        _rk = jax.random.key(seed)
        x = -0.0002928 + 1 * jax.random.normal(jax.random.fold_in(_rk, 1), (32, 128, 128), jnp.float32)
        _lenS = 128 - jax.random.randint(jax.random.fold_in(_rk, 7), (32,), 0, max(1, 128 // 4) + 1, jnp.int32)
        _lenS2 = 120 - jax.random.randint(jax.random.fold_in(_rk, 8), (32,), 0, max(1, 120 // 4) + 1, jnp.int32)
        _ctx_1024P = jax.random.normal(jax.random.fold_in(_rk, 11), (32, 16, 128), jnp.float32)
        _ctx_1024c = jax.random.dirichlet(jax.random.fold_in(_rk, 511), 0.3 * jnp.ones((16,), jnp.float32), (32, 120))
        _ctx_1024t = jnp.einsum('bsk,bkd->bsd', _ctx_1024c, _ctx_1024P)
        _ctx_1024t = _ctx_1024t * jax.lax.rsqrt(jnp.mean(jnp.square(_ctx_1024t)) + 1e-12) * 0.953939
        ctx_1024 = -1.39393e-06 + 0.999914 * (_ctx_1024t + 0.3 * jax.random.normal(jax.random.fold_in(_rk, 611), (32, 120, 128), jnp.float32))
        return (x, ctx_1024)
    x, ctx_1024 = _rec_inputs()

    def _L0_xattn_setup():
        import jax, jax.numpy as jnp
        import numpy as np
        B, S, SE, D, H, FF, E, K = (2, 256, 256, 128, 16, 512, 8, 2)
        HD = D // H

        def _layernorm(x, g, b):
            m = x.mean(-1, keepdims=True)
            v = ((x - m) ** 2).mean(-1, keepdims=True)
            return (x - m) / jnp.sqrt(v + 1e-05) * g + b

        def _attn(q_in, k_in, v_in, wq, bq, wk, bk, wv, bv, wo, bo, causal):
            Bq, Sq, Dm = q_in.shape
            Sk = k_in.shape[1]
            Q = (q_in @ wq + bq).reshape(Bq, Sq, H, HD)
            Kp = (k_in @ wk + bk).reshape(Bq, Sk, H, HD)
            V = (v_in @ wv + bv).reshape(Bq, Sk, H, HD)
            scores = jnp.einsum('bqhd,bkhd->bhqk', Q, Kp) / jnp.sqrt(jnp.float32(HD))
            if causal:
                mask = jnp.tril(jnp.ones((Sq, Sk), bool))
                scores = jnp.where(mask, scores, -jnp.inf)
            a = jax.nn.softmax(scores, axis=-1)
            o = jnp.einsum('bhqk,bkhd->bqhd', a, V).reshape(Bq, Sq, Dm)
            return o @ wo + bo

        def _moe(x, rw, rb, w1, b1, w2, b2):
            T = x.shape[0] * x.shape[1]
            xf = x.reshape(T, D)
            router_weights = jax.nn.softmax(xf @ rw + rb, axis=-1)
            topw, topi = jax.lax.top_k(router_weights, K)
            topw = jax.nn.softmax(topw, axis=-1)
            combine = jnp.zeros((T, E), xf.dtype).at[jnp.arange(T)[:, None], topi].add(topw)
            h = jax.nn.gelu(jnp.einsum('td,edf->etf', xf, w1) + b1[:, None, :], approximate=False)
            eo = jnp.einsum('etf,efd->etd', h, w2) + b2[:, None, :]
            out = jnp.einsum('etd,te->td', eo, combine)
            return out.reshape(x.shape)
        key = jax.random.key(seed)
        ks = jax.random.split(key, 32)
        w = lambda k, shape: jax.random.normal(k, shape, jnp.float32) * 0.02
        inp = {'x': jax.random.normal(ks[0], (B, S, D), jnp.float32), 'encoder_output': jax.random.normal(ks[1], (B, SE, D), jnp.float32), 'sa_wq': w(ks[2], (D, D)), 'sa_bq': jnp.zeros((D,), jnp.float32), 'sa_wk': w(ks[3], (D, D)), 'sa_bk': jnp.zeros((D,), jnp.float32), 'sa_wv': w(ks[4], (D, D)), 'sa_bv': jnp.zeros((D,), jnp.float32), 'sa_wo': w(ks[5], (D, D)), 'sa_bo': jnp.zeros((D,), jnp.float32), 'ca_wq': w(ks[6], (D, D)), 'ca_bq': jnp.zeros((D,), jnp.float32), 'ca_wk': w(ks[7], (D, D)), 'ca_bk': jnp.zeros((D,), jnp.float32), 'ca_wv': w(ks[8], (D, D)), 'ca_bv': jnp.zeros((D,), jnp.float32), 'ca_wo': w(ks[9], (D, D)), 'ca_bo': jnp.zeros((D,), jnp.float32), 'ln1_g': jnp.ones((D,), jnp.float32), 'ln1_b': jnp.zeros((D,), jnp.float32), 'ln2_g': jnp.ones((D,), jnp.float32), 'ln2_b': jnp.zeros((D,), jnp.float32), 'ln3_g': jnp.ones((D,), jnp.float32), 'ln3_b': jnp.zeros((D,), jnp.float32), 'router_w': w(ks[10], (D, E)), 'router_b': jnp.zeros((E,), jnp.float32), 'e_w1': w(ks[11], (E, D, FF)), 'e_b1': jnp.zeros((E, FF), jnp.float32), 'e_w2': w(ks[12], (E, FF, D)), 'e_b2': jnp.zeros((E, D), jnp.float32)}
        return inp
    _L0_xattn_all = _L0_xattn_setup()
    _L0_xattn_in = {k: v for k, v in _L0_xattn_all.items() if k in ('sa_wq', 'sa_bq', 'sa_wk', 'sa_bk', 'sa_wv', 'sa_bv', 'sa_wo', 'sa_bo', 'ca_wq', 'ca_bq', 'ca_wk', 'ca_bk', 'ca_wv', 'ca_bv', 'ca_wo', 'ca_bo', 'ln1_g', 'ln1_b', 'ln2_g', 'ln2_b', 'ln3_g', 'ln3_b', 'router_w', 'router_b', 'e_w1', 'e_b1', 'e_w2', 'e_b2')}
    del _L0_xattn_all
    return {'x': x, 'ctx_1024': ctx_1024, 'L0_xattn_sa_wq': _L0_xattn_in['sa_wq'], 'L0_xattn_sa_bq': _L0_xattn_in['sa_bq'], 'L0_xattn_sa_wk': _L0_xattn_in['sa_wk'], 'L0_xattn_sa_bk': _L0_xattn_in['sa_bk'], 'L0_xattn_sa_wv': _L0_xattn_in['sa_wv'], 'L0_xattn_sa_bv': _L0_xattn_in['sa_bv'], 'L0_xattn_sa_wo': _L0_xattn_in['sa_wo'], 'L0_xattn_sa_bo': _L0_xattn_in['sa_bo'], 'L0_xattn_ca_wq': _L0_xattn_in['ca_wq'], 'L0_xattn_ca_bq': _L0_xattn_in['ca_bq'], 'L0_xattn_ca_wk': _L0_xattn_in['ca_wk'], 'L0_xattn_ca_bk': _L0_xattn_in['ca_bk'], 'L0_xattn_ca_wv': _L0_xattn_in['ca_wv'], 'L0_xattn_ca_bv': _L0_xattn_in['ca_bv'], 'L0_xattn_ca_wo': _L0_xattn_in['ca_wo'], 'L0_xattn_ca_bo': _L0_xattn_in['ca_bo'], 'L0_xattn_ln1_g': _L0_xattn_in['ln1_g'], 'L0_xattn_ln1_b': _L0_xattn_in['ln1_b'], 'L0_xattn_ln2_g': _L0_xattn_in['ln2_g'], 'L0_xattn_ln2_b': _L0_xattn_in['ln2_b'], 'L0_xattn_ln3_g': _L0_xattn_in['ln3_g'], 'L0_xattn_ln3_b': _L0_xattn_in['ln3_b'], 'L0_xattn_router_w': _L0_xattn_in['router_w'], 'L0_xattn_router_b': _L0_xattn_in['router_b'], 'L0_xattn_e_w1': _L0_xattn_in['e_w1'], 'L0_xattn_e_b1': _L0_xattn_in['e_b1'], 'L0_xattn_e_w2': _L0_xattn_in['e_w2'], 'L0_xattn_e_b2': _L0_xattn_in['e_b2']}

def reference(x, ctx_1024, L0_xattn_sa_wq, L0_xattn_sa_bq, L0_xattn_sa_wk, L0_xattn_sa_bk, L0_xattn_sa_wv, L0_xattn_sa_bv, L0_xattn_sa_wo, L0_xattn_sa_bo, L0_xattn_ca_wq, L0_xattn_ca_bq, L0_xattn_ca_wk, L0_xattn_ca_bk, L0_xattn_ca_wv, L0_xattn_ca_bv, L0_xattn_ca_wo, L0_xattn_ca_bo, L0_xattn_ln1_g, L0_xattn_ln1_b, L0_xattn_ln2_g, L0_xattn_ln2_b, L0_xattn_ln3_g, L0_xattn_ln3_b, L0_xattn_router_w, L0_xattn_router_b, L0_xattn_e_w1, L0_xattn_e_b1, L0_xattn_e_w2, L0_xattn_e_b2):
    import jax
    import jax.numpy as jnp

    def _L0_xattn_ref(x, encoder_output, sa_wq, sa_bq, sa_wk, sa_bk, sa_wv, sa_bv, sa_wo, sa_bo, ca_wq, ca_bq, ca_wk, ca_bk, ca_wv, ca_bv, ca_wo, ca_bo, ln1_g, ln1_b, ln2_g, ln2_b, ln3_g, ln3_b, router_w, router_b, e_w1, e_b1, e_w2, e_b2):
        import jax, jax.numpy as jnp
        import numpy as np
        B, S, SE, D, H, FF, E, K = (2, 256, 256, 128, 16, 512, 8, 2)
        HD = D // H

        def _layernorm(x, g, b):
            m = x.mean(-1, keepdims=True)
            v = ((x - m) ** 2).mean(-1, keepdims=True)
            return (x - m) / jnp.sqrt(v + 1e-05) * g + b

        def _attn(q_in, k_in, v_in, wq, bq, wk, bk, wv, bv, wo, bo, causal):
            Bq, Sq, Dm = q_in.shape
            Sk = k_in.shape[1]
            Q = (q_in @ wq + bq).reshape(Bq, Sq, H, HD)
            Kp = (k_in @ wk + bk).reshape(Bq, Sk, H, HD)
            V = (v_in @ wv + bv).reshape(Bq, Sk, H, HD)
            scores = jnp.einsum('bqhd,bkhd->bhqk', Q, Kp) / jnp.sqrt(jnp.float32(HD))
            if causal:
                mask = jnp.tril(jnp.ones((Sq, Sk), bool))
                scores = jnp.where(mask, scores, -jnp.inf)
            a = jax.nn.softmax(scores, axis=-1)
            o = jnp.einsum('bhqk,bkhd->bqhd', a, V).reshape(Bq, Sq, Dm)
            return o @ wo + bo

        def _moe(x, rw, rb, w1, b1, w2, b2):
            T = x.shape[0] * x.shape[1]
            xf = x.reshape(T, D)
            router_weights = jax.nn.softmax(xf @ rw + rb, axis=-1)
            topw, topi = jax.lax.top_k(router_weights, K)
            topw = jax.nn.softmax(topw, axis=-1)
            combine = jnp.zeros((T, E), xf.dtype).at[jnp.arange(T)[:, None], topi].add(topw)
            h = jax.nn.gelu(jnp.einsum('td,edf->etf', xf, w1) + b1[:, None, :], approximate=False)
            eo = jnp.einsum('etf,efd->etd', h, w2) + b2[:, None, :]
            out = jnp.einsum('etd,te->td', eo, combine)
            return out.reshape(x.shape)
        x = _layernorm(x + _attn(x, x, x, sa_wq, sa_bq, sa_wk, sa_bk, sa_wv, sa_bv, sa_wo, sa_bo, True), ln1_g, ln1_b)
        x = _layernorm(x + _attn(x, encoder_output, encoder_output, ca_wq, ca_bq, ca_wk, ca_bk, ca_wv, ca_bv, ca_wo, ca_bo, False), ln2_g, ln2_b)
        x = _layernorm(x + _moe(x, router_w, router_b, e_w1, e_b1, e_w2, e_b2), ln3_g, ln3_b)
        return x
    x = _L0_xattn_ref(x, ctx_1024, L0_xattn_sa_wq, L0_xattn_sa_bq, L0_xattn_sa_wk, L0_xattn_sa_bk, L0_xattn_sa_wv, L0_xattn_sa_bv, L0_xattn_sa_wo, L0_xattn_sa_bo, L0_xattn_ca_wq, L0_xattn_ca_bq, L0_xattn_ca_wk, L0_xattn_ca_bk, L0_xattn_ca_wv, L0_xattn_ca_bv, L0_xattn_ca_wo, L0_xattn_ca_bo, L0_xattn_ln1_g, L0_xattn_ln1_b, L0_xattn_ln2_g, L0_xattn_ln2_b, L0_xattn_ln3_g, L0_xattn_ln3_b, L0_xattn_router_w, L0_xattn_router_b, L0_xattn_e_w1, L0_xattn_e_b1, L0_xattn_e_w2, L0_xattn_e_b2)
    return x

_drawn_inputs = setup_inputs


def setup_inputs(seed=0):
    import zlib

    import numpy as np

    out = dict(_drawn_inputs(seed))
    spreads = {'L0_xattn_sa_bq': (0.0, 0.8),
     'L0_xattn_sa_bk': (0.0, 2.0),
     'L0_xattn_sa_bv': (0.0, 0.273),
     'L0_xattn_sa_bo': (0.0, 0.1),
     'L0_xattn_ca_bq': (0.0, 2.0),
     'L0_xattn_ca_bk': (0.0, 2.0),
     'L0_xattn_ca_bv': (0.0, 0.313),
     'L0_xattn_ca_bo': (0.0, 0.1),
     'L0_xattn_ln1_g': (1.0, 0.2),
     'L0_xattn_ln1_b': (0.0, 0.1),
     'L0_xattn_ln2_g': (1.0, 0.2),
     'L0_xattn_ln2_b': (0.0, 0.1),
     'L0_xattn_ln3_g': (1.0, 0.2),
     'L0_xattn_ln3_b': (0.0, 0.1),
     'L0_xattn_router_b': (0.0, 0.1),
     'L0_xattn_e_b1': (0.0, 0.516),
     'L0_xattn_e_b2': (0.0, 0.1)}
    factors = {'L0_xattn_sa_wq': 8.0,
     'L0_xattn_sa_wk': 8.0,
     'L0_xattn_sa_wv': 4.606,
     'L0_xattn_ca_wq': 8.0,
     'L0_xattn_ca_wk': 8.0}
    for name, (base, spread) in spreads.items():
        noise = np.random.default_rng([zlib.crc32(name.encode()), seed]).standard_normal(out[name].shape)
        drawn = base * np.exp(spread * noise) if base else spread * noise
        out[name] = jnp.asarray(drawn.astype(out[name].dtype))
    for name, factor in factors.items():
        out[name] = (out[name] * factor).astype(out[name].dtype)
    return out
```

```python
import concourse.bass as bass
from concourse import mybir
from contextlib import ExitStack

fp32 = mybir.dt.float32
bf16 = mybir.dt.bfloat16
ALU = mybir.AluOpType
ACT = mybir.ActivationFunctionType
AX = mybir.AxisListType

B, SQ, SK, D, H = 32, 128, 120, 128, 16
HD = D // H
GB = 4
G = B // GB
HB = GB // 2
NT = GB * SQ
NU = H // 4
NP = H // 2
SLOTS = 6
ROWS = 2 * SLOTS * HD
SHIFT = 3
EPS = 1e-5
SCORE_SCALE = 1.0 / float(HD) ** 0.5
MASKED = -1e30
SELF, CROSS = 0, 1
KEYS = (SQ, SK)


def before(kind, g):
    return (CROSS, g - 2) if kind == SELF else (SELF, g + 1)


def behind(kind, g):
    return (CROSS, g - 1) if kind == SELF else (SELF, g + 2)


def exists(g):
    return not isinstance(g, int) or 0 <= g < G


def last_before(kind, g):
    for _ in range(4):
        kind, g = before(kind, g)
        if exists(g):
            return kind, g
    return None


def two_batches_ago(kind, g, b):
    if b >= 2:
        return kind, g, b - 2
    p = last_before(kind, g)
    return None if p is None else (*p, b + 2)


def wait(engine, sem, value):
    if not isinstance(value, int) or value > 0:
        engine.wait_ge(sem, value)


def wait_apart(engine, sem, value, passed):
    if isinstance(value, int):
        return wait(engine, sem, value)
    engine.wait_ge(sem, value)
    engine.sem_inc(passed, 1)


def attention(nc, ctx, t, x2_all, banks):
    sb = lambda n, s, d=fp32: ctx.enter_context(nc.sbuf_tensor(n, s, d))
    both = lambda n, s, d=fp32: [sb(f"{n}_self", s, d), sb(f"{n}_cross", s, d)]
    sem = lambda n: ctx.enter_context(nc.semaphore(n))
    sems = lambda n: [sem(f"{n}_self"), sem(f"{n}_cross")]

    wq, wk, wv, wo = (both(n, [D, D]) for n in ("wq", "wk", "wv", "wo"))
    bq, bk = both("bq", [D, 1]), both("bk", [D, 1])
    bv_rows = both("bv_rows", [128, D])
    bo_rows = both("bo_rows", [128, D])
    ln_g_rows, ln_b_rows = both("ln_g_rows", [128, D]), both("ln_b_rows", [128, D])
    res_rows = sb("res_rows", [128, D])
    ln_g_col, ln_b_col = sb("ln_g_col", [D, 1]), sb("ln_b_col", [D, 1])
    ident = sb("ident", [128, 128])
    ident_b = sb("ident_b", [128, 128], bf16)
    mask = sb("mask", [128, 4, SQ], bf16)
    head_ones = sb("head_ones", [128, 160])
    minus_half = sb("minus_half", [128, GB])
    xin = [sb("xin_self", [SQ, GB, D]), sb("xin_cross", [SK, GB, D])]
    src_t = [sb("src_t_self", [D, GB * SQ]), sb("src_t_cross", [D, GB * SK])]
    x1_t = sb("x1_t", [D, NT])
    q_res, k_res = sb("q_res", [D, NT]), sb("k_res", [D, NT])
    q_parts, k_parts = both("q_parts", [D, 3, NT], bf16), both("k_parts", [D, 3, NT], bf16)
    q_diag = both("q_diag", [128, NP, 2, NT], bf16)
    k_pack = both("k_pack", [128, NP, NT], bf16)
    v_wide = both("v_wide", [128, GB, 4, 160])
    row_max = both("row_max", [SQ, GB, H])
    max_rest = sb("max_rest", [SQ, 2, HB, H])
    max_parts = both("max_parts", [SQ, GB, SHIFT, H], bf16)
    max_t = sb("max_t", [SHIFT * H, NT], bf16)
    probs = sb("probs", [128, 2, H, SQ])
    recip = sb("recip", [128, 2, SQ])
    heads_t = sb("heads_t", [128, 2, SQ])
    resid = both("resid", [SQ, GB, D])
    summed = both("summed", [SQ, GB, D])
    stats = both("stats", [SQ, GB, 6])
    mean_var = both("mean_var", [SQ, GB, 2])
    var_eps = both("var_eps", [SQ, GB])
    rstd = both("rstd", [SQ, GB])
    z = both("z", [SQ, GB, D])
    zg = both("zg", [SQ, GB, D])

    t_bank, n_bank, o_bank, (m0, m1) = banks[0:2], banks[2:4], banks[4:6], banks[6:8]
    VALUES, SUMS, ROWS_OUT = slice(0, 128), slice(128, 256), slice(256, 384)

    q_dram = [nc.dram_tensor(f"q_dram{k}", (H, 3 * HD, NT), bf16, kind="Internal").ap() for k in (SELF, CROSS)]
    k_dram = [nc.dram_tensor(f"k_dram{k}", (H, 3 * HD, GB * KEYS[k]), bf16, kind="Internal").ap() for k in (SELF, CROSS)]
    m_dram = [nc.dram_tensor(f"m_dram{k}", (SHIFT * H, NT), bf16, kind="Internal").ap() for k in (SELF, CROSS)]

    passed = sem("passed")
    const_in = sem("const_in")
    consts = sem("consts")
    const_step = sem("const_step")
    x_in = sems("x_in")
    src_done, src_copied = sems("src_done"), sems("src_copied")
    k_done, q_done, v_done = sems("k_done"), sems("q_done"), sems("v_done")
    k_first, q_first = sems("k_first"), sems("q_first")
    k_rest, q_rest = sems("k_rest"), sems("q_rest")
    k_split, q_split = sems("k_split"), sems("q_split")
    k_last, q_last = sems("k_last"), sems("q_last")
    qk_stored = sems("qk_stored")
    packed = [[sem(f"packed_{k}_{h}") for h in range(2)] for k in ("self", "cross")]
    v_copied = sems("v_copied")
    nat_done, max_done = sems("nat_done"), sems("max_done")
    m_part = sems("m_part")
    m_split = sems("m_split")
    m_turned, m_copied = sems("m_turned"), sems("m_copied")
    m_stored = sems("m_stored")
    shifted = [[sem(f"shifted_{k}_{h}") for h in range(2)] for k in ("self", "cross")]
    t_done, exp_done = sems("t_done"), sems("exp_done")
    select_done = sem("select_done")
    pvs_done = sems("pvs_done")
    recip_done, heads_done = sems("recip_done"), sems("heads_done")
    y_done = sems("y_done")
    sum_done, stats_done, aggr_done = sems("sum_done"), sems("stats_done"), sems("aggr_done")
    eps_done, rstd_done, z_done = sems("eps_done"), sems("rstd_done"), sems("z_done")
    z_turned, x1_copied = sem("z_turned"), sem("x1_copied")
    zg_done, resid_done = sems("zg_done"), sems("resid_done")
    x2_done = sem("x2_done")

    block = ctx.enter_context(nc.Block())

    def stages(engine, stage):
        for it in (-1, 0, 1):
            stage(SELF, it)
            stage(CROSS, it - 1)
        with engine.Fori(2, G - 1) as it:
            stage(SELF, it)
            stage(CROSS, it - 1)
        for it in (G - 1, G):
            stage(SELF, it)
            stage(CROSS, it - 1)
        stage(SELF, G + 1)

    loads = []
    for k, p in ((SELF, "sa"), (CROSS, "ca")):
        for w, tile in (("wq", wq), ("wk", wk), ("wv", wv), ("wo", wo)):
            loads.append((tile[k][:], t[f"L0_xattn_{p}_{w}"]))
        for w, tile in (("bq", bq), ("bk", bk)):
            loads.append((tile[k][:], t[f"L0_xattn_{p}_{w}"].rearrange("(p a) -> p a", a=1)))
        for w, tile in (("bv", bv_rows), ("bo", bo_rows)):
            loads.append((tile[k][:], t[f"L0_xattn_{p}_{w}"].partition_broadcast(128)))
        loads.append((ln_g_rows[k][:], t[f"L0_xattn_ln{k + 1}_g"].partition_broadcast(128)))
        loads.append((ln_b_rows[k][:], t[f"L0_xattn_ln{k + 1}_b"].partition_broadcast(128)))
    loads.append((ln_g_col[:], t["L0_xattn_ln1_g"].rearrange("(p a) -> p a", a=1)))
    loads.append((ln_b_col[:], t["L0_xattn_ln1_b"].rearrange("(p a) -> p a", a=1)))
    ALL_LOADS = 16 * len(loads)
    CONSTS = 9

    @block.sync
    def _(sp):
        for dst, src in loads:
            sp.dma_start(dst, src).then_inc(const_in, 16)

        def shift_rows(kind, g, half):
            cols = slice(half * HB * SQ, (half + 1) * HB * SQ)
            wait(sp, m_copied[kind], 2 * g + half + 1)
            sp.dma_start(m_dram[kind][:, cols], max_t[:, cols]).then_inc(m_stored[kind], 16)
            wait(sp, m_stored[kind], 16 * (2 * g + half + 1))
            for c in range(2):
                src = m_dram[kind].rearrange("(r a c) t -> c r a t", r=SHIFT, c=2)[c][:, :, cols]
                r0 = ROWS + SHIFT * c
                sp.dma_start(q_diag[kind][r0:r0 + SHIFT, :, c, cols], src).then_inc(shifted[kind][half], 16)

        def stage(kind, g):
            nk, ng = behind(kind, g)
            if exists(g):
                shift_rows(kind, g, 1)
            if exists(g + 1):
                if kind == SELF:
                    wait(sp, resid_done[SELF], g + 1)
                    src = t["x"].rearrange("(g b) s d -> g s b d", b=GB)[g + 1]
                else:
                    wait(sp, src_done[CROSS], g + 1)
                    src = t["ctx_1024"].rearrange("(g b) s d -> g s b d", b=GB)[g + 1]
                sp.dma_start(xin[kind][:], src).then_inc(x_in[kind], 16)
            if exists(ng):
                shift_rows(nk, ng, 0)
            if exists(g + 1):
                n = g + 1
                KT = GB * KEYS[kind]
                wait(sp, k_split[kind], n + 1)
                wait(sp, k_last[kind], n + 1)
                wait(sp, k_first[kind], n + 1)
                for part in range(3):
                    sp.dma_start(k_dram[kind][:, (2 - part) * HD:(3 - part) * HD, :],
                                 k_parts[kind][:, part, 0:KT]).then_inc(qk_stored[kind], 16)
                wait(sp, q_split[kind], n + 1)
                wait(sp, q_last[kind], n + 1)
                wait(sp, q_first[kind], n + 1)
                for part in range(3):
                    sp.dma_start(q_dram[kind][:, part * HD:(part + 1) * HD, :],
                                 q_parts[kind][:, part, :]).then_inc(qk_stored[kind], 16)
                wait(sp, qk_stored[kind], 16 * 6 * (n + 1))
                for half in range(2):
                    wait(sp, t_done[kind], 16 * g + 8 * (half + 1))
                    qc = slice(half * HB * SQ, (half + 1) * HB * SQ)
                    kc = slice(half * HB * KEYS[kind], (half + 1) * HB * KEYS[kind])
                    for c in range(2):
                        at = 0
                        for run in (3, 2, 1):
                            r = slice(ROWS // 2 * c + HD * at, ROWS // 2 * c + HD * (at + run))
                            q_src = q_dram[kind].rearrange("(a c) r t -> c r a t", c=2)[c, 0:run * HD, :, qc]
                            k_src = k_dram[kind].rearrange("(a c) r t -> c r a t", c=2)[c, (3 - run) * HD:3 * HD, :, kc]
                            sp.dma_start(k_pack[kind][r, :, kc], k_src).then_inc(packed[kind][half], 16)
                            sp.dma_start(q_diag[kind][r, :, c, qc], q_src).then_inc(packed[kind][half], 16)
                            at += run

        stages(sp, stage)
        for kind in (SELF, CROSS):
            sp.wait_ge(qk_stored[kind], 16 * 6 * G)
            sp.wait_ge(m_stored[kind], 16 * 2 * G)

    @block.tensor
    def _(pe):
        pe.wait_ge(const_in, ALL_LOADS)
        pe.wait_ge(consts, CONSTS)

        def turn_shift(kind, g, half, clear):
            clear()
            wait_apart(pe, m_split[kind], 2 * g + half + 1, passed)
            for b in range(half * HB, (half + 1) * HB):
                out = m1[0:SHIFT * H, :].bitcast(bf16)[:, b * SQ:(b + 1) * SQ]
                last = nc.tensor.transpose(out, max_parts[kind][:, b].rearrange("p r h -> p (r h)"), ident_b[:])
            last.then_inc(m_turned[kind], 1)

        def stage(kind, g):
            nk, ng = behind(kind, g)
            pk, pg = before(kind, g)
            main = exists(g)

            def m1_clear(use):
                k_, g_, at = kind, g, use
                for _ in range(24):
                    at -= 1
                    if at < 0:
                        k_, g_ = before(k_, g_)
                        at = 3
                    if at == 0 and exists(g_):
                        return wait(pe, m_copied[k_], 2 * g_ + 2)
                    if at == 1 and k_ == CROSS and exists(before(k_, g_)[1]):
                        return wait(pe, x1_copied, before(k_, g_)[1] + 1)
                    if at == 2 and exists(g_ + 1):
                        wait(pe, k_first[k_], g_ + 2)
                        return wait(pe, k_rest[k_], g_ + 2)
                    if at == 3 and exists(behind(k_, g_)[1]):
                        k2, g2 = behind(k_, g_)
                        return wait(pe, m_copied[k2], 2 * g2 + 1)

            for b in range(GB):
                nat = (kind, g, GB - 1) if b == 0 else (nk, ng, b - 1)
                nat_before = (kind, g, GB - 2) if b == 0 else (kind, g, GB - 1) if b == 1 else (nk, ng, b - 2)
                last = (kind, g, b - 1) if b >= 1 else (pk, pg, GB - 1)
                for u in range(NU):
                    if main:
                        if b % HB == 0 and u == 0:
                            wait(pe, shifted[kind][b // HB], 32 * (g + 1))
                        if u >= 2:
                            wait(pe, exp_done[kind], 16 * g + 4 * b + u - 1)
                        elif b >= 1:
                            wait(pe, exp_done[kind], 16 * g + 4 * (b - 1) + u + 3)
                        elif (p := last_before(kind, g)) is not None:
                            wait(pe, exp_done[p[0]], 16 * p[1] + 12 + u + 3)
                        for i in range(2):
                            a = 2 * u + i
                            mm = nc.tensor.matmul(
                                t_bank[u % 2][0:KEYS[kind], i * 256:(i + 1) * 256].rearrange("p (c q) -> p c q", c=2),
                                k_pack[kind][:, a, b * KEYS[kind]:(b + 1) * KEYS[kind]],
                                q_diag[kind][:, a, :, b * SQ:(b + 1) * SQ], start=True, stop=True)
                        mm.then_inc(t_done[kind], 1)
                    if exists(nat[1]):
                        k_, g_, b_ = nat
                        if b_ % HB == 0 and u == 0:
                            wait(pe, packed[k_][b_ // HB], 16 * 12 * (g_ + 1))
                        if u >= 2:
                            wait(pe, max_done[k_], 16 * g_ + 4 * b_ + u - 1)
                        elif b_ >= 1:
                            wait(pe, max_done[k_], 16 * g_ + 4 * (b_ - 1) + u + 3)
                        else:
                            p = (kind, g) if exists(g) else last_before(kind, g)
                            if p is not None:
                                wait(pe, max_done[p[0]], 16 * p[1] + 12 + u + 3)
                        bank, keys = n_bank[u % 2], KEYS[k_]
                        if k_ == SELF:
                            nc.tensor.matmul(bank[:], ident_b[:], mask[:].rearrange("p h k -> p (h k)"), start=True, stop=False)
                        for i in range(4):
                            mm = nc.tensor.matmul(bank[:, i * keys:(i + 1) * keys],
                                                  q_diag[k_][0:ROWS, 2 * u + i // 2, i % 2, b_ * SQ:(b_ + 1) * SQ],
                                                  k_pack[k_][0:ROWS, 2 * u + i // 2, b_ * keys:(b_ + 1) * keys],
                                                  start=k_ == CROSS, stop=k_ == CROSS or i == 3)
                        mm.then_inc(nat_done[k_], 1)
                    ago = (kind, g, b - 2) if b >= 2 else (pk, pg, b + 2)
                    if u == 0 and exists(ago[1]):
                        k_, g_, b_ = ago
                        wait(pe, heads_done[k_], 4 * g_ + b_ + 1)
                        nc.tensor.matmul(o_bank[b_ % 2][:, ROWS_OUT], heads_t[:, b_ % 2],
                                         wo[k_][:], start=True, stop=True).then_inc(y_done[k_], 1)
                    if u in (1, 2) and exists(last[1]):
                        k_, g_, b_ = last
                        keys = KEYS[k_]
                        if u == 1:
                            if k_ == SELF:
                                wait(pe, select_done, 16 * g_ + 4 * b_ + 4)
                            else:
                                wait(pe, exp_done[k_], 16 * g_ + 4 * b_ + 4)
                            if b_ == 0:
                                wait(pe, v_copied[k_], g_ + 1)
                            if (w := two_batches_ago(*last)) is not None:
                                wait(pe, sum_done[w[0]], 4 * w[1] + w[2] + 1)
                        for c in range(4):
                            for j in range(4):
                                lhs = (v_wide[k_][0:keys, b_, j, 32 * c:32 * c + 32] if u == 1
                                       else head_ones[0:keys, 32 * c:32 * c + 32])
                                mm = nc.tensor.matmul(o_bank[b_ % 2][32 * j:32 * j + 32, VALUES if u == 1 else SUMS], lhs,
                                                      probs[0:keys, b_ % 2, 4 * j + c], start=c == 0, stop=c == 3)
                        if u == 2:
                            mm.then_inc(pvs_done[k_], 1)
                    if (b, u) == (1, 0) and main:
                        turn_shift(kind, g, 1, lambda: m1_clear(0))
                    if (b, u) == (1, 1) and exists(ng):
                        keys = KEYS[nk]
                        wait(pe, q_first[nk], ng + 1)
                        wait(pe, q_rest[nk], ng + 1)
                        for j in range(GB):
                            mm = nc.tensor.matmul(m0[0:keys, j * D:(j + 1) * D], src_t[nk][:, j * keys:(j + 1) * keys],
                                                  wv[nk][:], start=True, stop=True)
                        mm.then_inc(v_done[nk], 1)
                    if (b, u) == (1, 3) and exists(g + 1):
                        keys = KEYS[kind]
                        wait(pe, x_in[kind], 16 * (g + 2))
                        if exists(ng):
                            wait(pe, v_copied[nk], ng + 1)
                        for j in range(GB):
                            mm = nc.tensor.transpose(m0[:, j * keys:(j + 1) * keys], xin[kind][:, j, :], ident[0:keys, 0:keys])
                        mm.then_inc(src_done[kind], 1)
                    if (b, u) == (2, 0) and kind == CROSS and exists(pg):
                        wait(pe, z_done[SELF], pg + 1)
                        m1_clear(1)
                        for j in range(GB):
                            mm = nc.tensor.transpose(m1[:, j * SQ:(j + 1) * SQ], z[SELF][:, j, :], ident[:])
                        mm.then_inc(z_turned, 1)
                    if (b, u) == (2, 1) and exists(g + 1):
                        KT = GB * KEYS[kind]
                        wait(pe, src_copied[kind], g + 2)
                        m1_clear(2)
                        nc.tensor.matmul(m1[:, 0:KT], wk[kind][:], src_t[kind][:, 0:KT], start=True, stop=True).then_inc(k_done[kind], 1)
                    if (b, u) == (2, 3) and exists(g + 1):
                        if kind == CROSS:
                            wait(pe, x1_copied, g + 2)
                        nc.tensor.matmul(m0[:], wq[kind][:], (x1_t if kind == CROSS else src_t[SELF])[:], start=True,
                                         stop=True).then_inc(q_done[kind], 1)
                    if (b, u) == (3, 0) and exists(ng):
                        turn_shift(nk, ng, 0, lambda: m1_clear(3))

        stages(pe, stage)

    @block.scalar
    def _(act):
        act.wait_ge(const_in, ALL_LOADS)

        def copy_shift(kind, g, half):
            cols = slice(half * HB * SQ, (half + 1) * HB * SQ)
            wait(act, m_turned[kind], 2 * g + half + 1)
            if half == 0:
                p = last_before(kind, g)
                if p is not None:
                    wait(act, m_stored[p[0]], 16 * (2 * p[1] + 1))
            else:
                p = last_before(kind, g)
                if p is not None:
                    wait(act, m_stored[p[0]], 16 * (2 * p[1] + 2))
            nc.scalar.activation(max_t[:, cols], m1[0:SHIFT * H, :].bitcast(bf16)[:, cols], ACT.Copy).then_inc(m_copied[kind], 1)

        def stage(kind, g):
            nk, ng = behind(kind, g)
            pk, pg = before(kind, g)
            keys = KEYS[kind]
            for b in range(GB):
                for u in range(NU):
                    if exists(g):
                        if u == 0 and (w := two_batches_ago(kind, g, b)) is not None:
                            wait(act, pvs_done[w[0]], 4 * w[1] + w[2] + 1)
                        wait(act, t_done[kind], 16 * g + 4 * b + u + 1)
                        nc.scalar.activation(probs[0:keys, b % 2, 4 * u:4 * u + 4].rearrange("p h q -> p (h q)"),
                                             t_bank[u % 2][0:keys, :], ACT.Exp, scale=SCORE_SCALE).then_inc(exp_done[kind], 1)
                    if (b, u) == (1, 0) and exists(g):
                        copy_shift(kind, g, 1)
                    if (b, u) == (1, 3) and exists(g + 1):
                        wait(act, src_done[kind], g + 2)
                        nc.scalar.activation(src_t[kind][:], m0[:, 0:GB * keys], ACT.Copy).then_inc(src_copied[kind], 1)
                    if (b, u) == (2, 0) and kind == CROSS and exists(pg):
                        wait(act, z_turned, pg + 1)
                        nc.scalar.activation(x1_t[:], m1[:], ACT.Identity, bias=ln_b_col[:], scale=ln_g_col[:]).then_inc(x1_copied, 1)
                    if (b, u) == (2, 1) and exists(g + 1):
                        wait(act, k_done[kind], g + 2)
                        wait(act, qk_stored[kind], 16 * 6 * (g + 1))
                        nc.scalar.activation(k_parts[kind][:, 0, 0:GB * keys], m1[:, 0:GB * keys], ACT.Identity,
                                             bias=bk[kind][:]).then_inc(k_first[kind], 1)
                    if (b, u) == (2, 3) and exists(g + 1):
                        wait(act, q_done[kind], g + 2)
                        nc.scalar.activation(q_parts[kind][:, 0, :], m0[:], ACT.Identity, bias=bq[kind][:]).then_inc(q_first[kind], 1)
                    if (b, u) == (3, 0) and exists(ng):
                        copy_shift(nk, ng, 0)

        stages(act, stage)

    @block.vector
    def _(dve):
        nc.vector.memset(q_diag[SELF][:].rearrange("p a c t -> p (a c t)").bitcast(fp32), 0.0).then_inc(consts, 1)
        for kind in (SELF, CROSS):
            nc.vector.memset(k_pack[kind][96:128].rearrange("p a t -> p (a t)"), 1.0).then_inc(consts, 1)
        dve.wait_ge(const_in, ALL_LOADS)

        def stage(kind, g):
            nk, ng = behind(kind, g)
            pk, pg = before(kind, g)
            for b in range(GB):
                nat = (kind, g, GB - 1) if b == 0 else (nk, ng, b - 1)
                last = (kind, g, b - 1) if b >= 1 else (pk, pg, GB - 1)
                ago = (kind, g, b - 2) if b >= 2 else (pk, pg, b + 2)
                for u in range(NU):
                    if u == 3 and exists(last[1]):
                        k_, g_, b_ = last
                        wait(dve, pvs_done[k_], 4 * g_ + b_ + 1)
                        nc.vector.reciprocal(recip[:, b_ % 2], o_bank[b_ % 2][:, SUMS]).then_inc(recip_done[k_], 1)
                        wait(dve, recip_done[k_], 4 * g_ + b_ + 1)
                        nc.vector.tensor_tensor(heads_t[:, b_ % 2], o_bank[b_ % 2][:, VALUES], recip[:, b_ % 2],
                                                ALU.mult).then_inc(heads_done[k_], 1)
                    if exists(nat[1]):
                        k_, g_, b_ = nat
                        keys = KEYS[k_]
                        wait(dve, nat_done[k_], 16 * g_ + 4 * b_ + u + 1)
                        nc.vector.tensor_reduce(row_max[k_][:, b_, 4 * u:4 * u + 4],
                                                n_bank[u % 2][:, 0:4 * keys].rearrange("p (h k) -> p h k", h=4),
                                                AX.X, ALU.max, negate=True).then_inc(max_done[k_], 1)
                    if u == 0 and exists(ago[1]):
                        k_, g_, b_ = ago
                        wait(dve, y_done[k_], 4 * g_ + b_ + 1)
                        if b_ == 0:
                            wait(dve, resid_done[k_], g_ + 1)
                        nc.vector.tensor_tensor(summed[k_][:, b_], o_bank[b_ % 2][:, ROWS_OUT],
                                                resid[k_][:, b_], ALU.add).then_inc(sum_done[k_], 1)
                    if u == 1 and exists(ago[1]):
                        k_, g_, b_ = ago
                        wait(dve, sum_done[k_], 4 * g_ + b_ + 1)
                        nc.vector.bn_stats(stats[k_][:, b_], summed[k_][:, b_]).then_inc(stats_done[k_], 1)
                        wait_apart(dve, stats_done[k_], 4 * g_ + b_ + 1, passed)
                        nc.vector.bn_aggr(mean_var[k_][:, b_], stats[k_][:, b_]).then_inc(aggr_done[k_], 1)
                    if (b, u) == (1, 1) and exists(ng):
                        keys = KEYS[nk]
                        wait(dve, v_done[nk], ng + 1)
                        for j in range(GB):
                            out = v_wide[nk][0:keys, j].rearrange("p j (c r) -> p j c r", r=40)[:, :, :, 0:HD]
                            op = nc.vector.tensor_tensor(out, m0[0:keys, j * D:(j + 1) * D].rearrange("p (j c i) -> p j c i", j=4, i=HD),
                                                         bv_rows[nk][0:keys].rearrange("p (j c i) -> p j c i", j=4, i=HD), ALU.add)
                        op.then_inc(v_copied[nk], 1)
                    if (b, u) == (1, 3) and exists(pg):
                        wait(dve, rstd_done[pk], pg + 1)
                        for j in range(GB):
                            op = nc.vector.tensor_scalar(z[pk][:, j], summed[pk][:, j], mean_var[pk][:, j, 0:1], rstd[pk][:, j:j + 1],
                                                         ALU.subtract, ALU.mult)
                        op.then_inc(z_done[pk], 1)
                    if (b, u) == (2, 2) and exists(g + 1):
                        KT = GB * KEYS[kind]
                        wait(dve, k_first[kind], g + 2)
                        nc.vector.scalar_tensor_tensor(k_res[:, 0:KT], m1[:, 0:KT], bk[kind][:], k_parts[kind][:, 0, 0:KT], ALU.add,
                                                       ALU.subtract).then_inc(k_rest[kind], 1)
                    if (b, u) == (3, 0) and exists(g + 1):
                        wait(dve, q_first[kind], g + 2)
                        nc.vector.scalar_tensor_tensor(q_res[:], m0[:], bq[kind][:], q_parts[kind][:, 0, :], ALU.add,
                                                       ALU.subtract).then_inc(q_rest[kind], 1)

        stages(dve, stage)

    @block.gpsimd
    def _(pool):
        nc.gpsimd.memset(ident[:], 0.0).then_inc(const_step, 1)
        nc.gpsimd.memset(mask[:].rearrange("p h k -> p (h k)"), 0.0).then_inc(const_step, 1)
        nc.gpsimd.memset(head_ones[:], 0.0).then_inc(const_step, 1)
        nc.gpsimd.memset(minus_half[:], -0.5)
        for kind in (SELF, CROSS):
            nc.gpsimd.memset(v_wide[kind][:].rearrange("p b j c -> p (b j c)"), 0.0).then_inc(consts, 1)
        pool.wait_ge(const_step, 3)
        nc.gpsimd.affine_select(out=ident[:], in_=ident[:], compare_op=ALU.not_equal, fill=1.0, base=0,
                                pattern=[[-1, 128]], channel_multiplier=1).then_inc(const_step, 1)
        nc.gpsimd.affine_select(out=mask[:], in_=mask[:], compare_op=ALU.is_ge, fill=MASKED, base=0,
                                pattern=[[0, 4], [-1, SQ]], channel_multiplier=1).then_inc(consts, 1)
        nc.gpsimd.memset(head_ones[:].rearrange("p (c r) -> p c r", r=40)[:, :, 0:HD], 1.0).then_inc(consts, 1)
        pool.wait_ge(const_step, 4)
        nc.gpsimd.tensor_copy(ident_b[:], ident[:]).then_inc(consts, 1)
        nc.gpsimd.memset(q_diag[CROSS][:].rearrange("p a c t -> p (a c t)").bitcast(fp32), 0.0).then_inc(consts, 1)
        pool.wait_ge(const_in, ALL_LOADS)
        nc.gpsimd.tensor_tensor(res_rows[:], ln_b_rows[SELF][:], bo_rows[CROSS][:], ALU.add).then_inc(const_step, 1)
        pool.wait_ge(const_step, 5)

        def split_shift(kind, g, half):
            hb = slice(half * HB, (half + 1) * HB)
            parts, rest = max_parts[kind][:, hb], max_rest
            wait_apart(pool, max_done[kind], 16 * g + 8 * (half + 1), passed)
            nc.gpsimd.tensor_copy(parts[:, :, 0], row_max[kind][:, hb]).then_inc(m_part[kind], 1)
            wait_apart(pool, m_part[kind], 3 * (2 * g + half) + 1, passed)
            nc.gpsimd.tensor_tensor(rest[:, 0], row_max[kind][:, hb], parts[:, :, 0], ALU.subtract).then_inc(m_part[kind], 1)
            wait_apart(pool, m_part[kind], 3 * (2 * g + half) + 2, passed)
            nc.gpsimd.tensor_copy(parts[:, :, 1], rest[:, 0]).then_inc(m_part[kind], 1)
            wait_apart(pool, m_part[kind], 3 * (2 * g + half) + 3, passed)
            nc.gpsimd.tensor_tensor(parts[:, :, 2], rest[:, 0], parts[:, :, 1], ALU.subtract).then_inc(m_split[kind], 1)

        def split(parts, rest, rest_done, split_done, last_done, g, n):
            wait_apart(pool, rest_done, g + 1, passed)
            nc.gpsimd.tensor_copy(parts[:, 1, 0:n], rest[:, 0:n]).then_inc(split_done, 1)
            wait_apart(pool, split_done, g + 1, passed)
            nc.gpsimd.tensor_tensor(parts[:, 2, 0:n], rest[:, 0:n], parts[:, 1, 0:n], ALU.subtract).then_inc(last_done, 1)

        def rows(tile):
            return tile[:].unsqueeze(1).to_broadcast([128, GB, D])

        def stage(kind, g):
            nk, ng = behind(kind, g)
            pk, pg = before(kind, g)
            for b in range(GB):
                for u in range(NU):
                    if kind == SELF and exists(g):
                        wait_apart(pool, exp_done[SELF], 16 * g + 4 * b + u + 1, passed)
                        p = probs[:, b % 2, 4 * u:4 * u + 4]
                        nc.gpsimd.affine_select(out=p, in_=p, compare_op=ALU.is_ge, fill=0.0, base=0,
                                                pattern=[[0, 4], [1, SQ]], channel_multiplier=-1).then_inc(select_done, 1)
                    if (b, u) == (0, 0) and kind == SELF and exists(g):
                        wait_apart(pool, sum_done[SELF], 4 * g, passed)
                        wait_apart(pool, x_in[SELF], 16 * (g + 1), passed)
                        nc.gpsimd.tensor_tensor(resid[SELF][:], xin[SELF][:], rows(bo_rows[SELF]), ALU.add).then_inc(resid_done[SELF], 1)
                    if (b, u) == (0, 3) and exists(g):
                        split_shift(kind, g, 1)
                    if (b, u) == (1, 1) and exists(pg):
                        wait_apart(pool, aggr_done[pk], 4 * (pg + 1), passed)
                        nc.gpsimd.tensor_scalar(var_eps[pk][:], mean_var[pk][:, :, 1], EPS, None, ALU.add).then_inc(eps_done[pk], 1)
                        wait_apart(pool, eps_done[pk], pg + 1, passed)
                        nc.gpsimd.tensor_tensor(rstd[pk][:], var_eps[pk][:], minus_half[:], ALU.pow).then_inc(rstd_done[pk], 1)
                    if (b, u) == (2, 0) and pk == CROSS and exists(pg):
                        wait_apart(pool, z_done[CROSS], pg + 1, passed)
                        wait_apart(pool, x2_done, pg, passed)
                        nc.gpsimd.tensor_tensor(zg[CROSS][:], z[CROSS][:], rows(ln_g_rows[CROSS]), ALU.mult).then_inc(zg_done[CROSS], 1)
                        wait_apart(pool, zg_done[CROSS], pg + 1, passed)
                        nc.gpsimd.tensor_tensor(x2_all[:, bass.ds(pg * GB, GB), :], zg[CROSS][:], rows(ln_b_rows[CROSS]), ALU.add).then_inc(x2_done, 1)
                    if (b, u) == (2, 2) and kind == SELF and exists(ng):
                        wait_apart(pool, z_done[SELF], ng + 1, passed)
                        wait_apart(pool, sum_done[CROSS], 4 * ng, passed)
                        wait_apart(pool, resid_done[CROSS], ng, passed)
                        nc.gpsimd.tensor_tensor(zg[SELF][:], z[SELF][:], rows(ln_g_rows[SELF]), ALU.mult).then_inc(zg_done[SELF], 1)
                        wait_apart(pool, zg_done[SELF], ng + 1, passed)
                        nc.gpsimd.tensor_tensor(resid[CROSS][:], zg[SELF][:], rows(res_rows), ALU.add).then_inc(resid_done[CROSS], 1)
                    if (b, u) == (2, 3):
                        if exists(g + 1):
                            split(k_parts[kind], k_res, k_rest[kind], k_split[kind], k_last[kind], g + 1, GB * KEYS[kind])
                        if exists(ng):
                            split_shift(nk, ng, 0)
                    if (b, u) == (3, 1) and exists(g + 1):
                        split(q_parts[kind], q_res, q_rest[kind], q_split[kind], q_last[kind], g + 1, NT)

        stages(pool, stage)


E_, FF, TOPK = 8, 512, 2
FC = FF // 128
TOK = B * SQ
NTILE = TOK // 128
BLK = 256
RS = TOK + BLK
NULL_ROW = E_ * RS
ROW = D + 1
BLOCKS = TOPK * TOK // BLK + E_ - 1
SPARE = BLOCKS - TOPK * TOK // BLK
TRASH = TOPK * TOK
PADS = E_ + SPARE


def routing(nc, ctx, t, x2_all, weights, counts_tab, rows_dram, banks):
    sb = lambda n, s, d=fp32: ctx.enter_context(nc.sbuf_tensor(n, s, d))
    sem = lambda n: ctx.enter_context(nc.semaphore(n))
    i32 = mybir.dt.int32
    block_expert, block_row = counts_tab
    rw, rb_rows = sb("rw", [D, E_]), sb("rb_rows", [128, E_])
    ident = sb("ident_r", [128, 128])
    earlier = sb("earlier", [128, 128], bf16)
    ones_b = sb("ones_b", [128, 128], bf16)
    first_weight = sb("first_weight", [128, E_])
    region = sb("region", [128, E_])
    row_id = sb("row_id", [128, TOPK, GB])
    pad = sb("pad", [128, PADS, BLK // 128, ROW])
    stage = sb("stage", [128, TOPK, GB, ROW])
    x2_t = sb("x2_t", [D, NT])
    names = ("logit", "shifted_logit", "expo", "prob", "equal", "sel", "one_a", "prob_b", "equal_b", "sel_b", "one_b", "pos", "pick_a", "pick_b")
    w8 = {n: sb(f"r_{n}", [128, GB, E_]) for n in names}
    w1 = {n: sb(f"r_{n}", [128, GB]) for n in ("top", "total", "inv", "best", "first", "best_b", "first_b", "gap", "egap", "den", "inv2", "slot_a", "slot_b")}
    id_base = sb("r_id_base", [128, TOPK, GB], i32)
    chosen = sb("r_chosen", [128, GB, E_], bf16)
    run = sb("r_run", [128, GB + 1, E_])
    slot = sb("r_slot", [128, TOPK, GB], i32)
    m0, m1, m2 = banks
    step, const_in, consts = sem("r_step"), sem("r_const_in"), sem("r_consts")
    staged, turned, copied, logits, exped, gap_exped, counted = (sem(f"r_{n}") for n in
        ("staged", "turned", "copied", "logits", "exped", "gap_exped", "counted"))
    shift_done, gap_done, chosen_done, slot_done, ids_done, scattered = (sem(f"r_{n}") for n in
        ("shift_done", "gap_done", "chosen_done", "slot_done", "ids_done", "scattered"))
    passed = sem("r_passed")
    base_done = sem("r_base_done")
    padded, last_count, read_ok = sem("r_padded"), sem("r_last_count"), sem("r_read_ok")
    CONSTS = 7
    jt = sb("r_jt", [1, 16]); nb3 = sb("r_nb3", [1, E_, 16]); nb = sb("r_nb", [1, E_])
    tri = sb("r_tri", [1, E_, E_]); end3 = sb("r_end3", [1, E_, E_]); end = sb("r_end", [1, E_]); start = sb("r_start", [1, E_])
    jb = sb("r_jb", [1, BLOCKS, E_]); past = sb("r_past", [1, BLOCKS, E_]); reached = sb("r_reached", [1, BLOCKS, E_])
    inside = sb("r_inside", [1, BLOCKS, E_]); base8 = sb("r_base8", [1, E_]); at8 = sb("r_at8", [1, BLOCKS, E_]); at8b = sb("r_at8b", [1, BLOCKS, E_])
    bexp = sb("r_bexp", [1, BLOCKS]); used = sb("r_used", [1, BLOCKS]); brow = sb("r_brow", [1, BLOCKS]); brow2 = sb("r_brow2", [1, BLOCKS])
    used0, spare, spare2 = (sb(f"r_{n}", [1, BLOCKS]) for n in ("used0", "spare", "spare2"))
    bexp2 = sb("r_bexp2", [1, BLOCKS]); brow3 = sb("r_brow3", [1, BLOCKS])
    pad_at = sb("r_pad_at", [1, E_]); pad_row = sb("r_pad_row", [1, E_], i32)

    def rep(ap, n=E_):
        return ap.unsqueeze(2).to_broadcast([128, GB, n])

    def rows(ap):
        return ap.unsqueeze(1).to_broadcast([128, GB, E_])

    with nc.Block() as block:
        @block.sync
        def _(sp):
            sp.dma_start(rw[:], t["L0_xattn_router_w"]).then_inc(const_in, 16)
            sp.dma_start(rb_rows[:], t["L0_xattn_router_b"].partition_broadcast(128)).then_inc(const_in, 16)
            sp.wait_ge(consts, CONSTS)
            sp.dma_start(rows_dram[NULL_ROW:NULL_ROW + SPARE * BLK].rearrange("(a p) r -> p a r", p=128),
                         pad[:, E_:PADS].rearrange("p n a r -> p (n a) r")).then_inc(padded, 16)
            sp.wait_ge(last_count, 1)
            sp.wait_ge(scattered, 16 * TOPK * NTILE)
            for e in range(E_):
                at = sp.value_load(pad_row[0:1, e:e + 1], min_val=0, max_val=NULL_ROW - BLK)
                sp.dma_start(rows_dram[bass.ds(at, BLK)].rearrange("(a p) r -> p a r", p=128), pad[:, e]).then_inc(padded, 16)
            sp.wait_ge(padded, 16 * (E_ + 1))

        @block.gpsimd
        def _(pool):
            nc.gpsimd.memset(ident[:], 0.0).then_inc(read_ok, 1)
            nc.gpsimd.memset(earlier[:], 1.0).then_inc(read_ok, 1)
            nc.gpsimd.memset(ones_b[:], 1.0).then_inc(consts, 1)
            nc.gpsimd.memset(pad[:], 0.0).then_inc(read_ok, 1)
            nc.gpsimd.memset(tri[:], 1.0).then_inc(read_ok, 1)
            pool.wait_ge(read_ok, 4)
            nc.gpsimd.affine_select(out=ident[:], in_=ident[:], compare_op=ALU.not_equal, fill=1.0, base=0,
                                    pattern=[[-1, 128]], channel_multiplier=1).then_inc(consts, 1)
            nc.gpsimd.affine_select(out=earlier[:], in_=earlier[:], compare_op=ALU.is_gt, fill=0.0, base=0,
                                    pattern=[[1, 128]], channel_multiplier=-1).then_inc(consts, 1)
            nc.gpsimd.iota(first_weight[:], [[-1, E_]], base=E_, channel_multiplier=0, allow_small_or_imprecise_dtypes=True).then_inc(consts, 1)
            nc.gpsimd.iota(region[:], [[RS, E_]], base=0, channel_multiplier=0, allow_small_or_imprecise_dtypes=True).then_inc(consts, 1)
            nc.gpsimd.iota(row_id[:], [[TOK, TOPK], [128, GB]], base=0, channel_multiplier=1, allow_small_or_imprecise_dtypes=True).then_inc(consts, 1)
            nc.gpsimd.iota(pad[:, :, :, D:ROW].bitcast(i32), [[BLK, PADS], [128, BLK // 128], [0, 1]], base=TRASH, channel_multiplier=1)
            nc.gpsimd.iota(jt[:], [[BLK, 16]], base=0, channel_multiplier=0, allow_small_or_imprecise_dtypes=True)
            nc.gpsimd.affine_select(out=tri[:], in_=tri[:], compare_op=ALU.is_ge, fill=0.0, base=0,
                                    pattern=[[1, E_], [-1, E_]], channel_multiplier=0)
            nc.gpsimd.iota(jb[:], [[1, BLOCKS], [0, E_]], base=0, channel_multiplier=0, allow_small_or_imprecise_dtypes=True).then_inc(consts, 1)
            pool.wait_ge(consts, CONSTS)
            with pool.Fori(0, G) as g:
                wait_apart(pool, staged, g + 1, passed)
                for k in range(TOPK):
                    op = nc.gpsimd.iota(stage[:, k, :, D:ROW].bitcast(i32), [[128, GB], [0, 1]], base=k * TOK, channel_multiplier=1)
                op.then_inc(ids_done, 1)
                wait_apart(pool, ids_done, 2 * g + 1, passed)
                wait_apart(pool, base_done, g + 1, passed)
                nc.gpsimd.tensor_tensor(stage[:, :, :, D].bitcast(i32), stage[:, :, :, D].bitcast(i32), id_base[:], ALU.add).then_inc(ids_done, 1)
                wait_apart(pool, ids_done, 2 * g + 2, passed)
                nc.gpsimd.tensor_scalar(id_base[:], id_base[:], NT, None, ALU.add).then_inc(base_done, 1)
                wait_apart(pool, slot_done, g + 1, passed)
                for k in range(TOPK):
                    for j in range(GB):
                        nc.gpsimd.indirect_dma_start(rows_dram, bass.IndirectOffsetOnAxis(ap=slot[:, k, j:j + 1], axis=0),
                                                     stage[:, k, j, :], None).then_inc(scattered, 16)

        @block.tensor
        def _(pe):
            pe.wait_ge(const_in, 32)
            pe.wait_ge(consts, CONSTS)
            with pe.Fori(0, G) as g:
                pe.wait_ge(staged, g + 1)
                for j in range(GB):
                    mm = nc.tensor.transpose(m0[:, j * 128:(j + 1) * 128], stage[:, 0, j, 0:D], ident[:])
                mm.then_inc(turned, 1)
                pe.wait_ge(copied, g + 1)
                for j in range(GB):
                    mm = nc.tensor.matmul(m1[:, j * E_:(j + 1) * E_], x2_t[:, j * 128:(j + 1) * 128], rw[:], start=True, stop=True)
                mm.then_inc(logits, 1)
                pe.wait_ge(chosen_done, g + 1)
                nc.tensor.matmul(m2[:, 0:GB * E_], earlier[:], chosen[:].rearrange("p j e -> p (j e)"), start=True, stop=True)
                nc.tensor.matmul(m2[:, 64:64 + GB * E_], ones_b[:], chosen[:].rearrange("p j e -> p (j e)"), start=True, stop=True).then_inc(counted, 1)

        @block.scalar
        def _(act):
            with act.Fori(0, G) as g:
                act.wait_ge(scattered, 16 * TOPK * GB * g)
                src = x2_all[:, bass.ds(g * GB, GB), :]
                for k in range(TOPK):
                    op = nc.scalar.activation(stage[:, k, :, 0:D], src, ACT.Copy)
                op.then_inc(staged, 1)
                act.wait_ge(turned, g + 1)
                nc.scalar.activation(x2_t[:], m0[:], ACT.Copy).then_inc(copied, 1)
                act.wait_ge(shift_done, g + 1)
                nc.scalar.activation(w8["expo"][:], w8["shifted_logit"][:], ACT.Exp).then_inc(exped, 1)
                act.wait_ge(gap_done, g + 1)
                nc.scalar.activation(w1["egap"][:], w1["gap"][:], ACT.Exp).then_inc(gap_exped, 1)

        @block.vector
        def _(dve):
            v = nc.vector
            v.memset(run[:, GB], 0.0)
            v.memset(id_base[:], 0).then_inc(base_done, 1)
            dve.wait_ge(const_in, 32)
            dve.wait_ge(consts, CONSTS)
            STEPS = 27
            with dve.Fori(0, G) as g:
                n = [0]

                def link(op):
                    n[0] += 1
                    op.then_inc(step, 1)
                    dve.wait_ge(step, g * STEPS + n[0])

                dve.wait_ge(logits, g + 1)
                link(v.tensor_tensor(w8["logit"][:], m1[:, 0:GB * E_].rearrange("p (j e) -> p j e", e=E_), rows(rb_rows[:]), ALU.add))
                link(v.tensor_reduce(w1["top"][:], w8["logit"][:], AX.X, ALU.max))
                v.tensor_tensor(w8["shifted_logit"][:], w8["logit"][:], rep(w1["top"][:]), ALU.subtract).then_inc(shift_done, 1)
                dve.wait_ge(exped, g + 1)
                link(v.tensor_reduce(w1["total"][:], w8["expo"][:], AX.X, ALU.add))
                link(v.reciprocal(w1["inv"][:], w1["total"][:]))
                link(v.tensor_tensor(w8["prob"][:], w8["expo"][:], rep(w1["inv"][:]), ALU.mult))
                link(v.tensor_reduce(w1["best"][:], w8["prob"][:], AX.X, ALU.max))
                link(v.tensor_tensor(w8["equal"][:], w8["prob"][:], rep(w1["best"][:]), ALU.is_equal))
                link(v.tensor_tensor(w8["sel"][:], w8["equal"][:], rows(first_weight[:]), ALU.mult))
                link(v.tensor_reduce(w1["first"][:], w8["sel"][:], AX.X, ALU.max))
                link(v.tensor_tensor(w8["one_a"][:], w8["sel"][:], rep(w1["first"][:]), ALU.is_equal))
                link(v.scalar_tensor_tensor(w8["prob_b"][:], w8["one_a"][:], -2.0, w8["prob"][:], ALU.mult, ALU.add))
                link(v.tensor_reduce(w1["best_b"][:], w8["prob_b"][:], AX.X, ALU.max))
                v.tensor_tensor(w1["gap"][:], w1["best_b"][:], w1["best"][:], ALU.subtract).then_inc(gap_done, 1)
                link(v.tensor_tensor(w8["equal_b"][:], w8["prob_b"][:], rep(w1["best_b"][:]), ALU.is_equal))
                link(v.tensor_tensor(w8["sel_b"][:], w8["equal_b"][:], rows(first_weight[:]), ALU.mult))
                link(v.tensor_reduce(w1["first_b"][:], w8["sel_b"][:], AX.X, ALU.max))
                link(v.tensor_tensor(w8["one_b"][:], w8["sel_b"][:], rep(w1["first_b"][:]), ALU.is_equal))
                v.tensor_tensor(chosen[:], w8["one_a"][:], w8["one_b"][:], ALU.add).then_inc(chosen_done, 1)
                dve.wait_ge(gap_exped, g + 1)
                link(v.tensor_scalar(w1["den"][:], w1["egap"][:], 1.0, None, ALU.add))
                link(v.reciprocal(w1["inv2"][:], w1["den"][:]))
                v.tensor_copy(weights[:, 0, bass.ds(g * GB, GB)], w1["inv2"][:])
                v.tensor_tensor(weights[:, 1, bass.ds(g * GB, GB)], w1["egap"][:], w1["inv2"][:], ALU.mult)
                dve.wait_ge(counted, g + 1)
                link(v.tensor_copy(run[:, 0], run[:, GB]))
                for j in range(GB):
                    link(v.tensor_tensor(run[:, j + 1], run[:, j], m2[:, 64 + j * E_:64 + (j + 1) * E_], ALU.add))
                link(v.tensor_tensor(w8["pos"][:], m2[:, 0:GB * E_].rearrange("p (j e) -> p j e", e=E_), run[:, 0:GB], ALU.add))
                link(v.tensor_tensor(w8["pos"][:], w8["pos"][:], rows(region[:]), ALU.add))
                v.tensor_tensor(w8["pick_a"][:], w8["pos"][:], w8["one_a"][:], ALU.mult)
                link(v.tensor_tensor(w8["pick_b"][:], w8["pos"][:], w8["one_b"][:], ALU.mult))
                v.tensor_reduce(w1["slot_a"][:], w8["pick_a"][:], AX.X, ALU.add)
                link(v.tensor_reduce(w1["slot_b"][:], w8["pick_b"][:], AX.X, ALU.add))
                dve.wait_ge(scattered, 16 * TOPK * GB * g)
                v.tensor_copy(slot[:, 0], w1["slot_a"][:])
                v.tensor_copy(slot[:, 1], w1["slot_b"][:]).then_inc(slot_done, 1)
                assert n[0] == STEPS, n[0]

            m = [STEPS * G]

            def then(op):
                m[0] += 1
                op.then_inc(step, 1)
                dve.wait_ge(step, m[0])

            count = run[0:1, GB]
            then(v.tensor_tensor(pad_at[:], count, region[0:1], ALU.add))
            v.tensor_copy(pad_row[:], pad_at[:]).then_inc(last_count, 1)
            then(v.tensor_tensor(nb3[:], count.unsqueeze(2).to_broadcast([1, E_, 16]), jt[:].unsqueeze(1).to_broadcast([1, E_, 16]), ALU.is_gt))
            then(v.tensor_reduce(nb[:], nb3[:], AX.X, ALU.add))
            then(v.tensor_tensor(end3[:], tri[:], nb[:].unsqueeze(1).to_broadcast([1, E_, E_]), ALU.mult))
            then(v.tensor_reduce(end[:], end3[:], AX.X, ALU.add))
            then(v.tensor_tensor(start[:], end[:], nb[:], ALU.subtract))
            many = lambda ap: ap.unsqueeze(1).to_broadcast([1, BLOCKS, E_])
            then(v.tensor_tensor(past[:], jb[:], many(end[:]), ALU.is_ge))
            then(v.tensor_tensor(reached[:], jb[:], many(start[:]), ALU.is_ge))
            then(v.tensor_tensor(inside[:], reached[:], past[:], ALU.subtract))
            then(v.scalar_tensor_tensor(base8[:], start[:], -float(BLK), region[0:1], ALU.mult, ALU.add))
            then(v.scalar_tensor_tensor(at8[:], jb[:], float(BLK), many(base8[:]), ALU.mult, ALU.add))
            then(v.tensor_tensor(at8b[:], at8[:], inside[:], ALU.mult))
            v.tensor_reduce(brow[:], at8b[:], AX.X, ALU.add)
            v.tensor_reduce(used[:], inside[:], AX.X, ALU.add)
            then(v.tensor_reduce(bexp[:], past[:], AX.X, ALU.add))
            then(v.tensor_scalar(used0[:], used[:], -1.0, 1.0, ALU.mult, ALU.add))
            then(v.scalar_tensor_tensor(spare[:], jb[:, :, 0], end[:, E_ - 1:E_], used0[:], ALU.subtract, ALU.mult))
            then(v.tensor_scalar(spare2[:], spare[:], float(BLK), None, ALU.mult))
            then(v.scalar_tensor_tensor(brow2[:], used0[:], float(NULL_ROW), spare2[:], ALU.mult, ALU.add))
            then(v.tensor_tensor(brow3[:], brow2[:], brow[:], ALU.add))
            then(v.tensor_scalar(bexp2[:], bexp[:], float(E_ - 1), None, ALU.min))
            v.tensor_copy(block_row[:], brow3[:])
            then(v.tensor_copy(block_expert[:], bexp2[:]))


def experts(nc, ctx, t, x2_all, weights, counts_tab, rows_dram, out, banks):
    sb = lambda n, s, d=fp32: ctx.enter_context(nc.sbuf_tensor(n, s, d))
    sem = lambda n: ctx.enter_context(nc.semaphore(n))
    i32 = mybir.dt.int32
    block_expert, block_row = counts_tab
    two = lambda n, s, d=fp32: [sb(f"{n}{i}", s, d) for i in range(2)]
    w1 = two("w1_", [D, FF])
    w2 = sb("w2_all", [128, E_, FC, D])
    b1 = sb("b1_all", [128, E_, FC])
    b2 = sb("b2_all", [128, E_, D])
    ident = sb("ident_e", [128, 128])
    xr = two("x_rows", [128, BLK // 128, ROW])
    xt = two("x_t", [D, BLK])
    hid = two("hidden", [128, FC, BLK])
    res = [sb(f"result{r}", [128, BLK // 128, D]) for r in range(4)]
    where = [sb(f"where{r}", [128, BLK // 128], i32) for r in range(4)]
    const_in, consts = sem("e_const_in"), sem("e_consts")
    passed = sem("e_passed")
    ident_zero = sem("e_ident_zero")
    w1_in = [sem(f"w1_in{i}") for i in range(2)]
    x_in = [sem(f"rows_in{i}") for i in range(2)]
    x_turned, x_copied, up_done, gelu_done, down_done, res_done, where_done = (sem(f"e_{n}") for n in (
        "x_turned", "x_copied", "up_done", "gelu_done", "down_done", "res_done", "where_done"))
    placed = [sem(f"e_placed{r}") for r in range(4)]
    xb, hb, yb = banks
    result_dram = nc.dram_tensor("result_dram", (TRASH + PADS * BLK, D), fp32, kind="Internal").ap()

    NT2 = BLK // 128
    LAST = BLOCKS - 1

    def turns(engine, body):
        for r in range(4):
            body(0, r)
        with engine.Fori(1, BLOCKS // 4) as n:
            for r in range(4):
                body(n, r)
        for r in range(BLOCKS % 4):
            body(BLOCKS // 4, r)

    def follower(n, r):
        return (n, r + 1) if r < 3 else (n + 1, 0)

    def is_last(n, r):
        return isinstance(n, int) and 4 * n + r == LAST

    def expert_of(engine, j):
        return engine.value_load(block_expert[0:1, bass.ds(j, 1)], min_val=0, max_val=E_ - 1)

    with nc.Block() as block:
        @block.sync
        def _(sp):
            def consts_in():
                sp.dma_start(b1[:], t["L0_xattn_e_b1"].rearrange("e (c p) -> p e c", p=128),
                             allow_slow_non_contiguous=True).then_inc(const_in, 16)
                sp.dma_start(w2[:], t["L0_xattn_e_w2"].rearrange("e (c p) d -> p e c d", p=128)).then_inc(const_in, 16)
                sp.dma_start(b2[:], t["L0_xattn_e_b2"].partition_broadcast(128)).then_inc(const_in, 16)

            def body(n, r):
                j, i = 4 * n + r, r % 2
                e = expert_of(sp, j)
                at = sp.value_load(block_row[0:1, bass.ds(j, 1)], min_val=0, max_val=NULL_ROW + (SPARE - 1) * BLK)
                wait(sp, x_turned, j - 1)
                wait(sp, where_done, j - 1)
                sp.dma_start(xr[i][:], rows_dram[bass.ds(at, BLK)].rearrange("(a p) r -> p a r", p=128)).then_inc(x_in[i], 16)
                wait(sp, up_done, FC * (j - 1))
                sp.dma_start(w1[i][:], t["L0_xattn_e_w1"][bass.ds(e, 1)].rearrange("a d f -> d (a f)")).then_inc(w1_in[i], 16)
                if isinstance(n, int) and j == 1:
                    consts_in()

            turns(sp, body)

        @block.tensor
        def _(pe):
            pe.wait_ge(consts, 1)

            def up(n, r):
                j, i = 4 * n + r, r % 2
                pe.wait_ge(x_in[i], 16 * (2 * n + r // 2 + 1))
                wait(pe, x_copied, j - 1)
                for a in range(NT2):
                    mm = nc.tensor.transpose(xb[i][:, a * 128:(a + 1) * 128], xr[i][:, a, 0:D], ident[:])
                mm.then_inc(x_turned, 1)
                pe.wait_ge(w1_in[i], 16 * (2 * n + r // 2 + 1))
                pe.wait_ge(x_copied, j + 1)
                for c in range(FC):
                    if c % 2 == 0:
                        wait(pe, gelu_done, FC * (j - 2) + c + 2)
                    nc.tensor.matmul(hb[2 * i + c // 2][:, c % 2 * BLK:(c % 2 + 1) * BLK], w1[i][:, c * 128:(c + 1) * 128], xt[i][:],
                                     start=True, stop=True).then_inc(up_done, 1)

            def down(n, r):
                j, i = 4 * n + r, r % 2
                e = expert_of(pe, j)
                pe.wait_ge(gelu_done, FC * (j + 1))
                wait(pe, res_done, j - 1)
                for a in range(NT2):
                    for c in range(FC):
                        mm = nc.tensor.matmul(yb[i][:, a * D:(a + 1) * D], hid[i][:, c, a * 128:(a + 1) * 128],
                                              w2[:, bass.ds(e, 1), c, :].rearrange("p a d -> p (a d)"), start=c == 0, stop=c == FC - 1)
                mm.then_inc(down_done, 1)

            def body(n, r):
                if not is_last(n, r):
                    up(*follower(n, r))
                if isinstance(n, int) and 4 * n + r == 0:
                    pe.wait_ge(const_in, 48)
                down(n, r)

            up(0, 0)
            turns(pe, body)

        @block.scalar
        def _(act):
            act.wait_ge(const_in, 48)

            def body(n, r):
                j, i = 4 * n + r, r % 2
                e = expert_of(act, j)
                for c in range(FC):
                    act.wait_ge(up_done, FC * j + c + 1 if c % 2 else FC * j + c + 2)
                    if c == 0:
                        wait(act, down_done, j - 1)
                    nc.scalar.activation(hid[i][:, c, :], hb[2 * i + c // 2][:, c % 2 * BLK:(c % 2 + 1) * BLK], ACT.Gelu,
                                         bias=b1[:, bass.ds(e, 1), c]).then_inc(gelu_done, 1)

            turns(act, body)

        @block.vector
        def _(dve):
            def copy_x(n, r):
                j, i = 4 * n + r, r % 2
                dve.wait_ge(x_turned, j + 1)
                wait(dve, up_done, FC * (j - 1))
                nc.vector.tensor_copy(xt[i][:], xb[i][:, 0:BLK]).then_inc(x_copied, 1)
                wait(dve, placed[r], 16 * NT2 * n)
                nc.vector.tensor_copy(where[r][:], xr[i][:, :, D].bitcast(i32)).then_inc(where_done, 1)

            def finish(n, r):
                j, i = 4 * n + r, r % 2
                e = expert_of(dve, j)
                dve.wait_ge(down_done, j + 1)
                nc.vector.tensor_tensor(res[r][:], yb[i][:, 0:NT2 * D].rearrange("p (a d) -> p a d", d=D),
                                        b2[:, bass.ds(e, 1), :].to_broadcast([128, NT2, D]), ALU.add).then_inc(res_done, 1)

            def body(n, r):
                if not is_last(n, r):
                    copy_x(*follower(n, r))
                if isinstance(n, int) and 4 * n + r == 0:
                    dve.wait_ge(const_in, 48)
                finish(n, r)

            copy_x(0, 0)
            turns(dve, body)

        @block.gpsimd
        def _(pool):
            nc.gpsimd.memset(ident[:], 0.0).then_inc(ident_zero, 1)
            pool.wait_ge(ident_zero, 1)
            nc.gpsimd.affine_select(out=ident[:], in_=ident[:], compare_op=ALU.not_equal, fill=1.0, base=0,
                                    pattern=[[-1, 128]], channel_multiplier=1).then_inc(consts, 1)

            def body(n, r):
                j = 4 * n + r
                wait_apart(pool, res_done, j + 1, passed)
                wait_apart(pool, where_done, j + 1, passed)
                for a in range(NT2):
                    nc.gpsimd.indirect_dma_start(result_dram, bass.IndirectOffsetOnAxis(ap=where[r][:, a:a + 1], axis=0),
                                                 res[r][:, a, :], None).then_inc(placed[r], 16)

            turns(pool, body)
            for r in range(4):
                pool.wait_ge(placed[r], 16 * NT2 * ((BLOCKS + 3 - r) // 4))

    with ExitStack() as c2:
        sb = lambda n, s, d=fp32: c2.enter_context(nc.sbuf_tensor(n, s, d))
        sem = lambda n: c2.enter_context(nc.semaphore(n))
        y = [sb(f"f_y{i}", [128, TOPK, GB, D]) for i in range(2)]
        part, summed, zt, zg, outt = ([sb(f"f_{n}{i}", [128, GB, D]) for i in range(2)] for n in ("part", "summed", "z", "zg", "out"))
        st, mv = [sb(f"f_st{i}", [128, GB, 6]) for i in range(2)], [sb(f"f_mv{i}", [128, GB, 2]) for i in range(2)]
        ve, rs = [sb(f"f_ve{i}", [128, GB]) for i in range(2)], [sb(f"f_rs{i}", [128, GB]) for i in range(2)]
        g_rows, b_rows, mh = sb("f_g", [128, D]), sb("f_b", [128, D]), sb("f_mh", [128, GB])
        f_in = [sem(f"f_in{i}") for i in range(2)]
        c_in, part_done, sum_done, st_done, mv_done, ve_done, rs_done, z_done, zg_done, o_done = (sem(f"f_{n}") for n in (
            "c_in", "part_done", "sum_done", "st_done", "mv_done", "ve_done", "rs_done", "z_done", "zg_done", "o_done"))
        stored = [sem(f"f_stored{i}") for i in range(2)]
        out_v = out.rearrange("(g b) s d -> g s b d", b=GB)
        with nc.Block() as block:
            @block.sync
            def _(sp):
                sp.dma_start(g_rows[:], t["L0_xattn_ln3_g"].partition_broadcast(128)).then_inc(c_in, 16)
                sp.dma_start(b_rows[:], t["L0_xattn_ln3_b"].partition_broadcast(128)).then_inc(c_in, 16)

                def load(g, i):
                    for k in range(TOPK):
                        src = result_dram[k * TOK:(k + 1) * TOK].rearrange("(g j p) d -> g p j d", j=GB, p=128)[g]
                        sp.dma_start(y[i][:, k], src).then_inc(f_in[i], 16)

                load(0, 0)
                load(1, 1)
                for g in range(G):
                    if g + 2 < G:
                        sp.wait_ge(sum_done, GB * (g + 1))
                        load(g + 2, g % 2)
                    sp.wait_ge(o_done, g + 1)
                    sp.dma_start(out_v[g], outt[g % 2][:]).then_inc(stored[g % 2], 16)
                for i in range(2):
                    sp.wait_ge(stored[i], 16 * G // 2)

            @block.vector
            def _(dve):
                v = nc.vector

                def norm(g):
                    i = g % 2
                    dve.wait_ge(rs_done, g + 1)
                    for j in range(GB):
                        op = v.tensor_scalar(zt[i][:, j], summed[i][:, j], mv[i][:, j, 0:1], rs[i][:, j:j + 1], ALU.subtract, ALU.mult)
                    op.then_inc(z_done, 1)

                for g in range(G):
                    i = g % 2
                    dve.wait_ge(f_in[i], 32 * (g // 2 + 1))
                    for j in range(GB):
                        op = v.scalar_tensor_tensor(part[i][:, j], y[i][:, 0, j], weights[:, 0, GB * g + j:GB * g + j + 1],
                                                    x2_all[:, GB * g + j], ALU.mult, ALU.add).then_inc(part_done, 1)
                    for j in range(GB):
                        dve.wait_ge(part_done, GB * g + j + 1)
                        v.scalar_tensor_tensor(summed[i][:, j], y[i][:, 1, j], weights[:, 1, GB * g + j:GB * g + j + 1],
                                               part[i][:, j], ALU.mult, ALU.add).then_inc(sum_done, 1)
                    for j in range(GB):
                        dve.wait_ge(sum_done, GB * g + j + 1)
                        v.bn_stats(st[i][:, j], summed[i][:, j]).then_inc(st_done, 1)
                    for j in range(GB):
                        dve.wait_ge(st_done, GB * g + j + 1)
                        op = v.bn_aggr(mv[i][:, j], st[i][:, j])
                    op.then_inc(mv_done, 1)
                    if g:
                        norm(g - 1)
                norm(G - 1)

            @block.gpsimd
            def _(pool):
                nc.gpsimd.memset(mh[:], -0.5).then_inc(c_in, 16)
                pool.wait_ge(c_in, 48)
                rr = lambda ap: ap[:].unsqueeze(1).to_broadcast([128, GB, D])
                for g in range(G):
                    i = g % 2
                    wait_apart(pool, mv_done, g + 1, passed)
                    nc.gpsimd.tensor_scalar(ve[i][:], mv[i][:, :, 1], EPS, None, ALU.add).then_inc(ve_done, 1)
                    wait_apart(pool, ve_done, g + 1, passed)
                    nc.gpsimd.tensor_tensor(rs[i][:], ve[i][:], mh[:], ALU.pow).then_inc(rs_done, 1)
                    wait_apart(pool, z_done, g + 1, passed)
                    nc.gpsimd.tensor_tensor(zg[i][:], zt[i][:], rr(g_rows), ALU.mult).then_inc(zg_done, 1)
                    wait_apart(pool, zg_done, g + 1, passed)
                    if g >= 2:
                        pool.wait_ge(stored[i], 16 * (g // 2))
                    nc.gpsimd.tensor_tensor(outt[i][:], zg[i][:], rr(b_rows), ALU.add).then_inc(o_done, 1)


def decoder_layer(nc, t, out):
    with ExitStack() as ctx:
        banks = [ctx.enter_context(nc.psum_tensor(f"bank{i}", [128, 512], fp32)) for i in range(8)]
        x2_all = ctx.enter_context(nc.sbuf_tensor("x2_all", [128, NTILE, D], fp32))
        weights = ctx.enter_context(nc.sbuf_tensor("weights", [128, TOPK, NTILE], fp32))
        tables = [ctx.enter_context(nc.sbuf_tensor(n, [1, BLOCKS], mybir.dt.int32)) for n in ("block_expert", "block_row")]
        rows_dram = nc.dram_tensor("rows_dram", (NULL_ROW + SPARE * BLK, ROW), fp32, kind="Internal").ap()
        with ExitStack() as part:
            attention(nc, part, t, x2_all, banks)
        with ExitStack() as part:
            routing(nc, part, t, x2_all, weights, tables, rows_dram, banks[0:3])
        with ExitStack() as part:
            experts(nc, part, t, x2_all, weights, tables, rows_dram, out, (banks[0:2], banks[2:6], banks[6:8]))


def kernel(**inputs):
    import numpy as _np
    import concourse.bacc as _bacc
    from concourse import mybir as _mybir
    from concourse.bass_utils import run_bass_kernel_spmd as _run

    nc = _bacc.Bacc("TRN2", target_bir_lowering=False, num_devices=1)
    arrays, t = {}, {}
    for name, a in inputs.items():
        a = _np.ascontiguousarray(a)
        arrays[f"in_{name}"] = a
        t[name] = nc.dram_tensor(f"in_{name}", a.shape, _mybir.dt.from_np(a.dtype), kind="ExternalInput").ap()
    out = nc.dram_tensor("out", (B, SQ, D), _mybir.dt.float32, kind="ExternalOutput").ap()
    decoder_layer(nc, t, out)
    r = _run(nc, [arrays], core_ids=[0])
    return r.results[0]["out"]
```

```python
import concourse.bass as bass
from concourse import mybir
from contextlib import ExitStack

fp32 = mybir.dt.float32
bf16 = mybir.dt.bfloat16
ALU = mybir.AluOpType
ACT = mybir.ActivationFunctionType
AX = mybir.AxisListType

B, SQ, SK, D, H = 32, 128, 120, 128, 16
HD = D // H
GB = 4
G = B // GB
HB = GB // 2
NT = GB * SQ
NU = H // 4
NP = H // 2
SLOTS = 6
ROWS = 2 * SLOTS * HD
SHIFT = 3
EPS = 1e-5
SCORE_SCALE = 1.0 / float(HD) ** 0.5
MASKED = -1e30
SELF, CROSS = 0, 1
KEYS = (SQ, SK)


def before(kind, g):
    return (CROSS, g - 2) if kind == SELF else (SELF, g + 1)


def behind(kind, g):
    return (CROSS, g - 1) if kind == SELF else (SELF, g + 2)


def exists(g):
    return not isinstance(g, int) or 0 <= g < G


def last_before(kind, g):
    for _ in range(4):
        kind, g = before(kind, g)
        if exists(g):
            return kind, g
    return None


def two_batches_ago(kind, g, b):
    if b >= 2:
        return kind, g, b - 2
    p = last_before(kind, g)
    return None if p is None else (*p, b + 2)


def wait(engine, sem, value):
    if not isinstance(value, int) or value > 0:
        engine.wait_ge(sem, value)


def wait_apart(engine, sem, value, passed):
    if isinstance(value, int):
        return wait(engine, sem, value)
    engine.wait_ge(sem, value)
    engine.sem_inc(passed, 1)


def attention(nc, ctx, t, x2_all, banks):
    sb = lambda n, s, d=fp32: ctx.enter_context(nc.sbuf_tensor(n, s, d))
    both = lambda n, s, d=fp32: [sb(f"{n}_self", s, d), sb(f"{n}_cross", s, d)]
    sem = lambda n: ctx.enter_context(nc.semaphore(n))
    sems = lambda n: [sem(f"{n}_self"), sem(f"{n}_cross")]

    wq, wk, wv, wo = (both(n, [D, D]) for n in ("wq", "wk", "wv", "wo"))
    bq, bk = both("bq", [D, 1]), both("bk", [D, 1])
    bv_rows = both("bv_rows", [128, D])
    bo_rows = both("bo_rows", [128, D])
    ln_g_rows, ln_b_rows = both("ln_g_rows", [128, D]), both("ln_b_rows", [128, D])
    res_rows = sb("res_rows", [128, D])
    ln_g_col, ln_b_col = sb("ln_g_col", [D, 1]), sb("ln_b_col", [D, 1])
    ident = sb("ident", [128, 128])
    ident_b = sb("ident_b", [128, 128], bf16)
    mask = sb("mask", [128, 4, SQ], bf16)
    head_ones = sb("head_ones", [128, 160])
    minus_half = sb("minus_half", [128, GB])
    xin = [sb("xin_self", [SQ, GB, D]), sb("xin_cross", [SK, GB, D])]
    src_t = [sb("src_t_self", [D, GB * SQ]), sb("src_t_cross", [D, GB * SK])]
    x1_t = sb("x1_t", [D, NT])
    q_res, k_res = sb("q_res", [D, NT]), sb("k_res", [D, NT])
    q_parts, k_parts = both("q_parts", [D, 3, NT], bf16), both("k_parts", [D, 3, NT], bf16)
    q_diag = both("q_diag", [128, NP, 2, NT], bf16)
    k_pack = both("k_pack", [128, NP, NT], bf16)
    v_wide = both("v_wide", [128, GB, 4, 160])
    row_max = both("row_max", [SQ, GB, H])
    max_rest = sb("max_rest", [SQ, HB, H])
    max_parts = both("max_parts", [SQ, GB, 2, SHIFT, NP], bf16)
    max_t = both("max_t", [SHIFT * H, NT], bf16)
    probs = sb("probs", [128, 2, H, SQ])
    recip = sb("recip", [128, 2, SQ])
    heads_t = sb("heads_t", [128, 2, SQ])
    resid = both("resid", [SQ, GB, D])
    summed = both("summed", [SQ, GB, D])
    stats = both("stats", [SQ, GB, 6])
    mean_var = both("mean_var", [SQ, GB, 2])
    var_eps = both("var_eps", [SQ, GB])
    rstd = both("rstd", [SQ, GB])
    z = both("z", [SQ, GB, D])
    zg = both("zg", [SQ, GB, D])

    t_bank, n_bank, o_bank, (m0, m1) = banks[0:2], banks[2:4], banks[4:6], banks[6:8]
    VALUES, SUMS, ROWS_OUT = slice(0, 128), slice(128, 256), slice(256, 384)

    q_dram = [nc.dram_tensor(f"q_dram{k}", (D, SLOTS, NT), bf16, kind="Internal").ap() for k in (SELF, CROSS)]
    k_dram = [nc.dram_tensor(f"k_dram{k}", (D, SLOTS, GB * KEYS[k]), bf16, kind="Internal").ap() for k in (SELF, CROSS)]

    passed = sem("passed")
    const_in = sem("const_in")
    consts = sem("consts")
    const_step = sem("const_step")
    x_in = sems("x_in")
    src_done, src_copied = sems("src_done"), sems("src_copied")
    k_done, q_done, v_done = sems("k_done"), sems("q_done"), sems("v_done")
    k_first, q_first = sems("k_first"), sems("q_first")
    k_rest, q_rest = sems("k_rest"), sems("q_rest")
    k_split, q_split = sems("k_split"), sems("q_split")
    k_last, q_last = sems("k_last"), sems("q_last")
    k_stored, q_stored = sems("k_stored"), sems("q_stored")
    packed = [[sem(f"packed_{k}_{h}") for h in range(2)] for k in ("self", "cross")]
    v_copied = sems("v_copied")
    nat_done, max_done = sems("nat_done"), sems("max_done")
    m_part = sems("m_part")
    m_split = sems("m_split")
    m_turned, m_copied = sems("m_turned"), sems("m_copied")
    shifted = [[sem(f"shifted_{k}_{h}") for h in range(2)] for k in ("self", "cross")]
    t_done, exp_done = sems("t_done"), sems("exp_done")
    select_done = sem("select_done")
    pvs_done = sems("pvs_done")
    recip_done, heads_done = sems("recip_done"), sems("heads_done")
    y_done = sems("y_done")
    sum_done, stats_done, aggr_done = sems("sum_done"), sems("stats_done"), sems("aggr_done")
    eps_done, rstd_done, z_done = sems("eps_done"), sems("rstd_done"), sems("z_done")
    z_turned, x1_copied = sem("z_turned"), sem("x1_copied")
    zg_done, resid_done = sems("zg_done"), sems("resid_done")
    x2_done = sem("x2_done")

    block = ctx.enter_context(nc.Block())

    def stages(engine, stage):
        for it in (-1, 0, 1):
            stage(SELF, it)
            stage(CROSS, it - 1)
        with engine.Fori(2, G - 1) as it:
            stage(SELF, it)
            stage(CROSS, it - 1)
        for it in (G - 1, G):
            stage(SELF, it)
            stage(CROSS, it - 1)
        stage(SELF, G + 1)

    loads = []
    for k, p in ((SELF, "sa"), (CROSS, "ca")):
        for w, tile in (("wq", wq), ("wk", wk), ("wv", wv), ("wo", wo)):
            loads.append((tile[k][:], t[f"L0_xattn_{p}_{w}"]))
        for w, tile in (("bq", bq), ("bk", bk)):
            loads.append((tile[k][:], t[f"L0_xattn_{p}_{w}"].rearrange("(p a) -> p a", a=1)))
        for w, tile in (("bv", bv_rows), ("bo", bo_rows)):
            loads.append((tile[k][:], t[f"L0_xattn_{p}_{w}"].partition_broadcast(128)))
        loads.append((ln_g_rows[k][:], t[f"L0_xattn_ln{k + 1}_g"].partition_broadcast(128)))
        loads.append((ln_b_rows[k][:], t[f"L0_xattn_ln{k + 1}_b"].partition_broadcast(128)))
    loads.append((ln_g_col[:], t["L0_xattn_ln1_g"].rearrange("(p a) -> p a", a=1)))
    loads.append((ln_b_col[:], t["L0_xattn_ln1_b"].rearrange("(p a) -> p a", a=1)))
    ALL_LOADS = 16 * len(loads)
    CONSTS = 9

    @block.sync
    def _(sp):
        for dst, src in loads:
            sp.dma_start(dst, src).then_inc(const_in, 16)

        def shift_rows(kind, g, half):
            cols = slice(half * HB * SQ, (half + 1) * HB * SQ)
            wait(sp, m_copied[kind], 2 * g + half + 1)
            for c in range(2):
                r0 = ROWS + SHIFT * c
                sp.dma_start(q_diag[kind][r0:r0 + SHIFT, :, c, cols],
                             max_t[kind][SHIFT * NP * c:SHIFT * NP * (c + 1), cols]).then_inc(shifted[kind][half], 16)

        def stage(kind, g):
            nk, ng = behind(kind, g)
            if exists(g + 1):
                load_rows(kind, g + 1)
            if exists(g):
                shift_rows(kind, g, 1)
            if exists(g + 1):
                store(kind, g + 1, KEY, 0, k_first, slice(0, 3))
                store(kind, g + 1, QUERY, 0, q_first, slice(0, 4, 3))
                store(kind, g + 1, QUERY, 0, q_first, slice(5, 6))
                store(kind, g + 1, KEY, 1, k_split, slice(3, 5))
            if exists(ng):
                shift_rows(nk, ng, 0)
            if exists(g + 1):
                store(kind, g + 1, KEY, 2, k_last, slice(5, 6))
                store(kind, g + 1, QUERY, 1, q_split, slice(1, 5, 3))
                store(kind, g + 1, QUERY, 2, q_last, slice(2, 3))
                load_packed(kind, g + 1)

        def load_rows(kind, n):
            if kind == SELF:
                wait(sp, resid_done[SELF], n)
                src = t["x"].rearrange("(g b) s d -> g s b d", b=GB)[n]
            else:
                wait(sp, src_done[CROSS], n)
                src = t["ctx_1024"].rearrange("(g b) s d -> g s b d", b=GB)[n]
            sp.dma_start(xin[kind][:], src).then_inc(x_in[kind], 16)

        KEY, QUERY = (k_parts, k_dram, k_stored), (q_parts, q_dram, q_stored)

        def store(kind, n, what, part, ready, slots):
            parts, dram, stored = what
            wait(sp, ready[kind], n + 1)
            cols = GB * KEYS[kind] if what is KEY else NT
            copies = len(range(SLOTS)[slots])
            sp.dma_start(dram[kind][:, slots, :],
                         parts[kind][:, part, 0:cols].unsqueeze(1).to_broadcast([D, copies, cols])).then_inc(stored[kind], 16)

        def load_packed(kind, n):
            g = n - 1
            for half in range(2):
                wait_apart(sp, t_done[kind], 16 * g + 8 * (half + 1), passed)
                qc = slice(half * HB * SQ, (half + 1) * HB * SQ)
                kc = slice(half * HB * KEYS[kind], (half + 1) * HB * KEYS[kind])
                wait(sp, k_stored[kind], 16 * 3 * (n + 1))
                sp.dma_start(k_pack[kind][0:ROWS, :, kc],
                             k_dram[kind].rearrange("(a r) s t -> (r s) a t", a=NP)[:, :, kc]).then_inc(packed[kind][half], 16)
                wait(sp, q_stored[kind], 16 * 4 * (n + 1))
                for c in range(2):
                    sp.dma_start(q_diag[kind][ROWS // 2 * c:ROWS // 2 * (c + 1), :, c, qc],
                                 q_dram[kind].rearrange("(a c i) s t -> c (i s) a t", c=2, i=HD)[c, :, :, qc]).then_inc(packed[kind][half], 16)

        stages(sp, stage)
        for kind in (SELF, CROSS):
            sp.wait_ge(k_stored[kind], 16 * 3 * G)
            sp.wait_ge(q_stored[kind], 16 * 4 * G)

    @block.tensor
    def _(pe):
        pe.wait_ge(const_in, ALL_LOADS)
        pe.wait_ge(consts, CONSTS)

        def turn_shift(kind, g, half, clear):
            clear()
            wait_apart(pe, m_split[kind], 2 * g + half + 1, passed)
            for b in range(half * HB, (half + 1) * HB):
                out = m1[0:SHIFT * H, :].bitcast(bf16)[:, b * SQ:(b + 1) * SQ]
                last = nc.tensor.transpose(out, max_parts[kind][:, b].rearrange("p c r a -> p (c r a)"), ident_b[:])
            last.then_inc(m_turned[kind], 1)

        def stage(kind, g):
            nk, ng = behind(kind, g)
            pk, pg = before(kind, g)
            main = exists(g)

            def m1_clear(use):
                k_, g_, at = kind, g, use
                for _ in range(24):
                    at -= 1
                    if at < 0:
                        k_, g_ = before(k_, g_)
                        at = 3
                    if at == 0 and exists(g_):
                        return wait(pe, m_copied[k_], 2 * g_ + 2)
                    if at == 1 and k_ == CROSS and exists(before(k_, g_)[1]):
                        return wait(pe, x1_copied, before(k_, g_)[1] + 1)
                    if at == 2 and exists(g_ + 1):
                        wait(pe, k_first[k_], g_ + 2)
                        return wait(pe, k_rest[k_], g_ + 2)
                    if at == 3 and exists(behind(k_, g_)[1]):
                        k2, g2 = behind(k_, g_)
                        return wait(pe, m_copied[k2], 2 * g2 + 1)

            for b in range(GB):
                nat = (kind, g, GB - 1) if b == 0 else (nk, ng, b - 1)
                nat_before = (kind, g, GB - 2) if b == 0 else (kind, g, GB - 1) if b == 1 else (nk, ng, b - 2)
                last = (kind, g, b - 1) if b >= 1 else (pk, pg, GB - 1)
                for u in range(NU):
                    if main:
                        if b % HB == 0 and u == 0:
                            wait(pe, shifted[kind][b // HB], 32 * (g + 1))
                        if u >= 2:
                            wait(pe, exp_done[kind], 16 * g + 4 * b + u - 1)
                        elif b >= 1:
                            wait(pe, exp_done[kind], 16 * g + 4 * (b - 1) + u + 3)
                        elif (p := last_before(kind, g)) is not None:
                            wait(pe, exp_done[p[0]], 16 * p[1] + 12 + u + 3)
                        for i in range(2):
                            a = 2 * u + i
                            mm = nc.tensor.matmul(
                                t_bank[u % 2][0:KEYS[kind], i * 256:(i + 1) * 256].rearrange("p (c q) -> p c q", c=2),
                                k_pack[kind][:, a, b * KEYS[kind]:(b + 1) * KEYS[kind]],
                                q_diag[kind][:, a, :, b * SQ:(b + 1) * SQ], start=True, stop=True)
                        mm.then_inc(t_done[kind], 1)
                    if exists(nat[1]):
                        k_, g_, b_ = nat
                        if b_ % HB == 0 and u == 0:
                            wait(pe, packed[k_][b_ // HB], 16 * 3 * (g_ + 1))
                        if u >= 2:
                            wait(pe, max_done[k_], 16 * g_ + 4 * b_ + u - 1)
                        elif b_ >= 1:
                            wait(pe, max_done[k_], 16 * g_ + 4 * (b_ - 1) + u + 3)
                        else:
                            p = (kind, g) if exists(g) else last_before(kind, g)
                            if p is not None:
                                wait(pe, max_done[p[0]], 16 * p[1] + 12 + u + 3)
                        bank, keys = n_bank[u % 2], KEYS[k_]
                        if k_ == SELF:
                            nc.tensor.matmul(bank[:], ident_b[:], mask[:].rearrange("p h k -> p (h k)"), start=True, stop=False)
                        for i in range(4):
                            mm = nc.tensor.matmul(bank[:, i * keys:(i + 1) * keys],
                                                  q_diag[k_][0:ROWS, 2 * u + i // 2, i % 2, b_ * SQ:(b_ + 1) * SQ],
                                                  k_pack[k_][0:ROWS, 2 * u + i // 2, b_ * keys:(b_ + 1) * keys],
                                                  start=k_ == CROSS, stop=k_ == CROSS or i == 3)
                        mm.then_inc(nat_done[k_], 1)
                    ago = (kind, g, b - 2) if b >= 2 else (pk, pg, b + 2)
                    if (b, u) == (1, 1) and main:
                        turn_shift(kind, g, 1, lambda: m1_clear(0))
                    if (b, u) == (3, 1) and exists(ng):
                        turn_shift(nk, ng, 0, lambda: m1_clear(3))
                    if u in (1, 2) and exists(last[1]):
                        k_, g_, b_ = last
                        keys = KEYS[k_]
                        if u == 1:
                            if k_ == SELF:
                                wait(pe, select_done, 16 * g_ + 4 * b_ + 4)
                            else:
                                wait(pe, exp_done[k_], 16 * g_ + 4 * b_ + 4)
                            if b_ == 0:
                                wait(pe, v_copied[k_], g_ + 1)
                            if (w := two_batches_ago(*last)) is not None:
                                wait(pe, sum_done[w[0]], 4 * w[1] + w[2] + 1)
                        for c in range(4):
                            for j in range(4):
                                lhs = (v_wide[k_][0:keys, b_, j, 32 * c:32 * c + 32] if u == 1
                                       else head_ones[0:keys, 32 * c:32 * c + 32])
                                mm = nc.tensor.matmul(o_bank[b_ % 2][32 * j:32 * j + 32, VALUES if u == 1 else SUMS], lhs,
                                                      probs[0:keys, b_ % 2, 4 * j + c], start=c == 0, stop=c == 3)
                        if u == 2:
                            mm.then_inc(pvs_done[k_], 1)
                    if u == 1 and exists(ago[1]):
                        k_, g_, b_ = ago
                        wait(pe, heads_done[k_], 4 * g_ + b_ + 1)
                        nc.tensor.matmul(o_bank[b_ % 2][:, ROWS_OUT], heads_t[:, b_ % 2],
                                         wo[k_][:], start=True, stop=True).then_inc(y_done[k_], 1)
                    if (b, u) == (1, 1) and exists(ng):
                        keys = KEYS[nk]
                        wait(pe, q_first[nk], ng + 1)
                        wait(pe, q_rest[nk], ng + 1)
                        for j in range(GB):
                            mm = nc.tensor.matmul(m0[0:keys, j * D:(j + 1) * D], src_t[nk][:, j * keys:(j + 1) * keys],
                                                  wv[nk][:], start=True, stop=True)
                        mm.then_inc(v_done[nk], 1)
                    if (b, u) == (1, 3) and exists(g + 1):
                        keys = KEYS[kind]
                        wait(pe, x_in[kind], 16 * (g + 2))
                        if exists(ng):
                            wait(pe, v_copied[nk], ng + 1)
                        for j in range(GB):
                            mm = nc.tensor.transpose(m0[:, j * keys:(j + 1) * keys], xin[kind][:, j, :], ident[0:keys, 0:keys])
                        mm.then_inc(src_done[kind], 1)
                    if (b, u) == (2, 1) and kind == CROSS and exists(pg):
                        wait(pe, z_done[SELF], pg + 1)
                        m1_clear(1)
                        for j in range(GB):
                            mm = nc.tensor.transpose(m1[:, j * SQ:(j + 1) * SQ], z[SELF][:, j, :], ident[:])
                        mm.then_inc(z_turned, 1)
                    if (b, u) == (2, 2) and exists(g + 1):
                        KT = GB * KEYS[kind]
                        wait(pe, src_copied[kind], g + 2)
                        m1_clear(2)
                        nc.tensor.matmul(m1[:, 0:KT], wk[kind][:], src_t[kind][:, 0:KT], start=True, stop=True).then_inc(k_done[kind], 1)
                    if (b, u) == (2, 3) and exists(g + 1):
                        if kind == CROSS:
                            wait(pe, x1_copied, g + 2)
                        nc.tensor.matmul(m0[:], wq[kind][:], (x1_t if kind == CROSS else src_t[SELF])[:], start=True,
                                         stop=True).then_inc(q_done[kind], 1)

        stages(pe, stage)

    @block.scalar
    def _(act):
        act.wait_ge(const_in, ALL_LOADS)

        def copy_shift(kind, g, half):
            cols = slice(half * HB * SQ, (half + 1) * HB * SQ)
            wait(act, m_turned[kind], 2 * g + half + 1)
            nc.scalar.activation(max_t[kind][0:SHIFT * H, cols], m1[0:SHIFT * H, :].bitcast(bf16)[:, cols], ACT.Copy).then_inc(m_copied[kind], 1)

        def stage(kind, g):
            nk, ng = behind(kind, g)
            pk, pg = before(kind, g)
            keys = KEYS[kind]
            for b in range(GB):
                for u in range(NU):
                    if exists(g):
                        if u == 0 and (w := two_batches_ago(kind, g, b)) is not None:
                            wait(act, pvs_done[w[0]], 4 * w[1] + w[2] + 1)
                        wait(act, t_done[kind], 16 * g + 4 * b + u + 1)
                        nc.scalar.activation(probs[0:keys, b % 2, 4 * u:4 * u + 4].rearrange("p h q -> p (h q)"),
                                             t_bank[u % 2][0:keys, :], ACT.Exp, scale=SCORE_SCALE).then_inc(exp_done[kind], 1)
                    if (b, u) == (1, 1) and exists(g):
                        copy_shift(kind, g, 1)
                    if (b, u) == (3, 1) and exists(ng):
                        copy_shift(nk, ng, 0)
                    if (b, u) == (1, 3) and exists(g + 1):
                        wait(act, src_done[kind], g + 2)
                        nc.scalar.activation(src_t[kind][:], m0[:, 0:GB * keys], ACT.Copy).then_inc(src_copied[kind], 1)
                    if (b, u) == (2, 1) and kind == CROSS and exists(pg):
                        wait(act, z_turned, pg + 1)
                        nc.scalar.activation(x1_t[:], m1[:], ACT.Identity, bias=ln_b_col[:], scale=ln_g_col[:]).then_inc(x1_copied, 1)
                    if (b, u) == (2, 2) and exists(g + 1):
                        wait(act, k_done[kind], g + 2)
                        wait(act, k_stored[kind], 16 * 3 * (g + 1))
                        nc.scalar.activation(k_parts[kind][:, 0, 0:GB * keys], m1[:, 0:GB * keys], ACT.Identity,
                                             bias=bk[kind][:]).then_inc(k_first[kind], 1)
                    if (b, u) == (2, 3) and exists(g + 1):
                        wait(act, q_done[kind], g + 2)
                        wait(act, q_stored[kind], 16 * 4 * (g + 1))
                        nc.scalar.activation(q_parts[kind][:, 0, :], m0[:], ACT.Identity, bias=bq[kind][:]).then_inc(q_first[kind], 1)
                    if (b, u) == (3, 0) and exists(g + 1):
                        wait(act, k_rest[kind], g + 2)
                        nc.scalar.activation(k_parts[kind][:, 1, 0:GB * keys], k_res[:, 0:GB * keys], ACT.Copy).then_inc(k_split[kind], 1)
                    if (b, u) == (3, 1) and exists(g + 1):
                        wait(act, q_rest[kind], g + 2)
                        nc.scalar.activation(q_parts[kind][:, 1, :], q_res[:], ACT.Copy).then_inc(q_split[kind], 1)

        stages(act, stage)

    @block.vector
    def _(dve):
        nc.vector.memset(q_diag[SELF][:].rearrange("p a c t -> p (a c t)").bitcast(fp32), 0.0).then_inc(consts, 1)
        for kind in (SELF, CROSS):
            nc.vector.memset(k_pack[kind][96:128].rearrange("p a t -> p (a t)"), 1.0).then_inc(consts, 1)
        dve.wait_ge(const_in, ALL_LOADS)

        def split_shift(kind, g, half):
            hb = slice(half * HB, (half + 1) * HB)
            top = row_max[kind][:, hb].rearrange("p b (a c) -> p b c a", c=2)
            rest = max_rest[:].rearrange("p b (a c) -> p b c a", c=2)
            parts = [max_parts[kind][:, hb, :, r] for r in range(SHIFT)]
            wait(dve, max_done[kind], 16 * g + 8 * (half + 1))
            nc.vector.tensor_copy(parts[0], top).then_inc(m_part[kind], 1)
            wait(dve, m_part[kind], 3 * (2 * g + half) + 1)
            nc.vector.tensor_tensor(rest, top, parts[0], ALU.subtract).then_inc(m_part[kind], 1)
            wait(dve, m_part[kind], 3 * (2 * g + half) + 2)
            nc.vector.tensor_copy(parts[1], rest).then_inc(m_part[kind], 1)
            wait(dve, m_part[kind], 3 * (2 * g + half) + 3)
            nc.vector.tensor_tensor(parts[2], rest, parts[1], ALU.subtract).then_inc(m_split[kind], 1)

        def stage(kind, g):
            nk, ng = behind(kind, g)
            pk, pg = before(kind, g)
            for b in range(GB):
                nat = (kind, g, GB - 1) if b == 0 else (nk, ng, b - 1)
                last = (kind, g, b - 1) if b >= 1 else (pk, pg, GB - 1)
                ago = (kind, g, b - 2) if b >= 2 else (pk, pg, b + 2)
                for u in range(NU):
                    if exists(nat[1]):
                        k_, g_, b_ = nat
                        keys = KEYS[k_]
                        wait(dve, nat_done[k_], 16 * g_ + 4 * b_ + u + 1)
                        nc.vector.tensor_reduce(row_max[k_][:, b_, 4 * u:4 * u + 4],
                                                n_bank[u % 2][:, 0:4 * keys].rearrange("p (h k) -> p h k", h=4),
                                                AX.X, ALU.max, negate=True).then_inc(max_done[k_], 1)
                    if u == 2 and exists(ago[1]):
                        k_, g_, b_ = ago
                        wait(dve, y_done[k_], 4 * g_ + b_ + 1)
                        if b_ == 0:
                            wait(dve, resid_done[k_], g_ + 1)
                        nc.vector.tensor_tensor(summed[k_][:, b_], o_bank[b_ % 2][:, ROWS_OUT],
                                                resid[k_][:, b_], ALU.add).then_inc(sum_done[k_], 1)
                    if u == 2 and exists(ago[1]):
                        k_, g_, b_ = ago
                        wait(dve, sum_done[k_], 4 * g_ + b_ + 1)
                        nc.vector.bn_stats(stats[k_][:, b_], summed[k_][:, b_]).then_inc(stats_done[k_], 1)
                        wait_apart(dve, stats_done[k_], 4 * g_ + b_ + 1, passed)
                        nc.vector.bn_aggr(mean_var[k_][:, b_], stats[k_][:, b_]).then_inc(aggr_done[k_], 1)
                    if (b, u) == (1, 1) and exists(ng):
                        keys = KEYS[nk]
                        wait(dve, v_done[nk], ng + 1)
                        for j in range(GB):
                            out = v_wide[nk][0:keys, j].rearrange("p j (c r) -> p j c r", r=40)[:, :, :, 0:HD]
                            op = nc.vector.tensor_tensor(out, m0[0:keys, j * D:(j + 1) * D].rearrange("p (j c i) -> p j c i", j=4, i=HD),
                                                         bv_rows[nk][0:keys].rearrange("p (j c i) -> p j c i", j=4, i=HD), ALU.add)
                        op.then_inc(v_copied[nk], 1)
                    if (b, u) == (0, 3) and exists(g):
                        split_shift(kind, g, 1)
                    if (b, u) == (2, 3) and exists(ng):
                        split_shift(nk, ng, 0)
                    if (b, u) == (2, 3) and exists(g + 1):
                        KT = GB * KEYS[kind]
                        wait(dve, k_first[kind], g + 2)
                        nc.vector.scalar_tensor_tensor(k_res[:, 0:KT], m1[:, 0:KT], bk[kind][:], k_parts[kind][:, 0, 0:KT], ALU.add,
                                                       ALU.subtract).then_inc(k_rest[kind], 1)
                    if u == 3 and exists(last[1]):
                        k_, g_, b_ = last
                        wait(dve, pvs_done[k_], 4 * g_ + b_ + 1)
                        nc.vector.reciprocal(recip[:, b_ % 2], o_bank[b_ % 2][:, SUMS]).then_inc(recip_done[k_], 1)
                        wait(dve, recip_done[k_], 4 * g_ + b_ + 1)
                        nc.vector.tensor_tensor(heads_t[:, b_ % 2], o_bank[b_ % 2][:, VALUES], recip[:, b_ % 2],
                                                ALU.mult).then_inc(heads_done[k_], 1)
                    if (b, u) == (2, 0) and exists(pg):
                        wait(dve, rstd_done[pk], pg + 1)
                        for j in range(GB):
                            op = nc.vector.tensor_scalar(z[pk][:, j], summed[pk][:, j], mean_var[pk][:, j, 0:1], rstd[pk][:, j:j + 1],
                                                         ALU.subtract, ALU.mult)
                        op.then_inc(z_done[pk], 1)
                    if (b, u) == (3, 0) and exists(g + 1):
                        wait(dve, q_first[kind], g + 2)
                        nc.vector.scalar_tensor_tensor(q_res[:], m0[:], bq[kind][:], q_parts[kind][:, 0, :], ALU.add,
                                                       ALU.subtract).then_inc(q_rest[kind], 1)

        stages(dve, stage)

    @block.gpsimd
    def _(pool):
        nc.gpsimd.memset(ident[:], 0.0).then_inc(const_step, 1)
        nc.gpsimd.memset(mask[:].rearrange("p h k -> p (h k)"), 0.0).then_inc(const_step, 1)
        nc.gpsimd.memset(head_ones[:], 0.0).then_inc(const_step, 1)
        nc.gpsimd.memset(minus_half[:], -0.5)
        for kind in (SELF, CROSS):
            nc.gpsimd.memset(v_wide[kind][:].rearrange("p b j c -> p (b j c)"), 0.0).then_inc(consts, 1)
        pool.wait_ge(const_step, 3)
        nc.gpsimd.affine_select(out=ident[:], in_=ident[:], compare_op=ALU.not_equal, fill=1.0, base=0,
                                pattern=[[-1, 128]], channel_multiplier=1).then_inc(const_step, 1)
        nc.gpsimd.affine_select(out=mask[:], in_=mask[:], compare_op=ALU.is_ge, fill=MASKED, base=0,
                                pattern=[[0, 4], [-1, SQ]], channel_multiplier=1).then_inc(consts, 1)
        nc.gpsimd.memset(head_ones[:].rearrange("p (c r) -> p c r", r=40)[:, :, 0:HD], 1.0).then_inc(consts, 1)
        pool.wait_ge(const_step, 4)
        nc.gpsimd.tensor_copy(ident_b[:], ident[:]).then_inc(consts, 1)
        nc.gpsimd.memset(q_diag[CROSS][:].rearrange("p a c t -> p (a c t)").bitcast(fp32), 0.0).then_inc(consts, 1)
        pool.wait_ge(const_in, ALL_LOADS)
        nc.gpsimd.tensor_tensor(res_rows[:], ln_b_rows[SELF][:], bo_rows[CROSS][:], ALU.add).then_inc(const_step, 1)
        pool.wait_ge(const_step, 5)

        def rows(tile):
            return tile[:].unsqueeze(1).to_broadcast([128, GB, D])

        def second_result(g):
            wait_apart(pool, z_done[CROSS], g + 1, passed)
            wait_apart(pool, x2_done, g, passed)
            nc.gpsimd.tensor_tensor(zg[CROSS][:], z[CROSS][:], rows(ln_g_rows[CROSS]), ALU.mult).then_inc(zg_done[CROSS], 1)
            wait_apart(pool, zg_done[CROSS], g + 1, passed)
            nc.gpsimd.tensor_tensor(x2_all[:, bass.ds(g * GB, GB), :], zg[CROSS][:], rows(ln_b_rows[CROSS]), ALU.add).then_inc(x2_done, 1)

        def stage(kind, g):
            nk, ng = behind(kind, g)
            pk, pg = before(kind, g)
            for b in range(GB):
                for u in range(NU):
                    if kind == SELF and exists(g):
                        wait_apart(pool, exp_done[SELF], 16 * g + 4 * b + u + 1, passed)
                        p = probs[:, b % 2, 4 * u:4 * u + 4]
                        nc.gpsimd.affine_select(out=p, in_=p, compare_op=ALU.is_ge, fill=0.0, base=0,
                                                pattern=[[0, 4], [1, SQ]], channel_multiplier=-1).then_inc(select_done, 1)
                    if (b, u) == (0, 0) and kind == SELF and exists(g):
                        wait_apart(pool, sum_done[SELF], 4 * g, passed)
                        wait_apart(pool, x_in[SELF], 16 * (g + 1), passed)
                        nc.gpsimd.tensor_tensor(resid[SELF][:], xin[SELF][:], rows(bo_rows[SELF]), ALU.add).then_inc(resid_done[SELF], 1)
                    if (b, u) == (1, 2) and exists(pg):
                        wait_apart(pool, aggr_done[pk], 4 * (pg + 1), passed)
                        nc.gpsimd.tensor_scalar(var_eps[pk][:], mean_var[pk][:, :, 1], EPS, None, ALU.add).then_inc(eps_done[pk], 1)
                        wait_apart(pool, eps_done[pk], pg + 1, passed)
                        nc.gpsimd.tensor_tensor(rstd[pk][:], var_eps[pk][:], minus_half[:], ALU.pow).then_inc(rstd_done[pk], 1)
                    if (b, u) == (0, 0) and kind == CROSS and exists(g):
                        wait_apart(pool, z_done[SELF], g + 1, passed)
                        wait_apart(pool, sum_done[CROSS], 4 * g, passed)
                        wait_apart(pool, resid_done[CROSS], g, passed)
                        nc.gpsimd.tensor_tensor(zg[SELF][:], z[SELF][:], rows(ln_g_rows[SELF]), ALU.mult).then_inc(zg_done[SELF], 1)
                        wait_apart(pool, zg_done[SELF], g + 1, passed)
                        nc.gpsimd.tensor_tensor(resid[CROSS][:], zg[SELF][:], rows(res_rows), ALU.add).then_inc(resid_done[CROSS], 1)
                    if kind == CROSS and (b, u) == (1, 0) and exists(g - 1):
                        second_result(g - 1)
                    if kind == SELF and (b, u) == (2, 1) and isinstance(pg, int) and pg == G - 1:
                        second_result(pg)
                    for at, parts, rest, split_done, last_done, cols in (
                            ((3, 0), k_parts, k_res, k_split, k_last, GB * KEYS[kind]),
                            ((3, 1), q_parts, q_res, q_split, q_last, NT)):
                        if (b, u) == at and exists(g + 1):
                            wait_apart(pool, split_done[kind], g + 2, passed)
                            nc.gpsimd.tensor_tensor(parts[kind][:, 2, 0:cols], rest[:, 0:cols], parts[kind][:, 1, 0:cols],
                                                    ALU.subtract).then_inc(last_done[kind], 1)

        stages(pool, stage)


E_, FF, TOPK = 8, 512, 2
FC = FF // 128
TOK = B * SQ
NTILE = TOK // 128
BLK = 256
RS = TOK + BLK
NULL_ROW = E_ * RS
ROW = D + 1
BLOCKS = TOPK * TOK // BLK + E_ - 1
SPARE = BLOCKS - TOPK * TOK // BLK
TRASH = TOPK * TOK
PADS = E_ + SPARE


def routing(nc, ctx, t, x2_all, weights, counts_tab, rows_dram, banks, shared):
    sb = lambda n, s, d=fp32: ctx.enter_context(nc.sbuf_tensor(n, s, d))
    sem = lambda n: ctx.enter_context(nc.semaphore(n))
    i32 = mybir.dt.int32
    w2, b1, b2, ident, moe_in = shared
    block_expert, block_row = counts_tab
    rw, rb_rows = sb("rw", [D, E_]), sb("rb_rows", [128, E_])
    earlier = sb("earlier", [128, 128], bf16)
    ones_b = sb("ones_b", [128, 128], bf16)
    first_weight = sb("first_weight", [128, E_])
    region = sb("region", [128, E_])
    pad = sb("pad", [128, PADS, BLK // 128, ROW])
    stage = sb("stage", [128, TOPK, NTILE, ROW])
    x2_t = [sb(f"x2_t{i}", [D, NT]) for i in range(2)]
    names = ("logit", "shifted_logit", "expo", "prob", "equal", "sel", "one_a", "prob_b", "equal_b", "sel_b", "one_b",
             "within", "pos", "pick_a", "pick_b")
    w8 = {n: sb(f"r_{n}", [128, NTILE, E_]) for n in names}
    w1 = {n: sb(f"r_{n}", [128, NTILE]) for n in ("top", "total", "inv", "best", "first", "best_b", "first_b", "gap", "egap", "den")}
    chosen = sb("r_chosen", [128, NTILE, E_], bf16)
    ahead = [sb(f"r_ahead{i}", [128, NTILE, E_]) for i in range(2)]
    count_all = sb("r_count", [128, E_])
    slot_f = sb("r_slot_f", [128, TOPK, NTILE])
    slot = sb("r_slot", [128, TOPK, NTILE], i32)
    turn_bank, (logit_bank, count_bank) = banks[0:2], banks[2:4]
    NG = NTILE * E_
    within_cols, total_cols = count_bank[:, 0:NG], count_bank[:, NG:2 * NG]
    step, const_in, consts, const_step = sem("r_step"), sem("r_const_in"), sem("r_consts"), sem("r_const_step")
    staged, turned, copied, logits, exped, gap_exped, counted = (sem(f"r_{n}") for n in
        ("staged", "turned", "copied", "logits", "exped", "gap_exped", "counted"))
    shift_done, gap_done, chosen_done, slot_done, scattered = (sem(f"r_{n}") for n in
        ("shift_done", "gap_done", "chosen_done", "slot_done", "scattered"))
    padded, last_count = sem("r_padded"), sem("r_last_count")
    jt = sb("r_jt", [1, 16]); nb3 = sb("r_nb3", [1, E_, 16]); nb = sb("r_nb", [1, E_])
    tri = sb("r_tri", [1, E_, E_]); end3 = sb("r_end3", [1, E_, E_]); end = sb("r_end", [1, E_]); start = sb("r_start", [1, E_])
    jb = sb("r_jb", [1, BLOCKS, E_]); past = sb("r_past", [1, BLOCKS, E_]); reached = sb("r_reached", [1, BLOCKS, E_])
    inside = sb("r_inside", [1, BLOCKS, E_]); base8 = sb("r_base8", [1, E_]); at8 = sb("r_at8", [1, BLOCKS, E_]); at8b = sb("r_at8b", [1, BLOCKS, E_])
    bexp = sb("r_bexp", [1, BLOCKS]); used = sb("r_used", [1, BLOCKS]); brow = sb("r_brow", [1, BLOCKS]); brow2 = sb("r_brow2", [1, BLOCKS])
    used0, spare, spare2 = (sb(f"r_{n}", [1, BLOCKS]) for n in ("used0", "spare", "spare2"))
    bexp2 = sb("r_bexp2", [1, BLOCKS]); brow3 = sb("r_brow3", [1, BLOCKS])
    pad_at = sb("r_pad_at", [1, E_]); pad_row = sb("r_pad_row", [1, E_], i32)
    CONSTS = 9

    def rep(ap, n=E_):
        return ap.unsqueeze(2).to_broadcast([128, NTILE, n])

    def rows(ap):
        return ap.unsqueeze(1).to_broadcast([128, NTILE, E_])

    with nc.Block() as block:
        @block.sync
        def _(sp):
            sp.dma_start(rw[:], t["L0_xattn_router_w"]).then_inc(const_in, 16)
            sp.dma_start(rb_rows[:], t["L0_xattn_router_b"].partition_broadcast(128)).then_inc(const_in, 16)
            sp.dma_start(w2[:], t["L0_xattn_e_w2"].rearrange("e (c p) d -> p e c d", p=128)).then_inc(moe_in, 16)
            sp.dma_start(b1[:], t["L0_xattn_e_b1"].rearrange("e (c p) -> p e c", p=128),
                         allow_slow_non_contiguous=True).then_inc(moe_in, 16)
            sp.dma_start(b2[:], t["L0_xattn_e_b2"].partition_broadcast(128)).then_inc(moe_in, 16)
            sp.wait_ge(consts, CONSTS)
            sp.dma_start(rows_dram[NULL_ROW:NULL_ROW + SPARE * BLK].rearrange("(a p) r -> p a r", p=128),
                         pad[:, E_:PADS].rearrange("p n a r -> p (n a) r")).then_inc(padded, 16)
            sp.wait_ge(last_count, 1)
            for e in range(E_):
                at = sp.value_load(pad_row[0:1, e:e + 1], min_val=0, max_val=NULL_ROW - BLK)
                sp.dma_start(rows_dram[bass.ds(at, BLK)].rearrange("(a p) r -> p a r", p=128), pad[:, e]).then_inc(padded, 16)
            sp.wait_ge(padded, 16 * (E_ + 1))

        @block.gpsimd
        def _(pool):
            nc.gpsimd.memset(ident[:], 0.0).then_inc(const_step, 1)
            nc.gpsimd.memset(earlier[:], 1.0).then_inc(const_step, 1)
            nc.gpsimd.memset(ones_b[:], 1.0).then_inc(consts, 1)
            nc.gpsimd.memset(tri[:], 1.0).then_inc(const_step, 1)
            pool.wait_ge(const_step, 3)
            nc.gpsimd.affine_select(out=ident[:], in_=ident[:], compare_op=ALU.not_equal, fill=1.0, base=0,
                                    pattern=[[-1, 128]], channel_multiplier=1).then_inc(consts, 1)
            nc.gpsimd.affine_select(out=earlier[:], in_=earlier[:], compare_op=ALU.is_gt, fill=0.0, base=0,
                                    pattern=[[1, 128]], channel_multiplier=-1).then_inc(consts, 1)
            nc.gpsimd.iota(first_weight[:], [[-1, E_]], base=E_, channel_multiplier=0, allow_small_or_imprecise_dtypes=True).then_inc(consts, 1)
            nc.gpsimd.iota(region[:], [[RS, E_]], base=0, channel_multiplier=0, allow_small_or_imprecise_dtypes=True).then_inc(consts, 1)
            nc.gpsimd.iota(jt[:], [[BLK, 16]], base=0, channel_multiplier=0, allow_small_or_imprecise_dtypes=True).then_inc(consts, 1)
            nc.gpsimd.affine_select(out=tri[:], in_=tri[:], compare_op=ALU.is_ge, fill=0.0, base=0,
                                    pattern=[[1, E_], [-1, E_]], channel_multiplier=0).then_inc(consts, 1)
            nc.gpsimd.iota(jb[:], [[1, BLOCKS], [0, E_]], base=0, channel_multiplier=0, allow_small_or_imprecise_dtypes=True).then_inc(consts, 1)
            nc.gpsimd.memset(pad[:, :, :, 0:D], 0.0)
            nc.gpsimd.iota(pad[:, :, :, D:ROW].bitcast(i32), [[BLK, PADS], [128, BLK // 128], [0, 1]], base=TRASH,
                           channel_multiplier=1).then_inc(consts, 1)
            for k in range(TOPK):
                nc.gpsimd.iota(stage[:, k, :, D:ROW].bitcast(i32), [[128, NTILE], [0, 1]], base=k * TOK,
                               channel_multiplier=1).then_inc(const_step, 1)
            pool.wait_ge(const_step, 3 + TOPK)
            pool.wait_ge(staged, 8)
            pool.wait_ge(slot_done, 1)
            for j in range(NTILE):
                for k in range(TOPK):
                    nc.gpsimd.indirect_dma_start(rows_dram, bass.IndirectOffsetOnAxis(ap=slot[:, k, j:j + 1], axis=0),
                                                 stage[:, k, j, :], None).then_inc(scattered, 16)
            pool.wait_ge(scattered, 16 * TOPK * NTILE)

        @block.tensor
        def _(pe):
            pe.wait_ge(const_in, 32)
            pe.wait_ge(consts, CONSTS - 1)

            def logits_of(g):
                pe.wait_ge(copied, g + 1)
                for j in range(GB):
                    at = (GB * g + j) * E_
                    mm = nc.tensor.matmul(logit_bank[:, at:at + E_], x2_t[g % 2][:, j * 128:(j + 1) * 128], rw[:], start=True, stop=True)
                mm.then_inc(logits, 1)

            for g in range(G):
                if g >= 2:
                    pe.wait_ge(copied, g - 1)
                for j in range(GB):
                    mm = nc.tensor.transpose(turn_bank[g % 2][:, j * 128:(j + 1) * 128], x2_all[:, GB * g + j, :], ident[:])
                mm.then_inc(turned, 1)
                if g:
                    logits_of(g - 1)
            logits_of(G - 1)
            pe.wait_ge(chosen_done, 1)
            picks = chosen[:].rearrange("p j e -> p (j e)")
            nc.tensor.matmul(total_cols, ones_b[:], picks, start=True, stop=True)
            nc.tensor.matmul(within_cols, earlier[:], picks, start=True, stop=True).then_inc(counted, 1)

        @block.scalar
        def _(act):
            for g in range(G):
                act.wait_ge(turned, g + 1)
                wait(act, logits, g - 1)
                nc.scalar.activation(x2_t[g % 2][:], turn_bank[g % 2][:], ACT.Copy).then_inc(copied, 1)
            act.wait_ge(shift_done, 1)
            nc.scalar.activation(w8["expo"][:], w8["shifted_logit"][:], ACT.Exp).then_inc(exped, 1)
            quarter = NTILE // 4

            def rows_for_scatter(q, k):
                at = slice(q * quarter, (q + 1) * quarter)
                nc.scalar.activation(stage[:, k, at, 0:D], x2_all[:, at, :], ACT.Copy).then_inc(staged, 1)

            for q in range(4):
                rows_for_scatter(q, 0)
            act.wait_ge(gap_done, 1)
            nc.scalar.activation(w1["egap"][:], w1["gap"][:], ACT.Exp).then_inc(gap_exped, 1)
            for q in range(4):
                rows_for_scatter(q, 1)

        @block.vector
        def _(dve):
            v = nc.vector
            links = [0]

            def link(op):
                links[0] += 1
                op.then_inc(step, 1)
                dve.wait_ge(step, links[0])

            v.memset(ahead[0][:, 0], 0.0)
            dve.wait_ge(const_in, 32)
            dve.wait_ge(consts, CONSTS - 1)
            dve.wait_ge(logits, G)
            link(v.tensor_tensor(w8["logit"][:], logit_bank[:, 0:NG].rearrange("p (j e) -> p j e", e=E_), rows(rb_rows[:]), ALU.add))
            link(v.tensor_reduce(w1["top"][:], w8["logit"][:], AX.X, ALU.max))
            v.tensor_tensor(w8["shifted_logit"][:], w8["logit"][:], rep(w1["top"][:]), ALU.subtract).then_inc(shift_done, 1)
            dve.wait_ge(exped, 1)
            link(v.tensor_reduce(w1["total"][:], w8["expo"][:], AX.X, ALU.add))
            link(v.reciprocal(w1["inv"][:], w1["total"][:]))
            link(v.tensor_tensor(w8["prob"][:], w8["expo"][:], rep(w1["inv"][:]), ALU.mult))
            link(v.tensor_reduce(w1["best"][:], w8["prob"][:], AX.X, ALU.max))
            link(v.tensor_tensor(w8["equal"][:], w8["prob"][:], rep(w1["best"][:]), ALU.is_equal))
            link(v.tensor_tensor(w8["sel"][:], w8["equal"][:], rows(first_weight[:]), ALU.mult))
            link(v.tensor_reduce(w1["first"][:], w8["sel"][:], AX.X, ALU.max))
            link(v.tensor_tensor(w8["one_a"][:], w8["sel"][:], rep(w1["first"][:]), ALU.is_equal))
            link(v.scalar_tensor_tensor(w8["prob_b"][:], w8["one_a"][:], -2.0, w8["prob"][:], ALU.mult, ALU.add))
            link(v.tensor_reduce(w1["best_b"][:], w8["prob_b"][:], AX.X, ALU.max))
            link(v.tensor_tensor(w8["equal_b"][:], w8["prob_b"][:], rep(w1["best_b"][:]), ALU.is_equal))
            link(v.tensor_tensor(w8["sel_b"][:], w8["equal_b"][:], rows(first_weight[:]), ALU.mult))
            link(v.tensor_reduce(w1["first_b"][:], w8["sel_b"][:], AX.X, ALU.max))
            link(v.tensor_tensor(w8["one_b"][:], w8["sel_b"][:], rep(w1["first_b"][:]), ALU.is_equal))
            v.tensor_tensor(chosen[:], w8["one_a"][:], w8["one_b"][:], ALU.add).then_inc(chosen_done, 1)
            v.tensor_tensor(w1["gap"][:], w1["best_b"][:], w1["best"][:], ALU.subtract).then_inc(gap_done, 1)
            dve.wait_ge(counted, 1)
            totals = total_cols.rearrange("p (j e) -> p j e", e=E_)
            v.tensor_copy(w8["within"][:], within_cols.rearrange("p (j e) -> p j e", e=E_))
            link(v.tensor_copy(ahead[0][:, 1:NTILE], totals[:, 0:NTILE - 1]))
            span, now = 1, 0
            while span < NTILE:
                v.tensor_copy(ahead[1 - now][:, 0:span], ahead[now][:, 0:span])
                link(v.tensor_tensor(ahead[1 - now][:, span:NTILE], ahead[now][:, span:NTILE], ahead[now][:, 0:NTILE - span], ALU.add))
                span, now = 2 * span, 1 - now
            link(v.tensor_tensor(count_all[:], ahead[now][:, NTILE - 1], totals[:, NTILE - 1], ALU.add))
            count = count_all[0:1, :]
            link(v.tensor_tensor(pad_at[:], count, region[0:1], ALU.add))
            v.tensor_copy(pad_row[:], pad_at[:]).then_inc(last_count, 1)
            link(v.tensor_tensor(w8["pos"][:], w8["within"][:], ahead[now][:], ALU.add))
            link(v.tensor_tensor(w8["pos"][:], w8["pos"][:], rows(region[:]), ALU.add))
            v.tensor_tensor(w8["pick_a"][:], w8["pos"][:], w8["one_a"][:], ALU.mult)
            link(v.tensor_tensor(w8["pick_b"][:], w8["pos"][:], w8["one_b"][:], ALU.mult))
            v.tensor_reduce(slot_f[:, 0], w8["pick_a"][:], AX.X, ALU.add)
            link(v.tensor_reduce(slot_f[:, 1], w8["pick_b"][:], AX.X, ALU.add))
            v.tensor_copy(slot[:], slot_f[:]).then_inc(slot_done, 1)
            dve.wait_ge(gap_exped, 1)
            link(v.tensor_scalar(w1["den"][:], w1["egap"][:], 1.0, None, ALU.add))
            link(v.reciprocal(weights[:, 0], w1["den"][:]))
            v.tensor_tensor(weights[:, 1], w1["egap"][:], weights[:, 0], ALU.mult)
            link(v.tensor_tensor(nb3[:], count.unsqueeze(2).to_broadcast([1, E_, 16]), jt[:].unsqueeze(1).to_broadcast([1, E_, 16]), ALU.is_gt))
            link(v.tensor_reduce(nb[:], nb3[:], AX.X, ALU.add))
            link(v.tensor_tensor(end3[:], tri[:], nb[:].unsqueeze(1).to_broadcast([1, E_, E_]), ALU.mult))
            link(v.tensor_reduce(end[:], end3[:], AX.X, ALU.add))
            link(v.tensor_tensor(start[:], end[:], nb[:], ALU.subtract))
            many = lambda ap: ap.unsqueeze(1).to_broadcast([1, BLOCKS, E_])
            link(v.tensor_tensor(past[:], jb[:], many(end[:]), ALU.is_ge))
            link(v.tensor_tensor(reached[:], jb[:], many(start[:]), ALU.is_ge))
            link(v.tensor_tensor(inside[:], reached[:], past[:], ALU.subtract))
            link(v.scalar_tensor_tensor(base8[:], start[:], -float(BLK), region[0:1], ALU.mult, ALU.add))
            link(v.scalar_tensor_tensor(at8[:], jb[:], float(BLK), many(base8[:]), ALU.mult, ALU.add))
            link(v.tensor_tensor(at8b[:], at8[:], inside[:], ALU.mult))
            v.tensor_reduce(brow[:], at8b[:], AX.X, ALU.add)
            v.tensor_reduce(used[:], inside[:], AX.X, ALU.add)
            link(v.tensor_reduce(bexp[:], past[:], AX.X, ALU.add))
            link(v.tensor_scalar(used0[:], used[:], -1.0, 1.0, ALU.mult, ALU.add))
            link(v.scalar_tensor_tensor(spare[:], jb[:, :, 0], end[:, E_ - 1:E_], used0[:], ALU.subtract, ALU.mult))
            link(v.tensor_scalar(spare2[:], spare[:], float(BLK), None, ALU.mult))
            link(v.scalar_tensor_tensor(brow2[:], used0[:], float(NULL_ROW), spare2[:], ALU.mult, ALU.add))
            link(v.tensor_tensor(brow3[:], brow2[:], brow[:], ALU.add))
            link(v.tensor_scalar(bexp2[:], bexp[:], float(E_ - 1), None, ALU.min))
            v.tensor_copy(block_row[:], brow3[:])
            link(v.tensor_copy(block_expert[:], bexp2[:]))


def experts(nc, ctx, t, x2_all, weights, counts_tab, rows_dram, out, banks, shared):
    sb = lambda n, s, d=fp32: ctx.enter_context(nc.sbuf_tensor(n, s, d))
    sem = lambda n: ctx.enter_context(nc.semaphore(n))
    i32 = mybir.dt.int32
    block_expert, block_row = counts_tab
    two = lambda n, s, d=fp32: [sb(f"{n}{i}", s, d) for i in range(2)]
    w1 = two("w1_", [D, FF])
    w2, b1, b2, ident, moe_in = shared
    xr = two("x_rows", [128, BLK // 128, ROW])
    xt = two("x_t", [D, BLK])
    hid = two("hidden", [128, FC, BLK])
    res = [sb(f"result{r}", [128, BLK // 128, D]) for r in range(4)]
    where = [sb(f"where{r}", [128, BLK // 128], i32) for r in range(4)]
    passed = sem("e_passed")
    w1_in = [sem(f"w1_in{i}") for i in range(2)]
    x_in = [sem(f"rows_in{i}") for i in range(2)]
    x_turned, x_copied, up_done, gelu_done, down_done, res_done, where_done = (sem(f"e_{n}") for n in (
        "x_turned", "x_copied", "up_done", "gelu_done", "down_done", "res_done", "where_done"))
    placed = [sem(f"e_placed{r}") for r in range(4)]
    xb, hb, yb = banks
    result_dram = nc.dram_tensor("result_dram", (TRASH + PADS * BLK, D), fp32, kind="Internal").ap()

    NT2 = BLK // 128
    LAST = BLOCKS - 1

    def turns(engine, body):
        for r in range(4):
            body(0, r)
        with engine.Fori(1, BLOCKS // 4) as n:
            for r in range(4):
                body(n, r)
        for r in range(BLOCKS % 4):
            body(BLOCKS // 4, r)

    def follower(n, r):
        return (n, r + 1) if r < 3 else (n + 1, 0)

    def is_last(n, r):
        return isinstance(n, int) and 4 * n + r == LAST

    def expert_of(engine, j):
        return engine.value_load(block_expert[0:1, bass.ds(j, 1)], min_val=0, max_val=E_ - 1)

    with nc.Block() as block:
        @block.sync
        def _(sp):
            def body(n, r):
                j, i = 4 * n + r, r % 2
                e = expert_of(sp, j)
                at = sp.value_load(block_row[0:1, bass.ds(j, 1)], min_val=0, max_val=NULL_ROW + (SPARE - 1) * BLK)
                wait(sp, x_turned, j - 1)
                wait(sp, where_done, j - 1)
                sp.dma_start(xr[i][:], rows_dram[bass.ds(at, BLK)].rearrange("(a p) r -> p a r", p=128)).then_inc(x_in[i], 16)
                wait(sp, up_done, FC * (j - 1))
                sp.dma_start(w1[i][:], t["L0_xattn_e_w1"][bass.ds(e, 1)].rearrange("a d f -> d (a f)")).then_inc(w1_in[i], 16)

            turns(sp, body)

        @block.tensor
        def _(pe):
            pe.wait_ge(moe_in, 48)

            def turn(n, r):
                j, i = 4 * n + r, r % 2
                pe.wait_ge(x_in[i], 16 * (2 * n + r // 2 + 1))
                wait(pe, x_copied, j - 1)
                for a in range(NT2):
                    mm = nc.tensor.transpose(xb[i][:, a * 128:(a + 1) * 128], xr[i][:, a, 0:D], ident[:])
                mm.then_inc(x_turned, 1)

            def up(n, r):
                j, i = 4 * n + r, r % 2
                pe.wait_ge(w1_in[i], 16 * (2 * n + r // 2 + 1))
                pe.wait_ge(x_copied, j + 1)
                for c in range(FC):
                    if c % 2 == 0:
                        wait(pe, gelu_done, FC * (j - 2) + c + 2)
                    nc.tensor.matmul(hb[2 * i + c // 2][:, c % 2 * BLK:(c % 2 + 1) * BLK], w1[i][:, c * 128:(c + 1) * 128], xt[i][:],
                                     start=True, stop=True).then_inc(up_done, 1)

            def down(n, r):
                j, i = 4 * n + r, r % 2
                e = expert_of(pe, j)
                pe.wait_ge(gelu_done, FC * (j + 1))
                wait(pe, res_done, j - 1)
                for a in range(NT2):
                    for c in range(FC):
                        mm = nc.tensor.matmul(yb[i][:, a * D:(a + 1) * D], hid[i][:, c, a * 128:(a + 1) * 128],
                                              w2[:, bass.ds(e, 1), c, :].rearrange("p a d -> p (a d)"), start=c == 0, stop=c == FC - 1)
                mm.then_inc(down_done, 1)

            def body(n, r):
                if not is_last(n, r):
                    if not is_last(*follower(n, r)):
                        turn(*follower(*follower(n, r)))
                    up(*follower(n, r))
                down(n, r)

            turn(0, 0)
            turn(0, 1)
            up(0, 0)
            turns(pe, body)

        @block.scalar
        def _(act):
            act.wait_ge(moe_in, 48)

            def body(n, r):
                j, i = 4 * n + r, r % 2
                e = expert_of(act, j)
                for c in range(FC):
                    act.wait_ge(up_done, FC * j + c + 1 if c % 2 else FC * j + c + 2)
                    if c == 0:
                        wait(act, down_done, j - 1)
                    nc.scalar.activation(hid[i][:, c, :], hb[2 * i + c // 2][:, c % 2 * BLK:(c % 2 + 1) * BLK], ACT.Gelu,
                                         bias=b1[:, bass.ds(e, 1), c]).then_inc(gelu_done, 1)

            turns(act, body)

        @block.vector
        def _(dve):
            def copy_x(n, r):
                j, i = 4 * n + r, r % 2
                dve.wait_ge(x_turned, j + 1)
                wait(dve, up_done, FC * (j - 1))
                nc.vector.tensor_copy(xt[i][:], xb[i][:, 0:BLK]).then_inc(x_copied, 1)
                wait(dve, placed[r], 16 * NT2 * n)
                nc.vector.tensor_copy(where[r][:], xr[i][:, :, D].bitcast(i32)).then_inc(where_done, 1)

            def finish(n, r):
                j, i = 4 * n + r, r % 2
                e = expert_of(dve, j)
                dve.wait_ge(down_done, j + 1)
                nc.vector.tensor_tensor(res[r][:], yb[i][:, 0:NT2 * D].rearrange("p (a d) -> p a d", d=D),
                                        b2[:, bass.ds(e, 1), :].to_broadcast([128, NT2, D]), ALU.add).then_inc(res_done, 1)

            def body(n, r):
                if not (is_last(n, r) or is_last(*follower(n, r))):
                    copy_x(*follower(*follower(n, r)))
                finish(n, r)

            dve.wait_ge(moe_in, 48)
            copy_x(0, 0)
            copy_x(0, 1)
            turns(dve, body)

        @block.gpsimd
        def _(pool):
            def body(n, r):
                j = 4 * n + r
                wait_apart(pool, res_done, j + 1, passed)
                wait_apart(pool, where_done, j + 1, passed)
                for a in range(NT2):
                    nc.gpsimd.indirect_dma_start(result_dram, bass.IndirectOffsetOnAxis(ap=where[r][:, a:a + 1], axis=0),
                                                 res[r][:, a, :], None).then_inc(placed[r], 16)

            turns(pool, body)
            for r in range(4):
                pool.wait_ge(placed[r], 16 * NT2 * ((BLOCKS + 3 - r) // 4))

    with ExitStack() as c2:
        sb = lambda n, s, d=fp32: c2.enter_context(nc.sbuf_tensor(n, s, d))
        sem = lambda n: c2.enter_context(nc.semaphore(n))
        y = [sb(f"f_y{i}", [128, TOPK, GB, D]) for i in range(2)]
        part, summed, zt, zg, outt = ([sb(f"f_{n}{i}", [128, GB, D]) for i in range(2)] for n in ("part", "summed", "z", "zg", "out"))
        st, mv = [sb(f"f_st{i}", [128, GB, 6]) for i in range(2)], [sb(f"f_mv{i}", [128, GB, 2]) for i in range(2)]
        ve, rs = [sb(f"f_ve{i}", [128, GB]) for i in range(2)], [sb(f"f_rs{i}", [128, GB]) for i in range(2)]
        g_rows, b_rows, mh = sb("f_g", [128, D]), sb("f_b", [128, D]), sb("f_mh", [128, GB])
        f_in = [sem(f"f_in{i}") for i in range(2)]
        c_in, part_done, sum_done, st_done, mv_done, ve_done, rs_done, z_done, zg_done, o_done = (sem(f"f_{n}") for n in (
            "c_in", "part_done", "sum_done", "st_done", "mv_done", "ve_done", "rs_done", "z_done", "zg_done", "o_done"))
        stored = [sem(f"f_stored{i}") for i in range(2)]
        out_v = out.rearrange("(g b) s d -> g s b d", b=GB)
        with nc.Block() as block:
            @block.sync
            def _(sp):
                sp.dma_start(g_rows[:], t["L0_xattn_ln3_g"].partition_broadcast(128)).then_inc(c_in, 16)
                sp.dma_start(b_rows[:], t["L0_xattn_ln3_b"].partition_broadcast(128)).then_inc(c_in, 16)

                def load(g, i):
                    for k in range(TOPK):
                        src = result_dram[k * TOK:(k + 1) * TOK].rearrange("(g j p) d -> g p j d", j=GB, p=128)[g]
                        sp.dma_start(y[i][:, k], src).then_inc(f_in[i], 16)

                load(0, 0)
                load(1, 1)
                for g in range(G):
                    if g + 2 < G:
                        sp.wait_ge(sum_done, GB * (g + 1))
                        load(g + 2, g % 2)
                    sp.wait_ge(o_done, g + 1)
                    sp.dma_start(out_v[g], outt[g % 2][:]).then_inc(stored[g % 2], 16)
                for i in range(2):
                    sp.wait_ge(stored[i], 16 * G // 2)

            @block.vector
            def _(dve):
                v = nc.vector

                def norm(g):
                    i = g % 2
                    dve.wait_ge(rs_done, g + 1)
                    for j in range(GB):
                        op = v.tensor_scalar(zt[i][:, j], summed[i][:, j], mv[i][:, j, 0:1], rs[i][:, j:j + 1], ALU.subtract, ALU.mult)
                    op.then_inc(z_done, 1)

                for g in range(G):
                    i = g % 2
                    dve.wait_ge(f_in[i], 32 * (g // 2 + 1))
                    for j in range(GB):
                        op = v.scalar_tensor_tensor(part[i][:, j], y[i][:, 0, j], weights[:, 0, GB * g + j:GB * g + j + 1],
                                                    x2_all[:, GB * g + j], ALU.mult, ALU.add).then_inc(part_done, 1)
                    for j in range(GB):
                        dve.wait_ge(part_done, GB * g + j + 1)
                        v.scalar_tensor_tensor(summed[i][:, j], y[i][:, 1, j], weights[:, 1, GB * g + j:GB * g + j + 1],
                                               part[i][:, j], ALU.mult, ALU.add).then_inc(sum_done, 1)
                    for j in range(GB):
                        dve.wait_ge(sum_done, GB * g + j + 1)
                        v.bn_stats(st[i][:, j], summed[i][:, j]).then_inc(st_done, 1)
                    for j in range(GB):
                        dve.wait_ge(st_done, GB * g + j + 1)
                        op = v.bn_aggr(mv[i][:, j], st[i][:, j])
                    op.then_inc(mv_done, 1)
                    if g:
                        norm(g - 1)
                norm(G - 1)

            @block.gpsimd
            def _(pool):
                nc.gpsimd.memset(mh[:], -0.5).then_inc(c_in, 16)
                pool.wait_ge(c_in, 48)
                rr = lambda ap: ap[:].unsqueeze(1).to_broadcast([128, GB, D])
                for g in range(G):
                    i = g % 2
                    wait_apart(pool, mv_done, g + 1, passed)
                    nc.gpsimd.tensor_scalar(ve[i][:], mv[i][:, :, 1], EPS, None, ALU.add).then_inc(ve_done, 1)
                    wait_apart(pool, ve_done, g + 1, passed)
                    nc.gpsimd.tensor_tensor(rs[i][:], ve[i][:], mh[:], ALU.pow).then_inc(rs_done, 1)
                    wait_apart(pool, z_done, g + 1, passed)
                    nc.gpsimd.tensor_tensor(zg[i][:], zt[i][:], rr(g_rows), ALU.mult).then_inc(zg_done, 1)
                    wait_apart(pool, zg_done, g + 1, passed)
                    if g >= 2:
                        pool.wait_ge(stored[i], 16 * (g // 2))
                    nc.gpsimd.tensor_tensor(outt[i][:], zg[i][:], rr(b_rows), ALU.add).then_inc(o_done, 1)


def decoder_layer(nc, t, out):
    with ExitStack() as ctx:
        banks = [ctx.enter_context(nc.psum_tensor(f"bank{i}", [128, 512], fp32)) for i in range(8)]
        x2_all = ctx.enter_context(nc.sbuf_tensor("x2_all", [128, NTILE, D], fp32))
        weights = ctx.enter_context(nc.sbuf_tensor("weights", [128, TOPK, NTILE], fp32))
        tables = [ctx.enter_context(nc.sbuf_tensor(n, [1, BLOCKS], mybir.dt.int32)) for n in ("block_expert", "block_row")]
        rows_dram = nc.dram_tensor("rows_dram", (NULL_ROW + SPARE * BLK, ROW), fp32, kind="Internal").ap()
        with ExitStack() as part:
            attention(nc, part, t, x2_all, banks)
        with ExitStack() as moe:
            sb = lambda n, s: moe.enter_context(nc.sbuf_tensor(n, s, fp32))
            shared = (sb("w2_all", [128, E_, FC, D]), sb("b1_all", [128, E_, FC]), sb("b2_all", [128, E_, D]),
                      sb("ident_moe", [128, 128]), moe.enter_context(nc.semaphore("moe_in")))
            with ExitStack() as part:
                routing(nc, part, t, x2_all, weights, tables, rows_dram, banks[0:4], shared)
            with ExitStack() as part:
                experts(nc, part, t, x2_all, weights, tables, rows_dram, out, (banks[0:2], banks[2:6], banks[6:8]), shared)


def kernel(**inputs):
    import numpy as _np
    import concourse.bacc as _bacc
    from concourse import mybir as _mybir
    from concourse.bass_utils import run_bass_kernel_spmd as _run

    nc = _bacc.Bacc("TRN2", target_bir_lowering=False, num_devices=1)
    arrays, t = {}, {}
    for name, a in inputs.items():
        a = _np.ascontiguousarray(a)
        arrays[f"in_{name}"] = a
        t[name] = nc.dram_tensor(f"in_{name}", a.shape, _mybir.dt.from_np(a.dtype), kind="ExternalInput").ap()
    out = nc.dram_tensor("out", (B, SQ, D), _mybir.dt.float32, kind="ExternalOutput").ap()
    decoder_layer(nc, t, out)
    r = _run(nc, [arrays], core_ids=[0])
    return r.results[0]["out"]
```

```python
import concourse.bass as bass
from concourse import mybir
from contextlib import ExitStack

fp32 = mybir.dt.float32
bf16 = mybir.dt.bfloat16
ALU = mybir.AluOpType
ACT = mybir.ActivationFunctionType
AX = mybir.AxisListType

B, SQ, SK, D, H = 32, 128, 120, 128, 16
HD = D // H
GB = 4
G = B // GB
HB = GB // 2
NT = GB * SQ
NU = H // 4
NP = H // 2
SLOTS = 6
ROWS = 2 * SLOTS * HD
SHIFT = 3
EPS = 1e-5
SCORE_SCALE = 1.0 / float(HD) ** 0.5
MASKED = -1e30
SELF, CROSS = 0, 1
KEYS = (SQ, SK)


E_, FF, TOPK = 8, 512, 2
FC = FF // 128
TOK = B * SQ
NTILE = TOK // 128
BLK = 256
RS = TOK + BLK
NULL_ROW = E_ * RS
ROW = D + 1
BLOCKS = TOPK * TOK // BLK + E_ - 1
SPARE = BLOCKS - TOPK * TOK // BLK
TRASH = TOPK * TOK
PADS = E_ + SPARE
EARLY_SCATTERED = 14
IDLE_UNITS = (0, 1, 7, 8, 9, 10)
EARLY_TILES = (G - 2) * GB


def before(kind, g):
    return (CROSS, g - 2) if kind == SELF else (SELF, g + 1)


def behind(kind, g):
    return (CROSS, g - 1) if kind == SELF else (SELF, g + 2)


def exists(g):
    return not isinstance(g, int) or 0 <= g < G


def last_before(kind, g):
    for _ in range(4):
        kind, g = before(kind, g)
        if exists(g):
            return kind, g
    return None


def two_batches_ago(kind, g, b):
    if b >= 2:
        return kind, g, b - 2
    p = last_before(kind, g)
    return None if p is None else (*p, b + 2)


def wait(engine, sem, value):
    if not isinstance(value, int) or value > 0:
        engine.wait_ge(sem, value)


def wait_apart(engine, sem, value, passed):
    if isinstance(value, int):
        return wait(engine, sem, value)
    engine.wait_ge(sem, value)
    engine.sem_inc(passed, 1)


class Router:

    def __init__(self, nc, sb, slot, sem, name, first, last, x2_all, weights, tables, rows_dram, counts_before, stage,
                 turn_bank, logit_cols, within_cols, total_cols, after=None):
        self.nc, self.first, self.tiles, self.groups = nc, first, last - first, (last - first) // GB
        self.x2, self.weights, self.tables, self.rows_dram = x2_all, weights, tables, rows_dram
        self.counts_before, self.stage, self.turn_bank = counts_before, stage, turn_bank
        self.logit_cols, self.within_cols, self.total_cols = logit_cols, within_cols, total_cols
        n = self.tiles
        self.x2_t = [sb(f"{name}_x2_t{i}", [D, NT]) for i in range(2)]
        self.w8 = {w: sb(f"{name}_{w}", [128, n, E_]) for w in (
            "logit", "shifted_logit", "expo", "prob", "equal", "sel", "one_a", "prob_b", "one_b", "within", "pos", "pick_b")}
        self.w1 = {w: sb(f"{name}_{w}", [128, n]) for w in (
            "top", "total", "inv", "best", "first", "best_b", "first_b", "gap", "egap", "den")}
        self.chosen = sb(f"{name}_chosen", [128, n, E_], bf16)
        self.ahead = [sb(f"{name}_ahead{i}", [128, n, E_]) for i in range(2)]
        self.slot_f = sb(f"{name}_slot_f", [128, TOPK, n])
        self.slot = slot
        self.sems = after.sems if after else {w: sem(f"route_{w}") for w in self.ENDS}
        self.base = dict.fromkeys(self.ENDS, 0)
        if after:
            for w, end in after.ENDS.items():
                self.base[w] = after.links if w == "step_done" else end * (after.groups if w in self.PER_GROUP else 1)
        self.links = 0

    ENDS = {"step_done": 0, "turned": 1, "copied": 1, "logits_done": 1, "shift_done": 1, "exped": 1, "chosen_done": 1, "gap_done": 1,
            "gap_exped": 1, "counted": 1, "slot_done": 1, "staged": TOPK, "ids_done": TOPK, "scattered": 16 * TOPK * GB, "counts_read": 1}
    PER_GROUP = ("turned", "copied", "logits_done", "staged", "scattered")

    def await_(self, engine, name, value):
        wait(engine, self.sems[name], self.base[name] + value)

    def turn(self, q):
        pe, nc = self.nc.tensor, self.nc
        self.await_(pe, "copied", q if self.turn_bank[0] is self.turn_bank[1] else q - 1)
        for j in range(GB):
            mm = pe.transpose(self.turn_bank[q % 2][:, j * 128:(j + 1) * 128], self.x2[:, self.first + GB * q + j, :], self.tables["ident"][:])
        mm.then_inc(self.sems["turned"], 1)

    def logits(self, q):
        pe = self.nc.tensor
        self.await_(pe, "copied", q + 1)
        for j in range(GB):
            at = (GB * q + j) * E_
            mm = pe.matmul(self.logit_cols[:, at:at + E_], self.x2_t[q % 2][:, j * 128:(j + 1) * 128], self.tables["rw"][:], start=True, stop=True)
        mm.then_inc(self.sems["logits_done"], 1)

    def counts(self):
        pe = self.nc.tensor
        self.await_(pe, "chosen_done", 1)
        picks = self.chosen[:].rearrange("p j e -> p (j e)")
        pe.matmul(self.total_cols, self.tables["ones_b"][:], picks, start=True, stop=True)
        pe.matmul(self.within_cols, self.tables["earlier"][:], picks, start=True, stop=True).then_inc(self.sems["counted"], 1)

    def copy_turned(self, q):
        act = self.nc.scalar
        self.await_(act, "turned", q + 1)
        self.await_(act, "logits_done", q - 1)
        act.activation(self.x2_t[q % 2][:], self.turn_bank[q % 2][:], ACT.Copy).then_inc(self.sems["copied"], 1)

    def exp_logits(self):
        act = self.nc.scalar
        self.await_(act, "shift_done", 1)
        act.activation(self.w8["expo"][:], self.w8["shifted_logit"][:], ACT.Exp).then_inc(self.sems["exped"], 1)

    def exp_gap(self):
        act = self.nc.scalar
        self.await_(act, "gap_done", 1)
        act.activation(self.w1["egap"][:], self.w1["gap"][:], ACT.Exp).then_inc(self.sems["gap_exped"], 1)

    def copy_rows(self, q, k):
        at = slice(GB * q, GB * (q + 1))
        self.nc.scalar.activation(self.stage[k][:, at, 0:D], self.x2[:, self.first + GB * q:self.first + GB * (q + 1), :],
                                  ACT.Copy).then_inc(self.sems["staged"], 1)

    def link(self, op):
        self.links += 1
        op.then_inc(self.sems["step_done"], 1)
        self.await_(self.nc.vector, "step_done", self.links)

    def rep(self, ap):
        return ap.unsqueeze(2).to_broadcast([128, self.tiles, E_])

    def rows(self, ap):
        return ap.unsqueeze(1).to_broadcast([128, self.tiles, E_])

    def shift_logits(self):
        v, w8, w1, link = self.nc.vector, self.w8, self.w1, self.link
        self.await_(v, "logits_done", self.groups)
        link(v.tensor_tensor(w8["logit"][:], self.logit_cols.rearrange("p (j e) -> p j e", e=E_), self.rows(self.tables["rb_rows"][:]), ALU.add))
        link(v.tensor_reduce(w1["top"][:], w8["logit"][:], AX.X, ALU.max))
        v.tensor_tensor(w8["shifted_logit"][:], w8["logit"][:], self.rep(w1["top"][:]), ALU.subtract).then_inc(self.sems["shift_done"], 1)

    def choose_best(self):
        v, w8, w1, link, rep = self.nc.vector, self.w8, self.w1, self.link, self.rep
        self.await_(v, "exped", 1)
        link(v.tensor_reduce(w1["total"][:], w8["expo"][:], AX.X, ALU.add))
        link(v.reciprocal(w1["inv"][:], w1["total"][:]))
        link(v.tensor_tensor(w8["prob"][:], w8["expo"][:], rep(w1["inv"][:]), ALU.mult))
        link(v.tensor_reduce(w1["best"][:], w8["prob"][:], AX.X, ALU.max))
        link(v.tensor_tensor(w8["equal"][:], w8["prob"][:], rep(w1["best"][:]), ALU.is_equal))
        link(v.tensor_tensor(w8["sel"][:], w8["equal"][:], self.rows(self.tables["first_weight"][:]), ALU.mult))
        link(v.tensor_reduce(w1["first"][:], w8["sel"][:], AX.X, ALU.max))
        link(v.tensor_tensor(w8["one_a"][:], w8["sel"][:], rep(w1["first"][:]), ALU.is_equal))

    def choose_second(self):
        v, w8, w1, link, rep = self.nc.vector, self.w8, self.w1, self.link, self.rep
        link(v.scalar_tensor_tensor(w8["prob_b"][:], w8["one_a"][:], -2.0, w8["prob"][:], ALU.mult, ALU.add))
        link(v.tensor_reduce(w1["best_b"][:], w8["prob_b"][:], AX.X, ALU.max))
        link(v.tensor_tensor(w8["equal"][:], w8["prob_b"][:], rep(w1["best_b"][:]), ALU.is_equal))
        link(v.tensor_tensor(w8["sel"][:], w8["equal"][:], self.rows(self.tables["first_weight"][:]), ALU.mult))
        link(v.tensor_reduce(w1["first_b"][:], w8["sel"][:], AX.X, ALU.max))
        link(v.tensor_tensor(w8["one_b"][:], w8["sel"][:], rep(w1["first_b"][:]), ALU.is_equal))
        v.tensor_tensor(self.chosen[:], w8["one_a"][:], w8["one_b"][:], ALU.add).then_inc(self.sems["chosen_done"], 1)
        v.tensor_tensor(w1["gap"][:], w1["best_b"][:], w1["best"][:], ALU.subtract).then_inc(self.sems["gap_done"], 1)

    def places(self, counts):
        v, w8, link, n, ahead = self.nc.vector, self.w8, self.link, self.tiles, self.ahead
        self.await_(v, "counted", 1)
        totals = self.total_cols.rearrange("p (j e) -> p j e", e=E_)
        if self.counts_before is None:
            v.memset(ahead[0][:, 0], 0.0)
        else:
            v.tensor_copy(ahead[0][:, 0], self.counts_before[:])
        v.tensor_copy(w8["within"][:], self.within_cols.rearrange("p (j e) -> p j e", e=E_))
        link(v.tensor_copy(ahead[0][:, 1:n], totals[:, 0:n - 1]))
        span, now = 1, 0
        while span < n:
            v.tensor_copy(ahead[1 - now][:, 0:span], ahead[now][:, 0:span])
            link(v.tensor_tensor(ahead[1 - now][:, span:n], ahead[now][:, span:n], ahead[now][:, 0:n - span], ALU.add))
            span, now = 2 * span, 1 - now
        v.tensor_tensor(counts[:], ahead[now][:, n - 1], totals[:, n - 1], ALU.add).then_inc(self.sems["counts_read"], 1)
        link(v.tensor_tensor(w8["pos"][:], w8["within"][:], ahead[now][:], ALU.add))
        link(v.tensor_tensor(w8["within"][:], w8["pos"][:], self.rows(self.tables["region"][:]), ALU.add))
        v.tensor_tensor(w8["pos"][:], w8["within"][:], w8["one_a"][:], ALU.mult)
        link(v.tensor_tensor(w8["pick_b"][:], w8["within"][:], w8["one_b"][:], ALU.mult))
        v.tensor_reduce(self.slot_f[:, 0], w8["pos"][:], AX.X, ALU.add)
        link(v.tensor_reduce(self.slot_f[:, 1], w8["pick_b"][:], AX.X, ALU.add))
        v.tensor_copy(self.slot[:], self.slot_f[:]).then_inc(self.sems["slot_done"], 1)

    def weigh(self):
        v, w1, at = self.nc.vector, self.w1, slice(self.first, self.first + self.tiles)
        self.await_(v, "gap_exped", 1)
        self.link(v.tensor_scalar(w1["den"][:], w1["egap"][:], 1.0, None, ALU.add))
        self.link(v.reciprocal(self.weights[:, 0, at], w1["den"][:]))
        v.tensor_tensor(self.weights[:, 1, at], w1["egap"][:], self.weights[:, 0, at], ALU.mult)

    def row_ids(self):
        for k in range(TOPK):
            self.nc.gpsimd.iota(self.stage[k][:, :, D:ROW].bitcast(mybir.dt.int32), [[128, self.tiles], [0, 1]],
                                base=k * TOK + 128 * self.first, channel_multiplier=1).then_inc(self.sems["ids_done"], 1)

    def scatter(self, tiles):
        pool = self.nc.gpsimd
        self.await_(pool, "ids_done", TOPK)
        self.await_(pool, "staged", TOPK * self.groups)
        self.await_(pool, "slot_done", 1)
        for j in tiles:
            for k in range(TOPK):
                pool.indirect_dma_start(self.rows_dram, bass.IndirectOffsetOnAxis(ap=self.slot[:, k, j:j + 1], axis=0),
                                        self.stage[k][:, j, :], None).then_inc(self.sems["scattered"], 16)


def attention(nc, ctx, t, x2_all, banks, weights, tables, rows_dram, counts_early, q_diag_self, second_rows, early_slot, keep_sem):
    sb = lambda n, s, d=fp32: ctx.enter_context(nc.sbuf_tensor(n, s, d))
    both = lambda n, s, d=fp32: [sb(f"{n}_self", s, d), sb(f"{n}_cross", s, d)]
    sem = lambda n: ctx.enter_context(nc.semaphore(n))
    sems = lambda n: [sem(f"{n}_self"), sem(f"{n}_cross")]

    wq, wk, wv, wo = (both(n, [D, D]) for n in ("wq", "wk", "wv", "wo"))
    bq, bk = both("bq", [D, 1]), both("bk", [D, 1])
    bv_rows = both("bv_rows", [128, D])
    bo_rows = both("bo_rows", [128, D])
    ln_g_rows, ln_b_rows = both("ln_g_rows", [128, D]), both("ln_b_rows", [128, D])
    res_rows = sb("res_rows", [128, D])
    ln_g_col, ln_b_col = sb("ln_g_col", [D, 1]), sb("ln_b_col", [D, 1])
    ident = tables["ident"]
    ident_b = sb("ident_b", [128, 128], bf16)
    mask = sb("mask", [128, 4, SQ], bf16)
    head_ones = sb("head_ones", [128, 160])
    minus_half = sb("minus_half", [128, GB])
    xin = [sb("xin_self", [SQ, GB, D]), sb("xin_cross", [SK, GB, D])]
    src_t = [sb("src_t_self", [D, GB * SQ]), sb("src_t_cross", [D, GB * SK])]
    x1_t = sb("x1_t", [D, NT])
    q_res, k_res = sb("q_res", [D, NT]), sb("k_res", [D, NT])
    q_parts, k_parts = both("q_parts", [D, 3, NT], bf16), both("k_parts", [D, 3, NT], bf16)
    q_diag = [q_diag_self, sb("q_diag_cross", [128, NP, 2, NT], bf16)]
    k_pack = both("k_pack", [128, NP, NT], bf16)
    v_wide = both("v_wide", [128, GB, 4, 160])
    row_max = both("row_max", [SQ, GB, H])
    max_rest = sb("max_rest", [SQ, HB, H])
    max_parts = both("max_parts", [SQ, GB, 2, SHIFT, NP], bf16)
    max_t = both("max_t", [SHIFT * H, NT], bf16)
    probs = sb("probs", [128, 2, H, SQ])
    recip = sb("recip", [128, 2, SQ])
    heads_t = sb("heads_t", [128, 2, SQ])
    resid = both("resid", [SQ, GB, D])
    summed = both("summed", [SQ, GB, D])
    stats = both("stats", [SQ, GB, 6])
    mean_var = both("mean_var", [SQ, GB, 2])
    var_eps = both("var_eps", [SQ, GB])
    rstd = both("rstd", [SQ, GB])
    z = both("z", [SQ, GB, D])
    zg = both("zg", [SQ, GB, D])

    t_bank, n_bank, o_bank, (m0, m1) = banks[0:2], banks[2:4], banks[4:6], banks[6:8]
    VALUES, SUMS, ROWS_OUT = slice(0, 128), slice(128, 256), slice(256, 384)

    q_dram = [nc.dram_tensor(f"q_dram{k}", (D, SLOTS, NT), bf16, kind="Internal").ap() for k in (SELF, CROSS)]
    k_dram = [nc.dram_tensor(f"k_dram{k}", (D, SLOTS, GB * KEYS[k]), bf16, kind="Internal").ap() for k in (SELF, CROSS)]

    passed = sem("passed")
    idle = q_diag[SELF][:].rearrange("p a c t -> p (a c t)").bitcast(fp32)[:, 0:EARLY_TILES * ROW]
    router = Router(nc, sb, early_slot, keep_sem, "early", 0, EARLY_TILES, x2_all, weights, tables, rows_dram, None,
                    [idle.rearrange("p (j r) -> p j r", r=ROW), second_rows[:]],
                    [m0, m0], m1[:, 256:256 + EARLY_TILES * E_], m0[:, 0:EARLY_TILES * E_], m0[:, 256:256 + EARLY_TILES * E_])
    EARLY = EARLY_TILES // GB

    def unit_of(kind, g, b, u, *stage):
        return 4 * b + u if isinstance(g, int) and (kind, g) == stage else None

    first_in, early_in, late_in = sem("first_in"), sem("early_in"), sem("late_in")
    consts = sem("consts")
    const_step = sem("const_step")
    ident_zero, ident_done, earlier_set = sem("ident_zero"), sem("ident_done"), sem("earlier_set")
    x_in = sems("x_in")
    src_done, src_copied = sems("src_done"), sems("src_copied")
    k_done, q_done, v_done = sems("k_done"), sems("q_done"), sems("v_done")
    k_first, q_first = sems("k_first"), sems("q_first")
    k_rest, q_rest = sems("k_rest"), sems("q_rest")
    k_split, q_split = sems("k_split"), sems("q_split")
    k_last, q_last = sems("k_last"), sems("q_last")
    k_stored, q_stored = sems("k_stored"), sems("q_stored")
    packed = [[sem(f"packed_{k}_{h}") for h in range(2)] for k in ("self", "cross")]
    v_copied = sems("v_copied")
    nat_done, max_done = sems("nat_done"), sems("max_done")
    m_part = sems("m_part")
    m_split = sems("m_split")
    m_turned, m_copied = sems("m_turned"), sems("m_copied")
    shifted = [[sem(f"shifted_{k}_{h}") for h in range(2)] for k in ("self", "cross")]
    t_done, exp_done = sems("t_done"), sems("exp_done")
    select_done = sem("select_done")
    pvs_done = sems("pvs_done")
    recip_done, heads_done = sems("recip_done"), sems("heads_done")
    y_done = sems("y_done")
    sum_done, stats_done, aggr_done = sems("sum_done"), sems("stats_done"), sems("aggr_done")
    eps_done, rstd_done, z_done = sems("eps_done"), sems("rstd_done"), sems("z_done")
    z_turned, x1_copied = sem("z_turned"), sem("x1_copied")
    zg_done, resid_done = sems("zg_done"), sems("resid_done")
    x2_done = sem("x2_done")

    block = ctx.enter_context(nc.Block())

    def stages(engine, stage):
        stage(SELF, -1)
        engine.wait_ge(early_in, EARLY_LOADS)
        stage(CROSS, -2)
        stage(SELF, 0)
        engine.wait_ge(late_in, LATE_LOADS)
        stage(CROSS, -1)
        stage(SELF, 1)
        stage(CROSS, 0)
        with engine.Fori(2, G - 1) as it:
            stage(SELF, it)
            stage(CROSS, it - 1)
        for it in (G - 1, G):
            stage(SELF, it)
            stage(CROSS, it - 1)
        stage(SELF, G + 1)

    first_loads, early_loads, late_loads = [], [], []
    for w, tile in (("wk", wk), ("wq", wq)):
        first_loads.append((tile[SELF][:], t[f"L0_xattn_sa_{w}"]))
    for w, tile in (("bk", bk), ("bq", bq)):
        first_loads.append((tile[SELF][:], t[f"L0_xattn_sa_{w}"].rearrange("(p a) -> p a", a=1)))
    for k, p in ((SELF, "sa"), (CROSS, "ca")):
        into = early_loads if k == SELF else late_loads
        for w, tile in (("wv", wv), ("wo", wo)):
            into.append((tile[k][:], t[f"L0_xattn_{p}_{w}"]))
        for w, tile in (("bv", bv_rows), ("bo", bo_rows)):
            into.append((tile[k][:], t[f"L0_xattn_{p}_{w}"].partition_broadcast(128)))
        late_loads.append((ln_g_rows[k][:], t[f"L0_xattn_ln{k + 1}_g"].partition_broadcast(128)))
        late_loads.append((ln_b_rows[k][:], t[f"L0_xattn_ln{k + 1}_b"].partition_broadcast(128)))
    for w, tile in (("wk", wk), ("wq", wq)):
        late_loads.append((tile[CROSS][:], t[f"L0_xattn_ca_{w}"]))
    for w, tile in (("bq", bq), ("bk", bk)):
        late_loads.append((tile[CROSS][:], t[f"L0_xattn_ca_{w}"].rearrange("(p a) -> p a", a=1)))
    late_loads.append((tables["rw"][:], t["L0_xattn_router_w"]))
    late_loads.append((tables["rb_rows"][:], t["L0_xattn_router_b"].partition_broadcast(128)))
    late_loads.append((ln_g_col[:], t["L0_xattn_ln1_g"].rearrange("(p a) -> p a", a=1)))
    late_loads.append((ln_b_col[:], t["L0_xattn_ln1_b"].rearrange("(p a) -> p a", a=1)))
    FIRST_LOADS, EARLY_LOADS, LATE_LOADS = (16 * len(x) for x in (first_loads, early_loads, late_loads))
    CONSTS = 13

    @block.sync
    def _(sp):
        sp.dma_start(xin[SELF][:], t["x"].rearrange("(g b) s d -> g s b d", b=GB)[0]).then_inc(x_in[SELF], 16)
        for dst, src in first_loads:
            sp.dma_start(dst, src).then_inc(first_in, 16)

        def shift_rows(kind, g, half):
            cols = slice(half * HB * SQ, (half + 1) * HB * SQ)
            wait(sp, m_copied[kind], 2 * g + half + 1)
            for c in range(2):
                r0 = ROWS + SHIFT * c
                sp.dma_start(q_diag[kind][r0:r0 + SHIFT, :, c, cols],
                             max_t[kind][SHIFT * NP * c:SHIFT * NP * (c + 1), cols]).then_inc(shifted[kind][half], 16)

        def stage(kind, g):
            nk, ng = behind(kind, g)
            if isinstance(g, int) and (kind, g) == (SELF, -1):
                for dst, src in early_loads:
                    sp.dma_start(dst, src).then_inc(early_in, 16)
            elif exists(g + 1):
                load_rows(kind, g + 1)
            if exists(g):
                shift_rows(kind, g, 1)
            if exists(g + 1):
                store(kind, g + 1, KEY, 0, k_first, slice(0, 3))
                store(kind, g + 1, QUERY, 0, q_first, slice(0, 4, 3))
                store(kind, g + 1, QUERY, 0, q_first, slice(5, 6))
                store(kind, g + 1, KEY, 1, k_split, slice(3, 5))
            if exists(ng):
                shift_rows(nk, ng, 0)
            if exists(g + 1):
                store(kind, g + 1, KEY, 2, k_last, slice(5, 6))
                store(kind, g + 1, QUERY, 1, q_split, slice(1, 5, 3))
                store(kind, g + 1, QUERY, 2, q_last, slice(2, 3))
                load_packed(kind, g + 1)
            if isinstance(g, int) and (kind, g) == (SELF, -1):
                for dst, src in late_loads:
                    sp.dma_start(dst, src).then_inc(late_in, 16)

        def load_rows(kind, n):
            if kind == SELF:
                wait(sp, resid_done[SELF], n)
                src = t["x"].rearrange("(g b) s d -> g s b d", b=GB)[n]
            else:
                wait(sp, src_done[CROSS], n)
                src = t["ctx_1024"].rearrange("(g b) s d -> g s b d", b=GB)[n]
            sp.dma_start(xin[kind][:], src).then_inc(x_in[kind], 16)

        KEY, QUERY = (k_parts, k_dram, k_stored), (q_parts, q_dram, q_stored)

        def store(kind, n, what, part, ready, slots):
            parts, dram, stored = what
            wait(sp, ready[kind], n + 1)
            cols = GB * KEYS[kind] if what is KEY else NT
            copies = len(range(SLOTS)[slots])
            sp.dma_start(dram[kind][:, slots, :],
                         parts[kind][:, part, 0:cols].unsqueeze(1).to_broadcast([D, copies, cols])).then_inc(stored[kind], 16)

        def load_packed(kind, n):
            g = n - 1
            if isinstance(n, int) and n == 0:
                sp.wait_ge(consts, CONSTS)
            for half in range(2):
                wait_apart(sp, t_done[kind], 16 * g + 8 * (half + 1), passed)
                qc = slice(half * HB * SQ, (half + 1) * HB * SQ)
                kc = slice(half * HB * KEYS[kind], (half + 1) * HB * KEYS[kind])
                wait(sp, k_stored[kind], 16 * 3 * (n + 1))
                sp.dma_start(k_pack[kind][0:ROWS, :, kc],
                             k_dram[kind].rearrange("(a r) s t -> (r s) a t", a=NP)[:, :, kc]).then_inc(packed[kind][half], 16)
                wait(sp, q_stored[kind], 16 * 4 * (n + 1))
                for c in range(2):
                    sp.dma_start(q_diag[kind][ROWS // 2 * c:ROWS // 2 * (c + 1), :, c, qc],
                                 q_dram[kind].rearrange("(a c i) s t -> c (i s) a t", c=2, i=HD)[c, :, :, qc]).then_inc(packed[kind][half], 16)

        stages(sp, stage)
        for kind in (SELF, CROSS):
            sp.wait_ge(k_stored[kind], 16 * 3 * G)
            sp.wait_ge(q_stored[kind], 16 * 4 * G)

    @block.tensor
    def _(pe):
        pe.wait_ge(first_in, FIRST_LOADS)
        pe.wait_ge(ident_done, 1)

        def turn_shift(kind, g, half, clear):
            clear()
            wait_apart(pe, m_split[kind], 2 * g + half + 1, passed)
            for b in range(half * HB, (half + 1) * HB):
                out = m1[0:SHIFT * H, :].bitcast(bf16)[:, b * SQ:(b + 1) * SQ]
                last = nc.tensor.transpose(out, max_parts[kind][:, b].rearrange("p c r a -> p (c r a)"), ident_b[:])
            last.then_inc(m_turned[kind], 1)

        def stage(kind, g):
            nk, ng = behind(kind, g)
            pk, pg = before(kind, g)
            main = exists(g)

            def m1_clear(use):
                k_, g_, at = kind, g, use
                for _ in range(24):
                    at -= 1
                    if at < 0:
                        k_, g_ = before(k_, g_)
                        at = 3
                    if at == 0 and exists(g_):
                        return wait(pe, m_copied[k_], 2 * g_ + 2)
                    if at == 1 and k_ == CROSS and exists(before(k_, g_)[1]):
                        return wait(pe, x1_copied, before(k_, g_)[1] + 1)
                    if at == 2 and exists(g_ + 1):
                        wait(pe, k_first[k_], g_ + 2)
                        return wait(pe, k_rest[k_], g_ + 2)
                    if at == 3 and exists(behind(k_, g_)[1]):
                        k2, g2 = behind(k_, g_)
                        return wait(pe, m_copied[k2], 2 * g2 + 1)

            for b in range(GB):
                nat = (kind, g, GB - 1) if b == 0 else (nk, ng, b - 1)
                last = (kind, g, b - 1) if b >= 1 else (pk, pg, GB - 1)
                for u in range(NU):
                    if exists(nat[1]):
                        k_, g_, b_ = nat
                        if b_ % HB == 0 and u == 0:
                            wait(pe, packed[k_][b_ // HB], 16 * 3 * (g_ + 1))
                        if u >= 2:
                            wait(pe, max_done[k_], 16 * g_ + 4 * b_ + u - 1)
                        elif b_ >= 1:
                            wait(pe, max_done[k_], 16 * g_ + 4 * (b_ - 1) + u + 3)
                        else:
                            p = (kind, g) if exists(g) else last_before(kind, g)
                            if p is not None:
                                wait(pe, max_done[p[0]], 16 * p[1] + 12 + u + 3)
                        bank, keys = n_bank[u % 2], KEYS[k_]
                        if k_ == SELF:
                            nc.tensor.matmul(bank[:], ident_b[:], mask[:].rearrange("p h k -> p (h k)"), start=True, stop=False)
                        for i in range(4):
                            mm = nc.tensor.matmul(bank[:, i * keys:(i + 1) * keys],
                                                  q_diag[k_][0:ROWS, 2 * u + i // 2, i % 2, b_ * SQ:(b_ + 1) * SQ],
                                                  k_pack[k_][0:ROWS, 2 * u + i // 2, b_ * keys:(b_ + 1) * keys],
                                                  start=k_ == CROSS, stop=k_ == CROSS or i == 3)
                        mm.then_inc(nat_done[k_], 1)
                    if main:
                        if b % HB == 0 and u == 0:
                            wait(pe, shifted[kind][b // HB], 32 * (g + 1))
                        if u >= 2:
                            wait(pe, exp_done[kind], 16 * g + 4 * b + u - 1)
                        elif b >= 1:
                            wait(pe, exp_done[kind], 16 * g + 4 * (b - 1) + u + 3)
                        elif (p := last_before(kind, g)) is not None:
                            wait(pe, exp_done[p[0]], 16 * p[1] + 12 + u + 3)
                        for i in range(2):
                            a = 2 * u + i
                            mm = nc.tensor.matmul(
                                t_bank[u % 2][0:KEYS[kind], i * 256:(i + 1) * 256].rearrange("p (c q) -> p c q", c=2),
                                k_pack[kind][:, a, b * KEYS[kind]:(b + 1) * KEYS[kind]],
                                q_diag[kind][:, a, :, b * SQ:(b + 1) * SQ], start=True, stop=True)
                        mm.then_inc(t_done[kind], 1)
                    ago = (kind, g, b - 2) if b >= 2 else (pk, pg, b + 2)
                    if (b, u) == (1, 1) and exists(ng):
                        keys = KEYS[nk]
                        wait(pe, q_first[nk], ng + 1)
                        wait(pe, q_rest[nk], ng + 1)
                        if isinstance(g, int) and g == G:
                            router.await_(pe, "counts_read", 1)
                        for j in range(GB):
                            mm = nc.tensor.matmul(m0[0:keys, j * D:(j + 1) * D], src_t[nk][:, j * keys:(j + 1) * keys],
                                                  wv[nk][:], start=True, stop=True)
                        mm.then_inc(v_done[nk], 1)
                    if (b, u) == (1, 1) and main:
                        turn_shift(kind, g, 1, lambda: m1_clear(0))
                    if (b, u) == (3, 1) and exists(ng):
                        turn_shift(nk, ng, 0, lambda: m1_clear(3))
                    if u in (1, 2) and exists(last[1]):
                        k_, g_, b_ = last
                        keys = KEYS[k_]
                        if u == 1:
                            if k_ == SELF:
                                wait(pe, select_done, 16 * g_ + 4 * b_ + 4)
                            else:
                                wait(pe, exp_done[k_], 16 * g_ + 4 * b_ + 4)
                            if b_ == 0:
                                wait(pe, v_copied[k_], g_ + 1)
                            if (w := two_batches_ago(*last)) is not None:
                                wait(pe, sum_done[w[0]], 4 * w[1] + w[2] + 1)
                        for c in range(4):
                            for j in range(4):
                                lhs = (v_wide[k_][0:keys, b_, j, 32 * c:32 * c + 32] if u == 1
                                       else head_ones[0:keys, 32 * c:32 * c + 32])
                                mm = nc.tensor.matmul(o_bank[b_ % 2][32 * j:32 * j + 32, VALUES if u == 1 else SUMS], lhs,
                                                      probs[0:keys, b_ % 2, 4 * j + c], start=c == 0, stop=c == 3)
                        if u == 2:
                            mm.then_inc(pvs_done[k_], 1)
                    if u == 1 and exists(ago[1]):
                        k_, g_, b_ = ago
                        wait(pe, heads_done[k_], 4 * g_ + b_ + 1)
                        nc.tensor.matmul(o_bank[b_ % 2][:, ROWS_OUT], heads_t[:, b_ % 2],
                                         wo[k_][:], start=True, stop=True).then_inc(y_done[k_], 1)
                    if (b, u) == (1, 3) and exists(g + 1):
                        keys = KEYS[kind]
                        wait(pe, x_in[kind], 16 * (g + 2))
                        if exists(ng):
                            wait(pe, v_copied[nk], ng + 1)
                        for j in range(GB):
                            mm = nc.tensor.transpose(m0[:, j * keys:(j + 1) * keys], xin[kind][:, j, :], ident[0:keys, 0:keys])
                        mm.then_inc(src_done[kind], 1)
                    if (b, u) == (2, 1) and kind == CROSS and exists(pg):
                        wait(pe, z_done[SELF], pg + 1)
                        m1_clear(1)
                        for j in range(GB):
                            mm = nc.tensor.transpose(m1[:, j * SQ:(j + 1) * SQ], z[SELF][:, j, :], ident[:])
                        mm.then_inc(z_turned, 1)
                    if (b, u) == (2, 2) and exists(g + 1):
                        KT = GB * KEYS[kind]
                        wait(pe, src_copied[kind], g + 2)
                        m1_clear(2)
                        nc.tensor.matmul(m1[:, 0:KT], wk[kind][:], src_t[kind][:, 0:KT], start=True, stop=True).then_inc(k_done[kind], 1)
                    if (b, u) == (2, 3) and exists(g + 1):
                        if kind == CROSS:
                            wait(pe, x1_copied, g + 2)
                        nc.tensor.matmul(m0[:], wq[kind][:], (x1_t if kind == CROSS else src_t[SELF])[:], start=True,
                                         stop=True).then_inc(q_done[kind], 1)
                    if (i := unit_of(kind, g, b, u, SELF, G - 1)) is not None and i >= 6:
                        if i == 6:
                            pe.wait_ge(x2_done, EARLY - 1)
                            pe.wait_ge(v_copied[CROSS], G - 1)
                            pe.wait_ge(m_copied[SELF], 2 * G)
                        if i % 2 == 0:
                            router.turn(i // 2 - 3)
                        else:
                            if i == 13:
                                pe.wait_ge(m_copied[CROSS], 2 * (G - 2) + 1)
                            router.logits(i // 2 - 3)
                    if (i := unit_of(kind, g, b, u, CROSS, G - 2)) == 4:
                        pe.wait_ge(x2_done, EARLY)
                        router.turn(EARLY - 1)
                    if i == 6:
                        pe.wait_ge(m_copied[CROSS], 2 * (G - 1))
                        router.logits(EARLY - 1)
                    if i == 14:
                        pe.wait_ge(q_rest[CROSS], G)
                        router.counts()

        stages(pe, stage)

    @block.scalar
    def _(act):
        act.wait_ge(first_in, FIRST_LOADS)

        def copy_shift(kind, g, half):
            cols = slice(half * HB * SQ, (half + 1) * HB * SQ)
            wait(act, m_turned[kind], 2 * g + half + 1)
            nc.scalar.activation(max_t[kind][0:SHIFT * H, cols], m1[0:SHIFT * H, :].bitcast(bf16)[:, cols], ACT.Copy).then_inc(m_copied[kind], 1)

        def stage(kind, g):
            nk, ng = behind(kind, g)
            pk, pg = before(kind, g)
            keys = KEYS[kind]
            for b in range(GB):
                for u in range(NU):
                    if exists(g):
                        if u == 0 and (w := two_batches_ago(kind, g, b)) is not None:
                            wait(act, pvs_done[w[0]], 4 * w[1] + w[2] + 1)
                        wait(act, t_done[kind], 16 * g + 4 * b + u + 1)
                        nc.scalar.activation(probs[0:keys, b % 2, 4 * u:4 * u + 4].rearrange("p h q -> p (h q)"),
                                             t_bank[u % 2][0:keys, :], ACT.Exp, scale=SCORE_SCALE).then_inc(exp_done[kind], 1)
                    if (b, u) == (1, 1) and exists(g):
                        copy_shift(kind, g, 1)
                    if (b, u) == (3, 1) and exists(ng):
                        copy_shift(nk, ng, 0)
                    if (b, u) == (1, 3) and exists(g + 1):
                        wait(act, src_done[kind], g + 2)
                        nc.scalar.activation(src_t[kind][:], m0[:, 0:GB * keys], ACT.Copy).then_inc(src_copied[kind], 1)
                    if (b, u) == (2, 1) and kind == CROSS and exists(pg):
                        wait(act, z_turned, pg + 1)
                        nc.scalar.activation(x1_t[:], m1[:], ACT.Identity, bias=ln_b_col[:], scale=ln_g_col[:]).then_inc(x1_copied, 1)
                    if (b, u) == (2, 2) and exists(g + 1):
                        wait(act, k_done[kind], g + 2)
                        wait(act, k_stored[kind], 16 * 3 * (g + 1))
                        nc.scalar.activation(k_parts[kind][:, 0, 0:GB * keys], m1[:, 0:GB * keys], ACT.Identity,
                                             bias=bk[kind][:]).then_inc(k_first[kind], 1)
                    if (b, u) == (2, 3) and exists(g + 1):
                        wait(act, q_done[kind], g + 2)
                        wait(act, q_stored[kind], 16 * 4 * (g + 1))
                        nc.scalar.activation(q_parts[kind][:, 0, :], m0[:], ACT.Identity, bias=bq[kind][:]).then_inc(q_first[kind], 1)
                    if (b, u) == (3, 0) and exists(g + 1):
                        wait(act, k_rest[kind], g + 2)
                        nc.scalar.activation(k_parts[kind][:, 1, 0:GB * keys], k_res[:, 0:GB * keys], ACT.Copy).then_inc(k_split[kind], 1)
                    if (b, u) == (3, 1) and exists(g + 1):
                        wait(act, q_rest[kind], g + 2)
                        nc.scalar.activation(q_parts[kind][:, 1, :], q_res[:], ACT.Copy).then_inc(q_split[kind], 1)
                    if (i := unit_of(kind, g, b, u, SELF, G - 1)) is not None and i >= 6 and i % 2 == 0:
                        router.copy_turned(i // 2 - 3)
                    if (i := unit_of(kind, g, b, u, CROSS, G - 2)) is not None:
                        if i == 4:
                            router.copy_turned(EARLY - 1)
                        if i == 7:
                            router.exp_logits()
                        if i == 13:
                            router.exp_gap()
                        if 8 <= i < 8 + EARLY:
                            for k in range(TOPK):
                                router.copy_rows(i - 8, k)

        stages(act, stage)

    @block.vector
    def _(dve):
        nc.vector.memset(q_diag[SELF][:].rearrange("p a c t -> p (a c t)").bitcast(fp32), 0.0).then_inc(consts, 1)
        for kind in (SELF, CROSS):
            nc.vector.memset(k_pack[kind][96:128].rearrange("p a t -> p (a t)"), 1.0).then_inc(consts, 1)
        dve.wait_ge(first_in, FIRST_LOADS)

        def split_shift(kind, g, half):
            hb = slice(half * HB, (half + 1) * HB)
            top = row_max[kind][:, hb].rearrange("p b (a c) -> p b c a", c=2)
            rest = max_rest[:].rearrange("p b (a c) -> p b c a", c=2)
            parts = [max_parts[kind][:, hb, :, r] for r in range(SHIFT)]
            wait(dve, max_done[kind], 16 * g + 8 * (half + 1))
            nc.vector.tensor_copy(parts[0], top).then_inc(m_part[kind], 1)
            wait(dve, m_part[kind], 3 * (2 * g + half) + 1)
            nc.vector.tensor_tensor(rest, top, parts[0], ALU.subtract).then_inc(m_part[kind], 1)
            wait(dve, m_part[kind], 3 * (2 * g + half) + 2)
            nc.vector.tensor_copy(parts[1], rest).then_inc(m_part[kind], 1)
            wait(dve, m_part[kind], 3 * (2 * g + half) + 3)
            nc.vector.tensor_tensor(parts[2], rest, parts[1], ALU.subtract).then_inc(m_split[kind], 1)

        def stage(kind, g):
            nk, ng = behind(kind, g)
            pk, pg = before(kind, g)
            for b in range(GB):
                nat = (kind, g, GB - 1) if b == 0 else (nk, ng, b - 1)
                last = (kind, g, b - 1) if b >= 1 else (pk, pg, GB - 1)
                ago = (kind, g, b - 2) if b >= 2 else (pk, pg, b + 2)
                for u in range(NU):
                    if exists(nat[1]):
                        k_, g_, b_ = nat
                        keys = KEYS[k_]
                        wait(dve, nat_done[k_], 16 * g_ + 4 * b_ + u + 1)
                        nc.vector.tensor_reduce(row_max[k_][:, b_, 4 * u:4 * u + 4],
                                                n_bank[u % 2][:, 0:4 * keys].rearrange("p (h k) -> p h k", h=4),
                                                AX.X, ALU.max, negate=True).then_inc(max_done[k_], 1)
                    if u == 2 and exists(ago[1]):
                        k_, g_, b_ = ago
                        wait(dve, y_done[k_], 4 * g_ + b_ + 1)
                        if b_ == 0:
                            wait(dve, resid_done[k_], g_ + 1)
                        nc.vector.tensor_tensor(summed[k_][:, b_], o_bank[b_ % 2][:, ROWS_OUT],
                                                resid[k_][:, b_], ALU.add).then_inc(sum_done[k_], 1)
                    if u == 2 and exists(ago[1]):
                        k_, g_, b_ = ago
                        wait(dve, sum_done[k_], 4 * g_ + b_ + 1)
                        nc.vector.bn_stats(stats[k_][:, b_], summed[k_][:, b_]).then_inc(stats_done[k_], 1)
                        wait_apart(dve, stats_done[k_], 4 * g_ + b_ + 1, passed)
                        nc.vector.bn_aggr(mean_var[k_][:, b_], stats[k_][:, b_]).then_inc(aggr_done[k_], 1)
                    if (b, u) == (1, 1) and exists(ng):
                        keys = KEYS[nk]
                        wait(dve, v_done[nk], ng + 1)
                        for j in range(GB):
                            out = v_wide[nk][0:keys, j].rearrange("p j (c r) -> p j c r", r=40)[:, :, :, 0:HD]
                            op = nc.vector.tensor_tensor(out, m0[0:keys, j * D:(j + 1) * D].rearrange("p (j c i) -> p j c i", j=4, i=HD),
                                                         bv_rows[nk][0:keys].rearrange("p (j c i) -> p j c i", j=4, i=HD), ALU.add)
                        op.then_inc(v_copied[nk], 1)
                    if (b, u) == (0, 3) and exists(g):
                        split_shift(kind, g, 1)
                    if (b, u) == (2, 3) and exists(ng):
                        split_shift(nk, ng, 0)
                    if (b, u) == (2, 3) and exists(g + 1):
                        KT = GB * KEYS[kind]
                        wait(dve, k_first[kind], g + 2)
                        nc.vector.scalar_tensor_tensor(k_res[:, 0:KT], m1[:, 0:KT], bk[kind][:], k_parts[kind][:, 0, 0:KT], ALU.add,
                                                       ALU.subtract).then_inc(k_rest[kind], 1)
                    if u == 3 and exists(last[1]):
                        k_, g_, b_ = last
                        wait(dve, pvs_done[k_], 4 * g_ + b_ + 1)
                        nc.vector.reciprocal(recip[:, b_ % 2], o_bank[b_ % 2][:, SUMS]).then_inc(recip_done[k_], 1)
                        wait(dve, recip_done[k_], 4 * g_ + b_ + 1)
                        nc.vector.tensor_tensor(heads_t[:, b_ % 2], o_bank[b_ % 2][:, VALUES], recip[:, b_ % 2],
                                                ALU.mult).then_inc(heads_done[k_], 1)
                    if (b, u) == (2, 0) and exists(pg):
                        wait(dve, rstd_done[pk], pg + 1)
                        for j in range(GB):
                            op = nc.vector.tensor_scalar(z[pk][:, j], summed[pk][:, j], mean_var[pk][:, j, 0:1], rstd[pk][:, j:j + 1],
                                                         ALU.subtract, ALU.mult)
                        op.then_inc(z_done[pk], 1)
                    if (b, u) == (3, 0) and exists(g + 1):
                        wait(dve, q_first[kind], g + 2)
                        nc.vector.scalar_tensor_tensor(q_res[:], m0[:], bq[kind][:], q_parts[kind][:, 0, :], ALU.add,
                                                       ALU.subtract).then_inc(q_rest[kind], 1)
                    if (i := unit_of(kind, g, b, u, CROSS, G - 2)) is not None:
                        if i == 7:
                            router.shift_logits()
                        if i == 8:
                            router.choose_best()
                        if i == 12:
                            router.choose_second()
                    if unit_of(kind, g, b, u, SELF, G) == 0:
                        router.places(counts_early)
                        router.weigh()

        stages(dve, stage)

    @block.gpsimd
    def _(pool):
        nc.gpsimd.memset(ident[:], 0.0).then_inc(ident_zero, 1)
        pool.wait_ge(ident_zero, 1)
        nc.gpsimd.affine_select(out=ident[:], in_=ident[:], compare_op=ALU.not_equal, fill=1.0, base=0,
                                pattern=[[-1, 128]], channel_multiplier=1).then_inc(ident_done, 1)
        nc.gpsimd.memset(mask[:].rearrange("p h k -> p (h k)"), 0.0).then_inc(const_step, 1)
        nc.gpsimd.memset(head_ones[:], 0.0).then_inc(const_step, 1)
        nc.gpsimd.memset(minus_half[:], -0.5)
        for kind in (SELF, CROSS):
            nc.gpsimd.memset(v_wide[kind][:].rearrange("p b j c -> p (b j c)"), 0.0).then_inc(consts, 1)
        pool.wait_ge(const_step, 2)
        nc.gpsimd.affine_select(out=mask[:], in_=mask[:], compare_op=ALU.is_ge, fill=MASKED, base=0,
                                pattern=[[0, 4], [-1, SQ]], channel_multiplier=1).then_inc(consts, 1)
        nc.gpsimd.memset(head_ones[:].rearrange("p (c r) -> p c r", r=40)[:, :, 0:HD], 1.0).then_inc(consts, 1)
        pool.wait_ge(ident_done, 1)
        nc.gpsimd.tensor_copy(ident_b[:], ident[:]).then_inc(consts, 1)
        nc.gpsimd.memset(tables["earlier"][:], 1.0).then_inc(earlier_set, 1)
        nc.gpsimd.memset(tables["ones_b"][:], 1.0).then_inc(consts, 1)
        pool.wait_ge(earlier_set, 1)
        nc.gpsimd.affine_select(out=tables["earlier"][:], in_=tables["earlier"][:], compare_op=ALU.is_gt, fill=0.0, base=0,
                                pattern=[[1, 128]], channel_multiplier=-1).then_inc(consts, 1)
        nc.gpsimd.iota(tables["first_weight"][:], [[-1, E_]], base=E_, channel_multiplier=0,
                       allow_small_or_imprecise_dtypes=True).then_inc(consts, 1)
        nc.gpsimd.iota(tables["region"][:], [[RS, E_]], base=0, channel_multiplier=0,
                       allow_small_or_imprecise_dtypes=True).then_inc(consts, 1)
        nc.gpsimd.memset(q_diag[CROSS][:].rearrange("p a c t -> p (a c t)").bitcast(fp32), 0.0).then_inc(consts, 1)

        def rows(tile):
            return tile[:].unsqueeze(1).to_broadcast([128, GB, D])

        def second_result(g):
            wait_apart(pool, z_done[CROSS], g + 1, passed)
            wait_apart(pool, x2_done, g, passed)
            nc.gpsimd.tensor_tensor(zg[CROSS][:], z[CROSS][:], rows(ln_g_rows[CROSS]), ALU.mult).then_inc(zg_done[CROSS], 1)
            wait_apart(pool, zg_done[CROSS], g + 1, passed)
            nc.gpsimd.tensor_tensor(x2_all[:, bass.ds(g * GB, GB), :], zg[CROSS][:], rows(ln_b_rows[CROSS]), ALU.add).then_inc(x2_done, 1)

        def stage(kind, g):
            nk, ng = behind(kind, g)
            pk, pg = before(kind, g)
            for b in range(GB):
                for u in range(NU):
                    if kind == SELF and exists(g):
                        wait_apart(pool, exp_done[SELF], 16 * g + 4 * b + u + 1, passed)
                        p = probs[:, b % 2, 4 * u:4 * u + 4]
                        nc.gpsimd.affine_select(out=p, in_=p, compare_op=ALU.is_ge, fill=0.0, base=0,
                                                pattern=[[0, 4], [1, SQ]], channel_multiplier=-1).then_inc(select_done, 1)
                    if (b, u) == (0, 0) and kind == SELF and exists(g):
                        wait_apart(pool, sum_done[SELF], 4 * g, passed)
                        wait_apart(pool, x_in[SELF], 16 * (g + 1), passed)
                        nc.gpsimd.tensor_tensor(resid[SELF][:], xin[SELF][:], rows(bo_rows[SELF]), ALU.add).then_inc(resid_done[SELF], 1)
                    if (b, u) == (1, 2) and exists(pg):
                        wait_apart(pool, aggr_done[pk], 4 * (pg + 1), passed)
                        nc.gpsimd.tensor_scalar(var_eps[pk][:], mean_var[pk][:, :, 1], EPS, None, ALU.add).then_inc(eps_done[pk], 1)
                        wait_apart(pool, eps_done[pk], pg + 1, passed)
                        nc.gpsimd.tensor_tensor(rstd[pk][:], var_eps[pk][:], minus_half[:], ALU.pow).then_inc(rstd_done[pk], 1)
                    if (b, u) == (0, 0) and isinstance(g, int) and (kind, g) == (CROSS, -1):
                        nc.gpsimd.tensor_tensor(res_rows[:], ln_b_rows[SELF][:], bo_rows[CROSS][:], ALU.add).then_inc(const_step, 1)
                        pool.wait_ge(const_step, 3)
                    if (b, u) == (0, 0) and kind == CROSS and exists(g):
                        wait_apart(pool, z_done[SELF], g + 1, passed)
                        wait_apart(pool, sum_done[CROSS], 4 * g, passed)
                        wait_apart(pool, resid_done[CROSS], g, passed)
                        nc.gpsimd.tensor_tensor(zg[SELF][:], z[SELF][:], rows(ln_g_rows[SELF]), ALU.mult).then_inc(zg_done[SELF], 1)
                        wait_apart(pool, zg_done[SELF], g + 1, passed)
                        nc.gpsimd.tensor_tensor(resid[CROSS][:], zg[SELF][:], rows(res_rows), ALU.add).then_inc(resid_done[CROSS], 1)
                    if kind == CROSS and (b, u) == (0, 1) and exists(g - 1):
                        second_result(g - 1)
                    if kind == SELF and (b, u) == (2, 1) and isinstance(pg, int) and pg == G - 1:
                        second_result(pg)
                    for at, parts, rest, split_done, last_done, cols in (
                            ((3, 0), k_parts, k_res, k_split, k_last, GB * KEYS[kind]),
                            ((3, 1), q_parts, q_res, q_split, q_last, NT)):
                        if (b, u) == at and exists(g + 1):
                            wait_apart(pool, split_done[kind], g + 2, passed)
                            nc.gpsimd.tensor_tensor(parts[kind][:, 2, 0:cols], rest[:, 0:cols], parts[kind][:, 1, 0:cols],
                                                    ALU.subtract).then_inc(last_done[kind], 1)
                    if unit_of(kind, g, b, u, CROSS, G - 2) == 1:
                        router.row_ids()
                    if (i := unit_of(kind, g, b, u, SELF, G)) in IDLE_UNITS:
                        router.scatter([IDLE_UNITS.index(i)])
                    if (i := unit_of(kind, g, b, u, CROSS, G - 1)) is not None and 1 <= i < 1 + EARLY_SCATTERED - len(IDLE_UNITS):
                        router.scatter([len(IDLE_UNITS) - 1 + i])

        stages(pool, stage)

    return router


def routing(nc, ctx, t, x2_all, weights, counts_tab, rows_dram, banks, shared, tables, counts_early, early):
    sb = lambda n, s, d=fp32: ctx.enter_context(nc.sbuf_tensor(n, s, d))
    sem = lambda n: ctx.enter_context(nc.semaphore(n))
    i32 = mybir.dt.int32
    w2, b1, b2, moe_in = shared
    block_expert, block_row = counts_tab
    region = tables["region"]
    pad = sb("pad", [128, PADS, BLK // 128, ROW])
    LATE_TILES = NTILE - EARLY_TILES
    NG = LATE_TILES * E_
    router = Router(nc, sb, sb("late_slot", [128, TOPK, LATE_TILES], i32), sem, "late", EARLY_TILES, NTILE, x2_all, weights, tables, rows_dram, counts_early,
                    [sb(f"rb_rows{k}", [128, LATE_TILES, ROW])[:] for k in range(TOPK)],
                    banks[0:2], banks[2][:, 0:NG], banks[3][:, 0:NG], banks[3][:, NG:2 * NG], early)
    count_all = sb("r_count", [128, E_])
    step, consts, tri_set = sem("r_step"), sem("r_consts"), sem("r_tri_set")
    padded, last_count, count_done = sem("r_padded"), sem("r_last_count"), sem("r_count_done")
    jt = sb("r_jt", [1, 16]); nb3 = sb("r_nb3", [1, E_, 16]); nb = sb("r_nb", [1, E_])
    tri = sb("r_tri", [1, E_, E_]); end3 = sb("r_end3", [1, E_, E_]); end = sb("r_end", [1, E_]); start = sb("r_start", [1, E_])
    jb = sb("r_jb", [1, BLOCKS, E_]); past = sb("r_past", [1, BLOCKS, E_]); reached = sb("r_reached", [1, BLOCKS, E_])
    inside = sb("r_inside", [1, BLOCKS, E_]); base8 = sb("r_base8", [1, E_]); at8 = sb("r_at8", [1, BLOCKS, E_]); at8b = sb("r_at8b", [1, BLOCKS, E_])
    bexp = sb("r_bexp", [1, BLOCKS]); used = sb("r_used", [1, BLOCKS]); brow = sb("r_brow", [1, BLOCKS]); brow2 = sb("r_brow2", [1, BLOCKS])
    used0, spare, spare2 = (sb(f"r_{n}", [1, BLOCKS]) for n in ("used0", "spare", "spare2"))
    bexp2 = sb("r_bexp2", [1, BLOCKS]); brow3 = sb("r_brow3", [1, BLOCKS])
    pad_at = sb("r_pad_at", [1, E_]); pad_row = sb("r_pad_row", [1, E_], i32)
    CONSTS = 5

    with nc.Block() as block:
        @block.sync
        def _(sp):
            sp.dma_start(w2[:], t["L0_xattn_e_w2"].rearrange("e (c p) d -> p e c d", p=128)).then_inc(moe_in, 16)
            sp.dma_start(b1[:], t["L0_xattn_e_b1"].rearrange("e (c p) -> p e c", p=128),
                         allow_slow_non_contiguous=True).then_inc(moe_in, 16)
            sp.dma_start(b2[:], t["L0_xattn_e_b2"].partition_broadcast(128)).then_inc(moe_in, 16)
            sp.wait_ge(consts, CONSTS)
            sp.dma_start(rows_dram[NULL_ROW:NULL_ROW + SPARE * BLK].rearrange("(a p) r -> p a r", p=128),
                         pad[:, E_:PADS].rearrange("p n a r -> p (n a) r")).then_inc(padded, 16)
            sp.wait_ge(last_count, 1)
            for e in range(E_):
                at = sp.value_load(pad_row[0:1, e:e + 1], min_val=0, max_val=NULL_ROW - BLK)
                sp.dma_start(rows_dram[bass.ds(at, BLK)].rearrange("(a p) r -> p a r", p=128), pad[:, e]).then_inc(padded, 16)
            sp.wait_ge(padded, 16 * (E_ + 1))

        @block.gpsimd
        def _(pool):
            router.row_ids()
            nc.gpsimd.iota(jt[:], [[BLK, 16]], base=0, channel_multiplier=0, allow_small_or_imprecise_dtypes=True).then_inc(consts, 1)
            nc.gpsimd.memset(tri[:], 1.0).then_inc(tri_set, 1)
            pool.wait_ge(tri_set, 1)
            nc.gpsimd.affine_select(out=tri[:], in_=tri[:], compare_op=ALU.is_ge, fill=0.0, base=0,
                                    pattern=[[1, E_], [-1, E_]], channel_multiplier=0).then_inc(consts, 1)
            nc.gpsimd.iota(jb[:], [[1, BLOCKS], [0, E_]], base=0, channel_multiplier=0, allow_small_or_imprecise_dtypes=True).then_inc(consts, 1)
            nc.gpsimd.iota(pad[:, :, :, D:ROW].bitcast(i32), [[BLK, PADS], [128, BLK // 128], [0, 1]], base=TRASH,
                           channel_multiplier=1).then_inc(consts, 1)
            early.scatter(range(EARLY_SCATTERED, EARLY_TILES))
            router.scatter(range(LATE_TILES))
            router.await_(pool, "scattered", 16 * TOPK * LATE_TILES)

        @block.tensor
        def _(pe):
            for g in range(LATE_TILES // GB):
                router.turn(g)
                if g:
                    router.logits(g - 1)
            router.logits(LATE_TILES // GB - 1)
            router.counts()

        @block.scalar
        def _(act):
            for g in range(LATE_TILES // GB):
                router.copy_turned(g)
            for g in range(LATE_TILES // GB):
                router.copy_rows(g, 0)
            router.exp_logits()
            for g in range(LATE_TILES // GB):
                router.copy_rows(g, 1)
            router.exp_gap()

        @block.vector
        def _(dve):
            v = nc.vector
            links = [0]

            def link(op):
                links[0] += 1
                op.then_inc(step, 1)
                dve.wait_ge(step, links[0])

            v.memset(pad[:, :, :, 0:D], 0.0).then_inc(consts, 1)
            router.shift_logits()
            router.choose_best()
            router.choose_second()
            router.places(count_all)
            router.weigh()
            dve.wait_ge(consts, CONSTS)
            router.await_(dve, "counts_read", 1)
            count = count_all[0:1, :]
            link(v.tensor_tensor(pad_at[:], count, region[0:1], ALU.add))
            v.tensor_copy(pad_row[:], pad_at[:]).then_inc(last_count, 1)
            link(v.tensor_tensor(nb3[:], count.unsqueeze(2).to_broadcast([1, E_, 16]), jt[:].unsqueeze(1).to_broadcast([1, E_, 16]), ALU.is_gt))
            link(v.tensor_reduce(nb[:], nb3[:], AX.X, ALU.add))
            link(v.tensor_tensor(end3[:], tri[:], nb[:].unsqueeze(1).to_broadcast([1, E_, E_]), ALU.mult))
            link(v.tensor_reduce(end[:], end3[:], AX.X, ALU.add))
            link(v.tensor_tensor(start[:], end[:], nb[:], ALU.subtract))
            many = lambda ap: ap.unsqueeze(1).to_broadcast([1, BLOCKS, E_])
            link(v.tensor_tensor(past[:], jb[:], many(end[:]), ALU.is_ge))
            link(v.tensor_tensor(reached[:], jb[:], many(start[:]), ALU.is_ge))
            link(v.tensor_tensor(inside[:], reached[:], past[:], ALU.subtract))
            link(v.scalar_tensor_tensor(base8[:], start[:], -float(BLK), region[0:1], ALU.mult, ALU.add))
            link(v.scalar_tensor_tensor(at8[:], jb[:], float(BLK), many(base8[:]), ALU.mult, ALU.add))
            link(v.tensor_tensor(at8b[:], at8[:], inside[:], ALU.mult))
            v.tensor_reduce(brow[:], at8b[:], AX.X, ALU.add)
            v.tensor_reduce(used[:], inside[:], AX.X, ALU.add)
            link(v.tensor_reduce(bexp[:], past[:], AX.X, ALU.add))
            link(v.tensor_scalar(used0[:], used[:], -1.0, 1.0, ALU.mult, ALU.add))
            link(v.scalar_tensor_tensor(spare[:], jb[:, :, 0], end[:, E_ - 1:E_], used0[:], ALU.subtract, ALU.mult))
            link(v.tensor_scalar(spare2[:], spare[:], float(BLK), None, ALU.mult))
            link(v.scalar_tensor_tensor(brow2[:], used0[:], float(NULL_ROW), spare2[:], ALU.mult, ALU.add))
            link(v.tensor_tensor(brow3[:], brow2[:], brow[:], ALU.add))
            link(v.tensor_scalar(bexp2[:], bexp[:], float(E_ - 1), None, ALU.min))
            v.tensor_copy(block_row[:], brow3[:])
            link(v.tensor_copy(block_expert[:], bexp2[:]))


def experts(nc, ctx, t, x2_all, weights, counts_tab, rows_dram, out, banks, shared, tables):
    sb = lambda n, s, d=fp32: ctx.enter_context(nc.sbuf_tensor(n, s, d))
    sem = lambda n: ctx.enter_context(nc.semaphore(n))
    i32 = mybir.dt.int32
    block_expert, block_row = counts_tab
    two = lambda n, s, d=fp32: [sb(f"{n}{i}", s, d) for i in range(2)]
    w1 = two("w1_", [D, FF])
    w2, b1, b2, moe_in = shared
    ident = tables["ident"]
    xr = two("x_rows", [128, BLK // 128, ROW])
    xt = two("x_t", [D, BLK])
    hid = two("hidden", [128, FC, BLK])
    res = [sb(f"result{r}", [128, BLK // 128, D]) for r in range(4)]
    where = [sb(f"where{r}", [128, BLK // 128], i32) for r in range(4)]
    passed = sem("e_passed")
    w1_in = [sem(f"w1_in{i}") for i in range(2)]
    x_in = [sem(f"rows_in{i}") for i in range(2)]
    x_turned, x_copied, up_done, gelu_done, down_done, res_done, where_done = (sem(f"e_{n}") for n in (
        "x_turned", "x_copied", "up_done", "gelu_done", "down_done", "res_done", "where_done"))
    placed = [sem(f"e_placed{r}") for r in range(4)]
    xb, hb, yb = banks
    result_dram = nc.dram_tensor("result_dram", (TRASH + PADS * BLK, D), fp32, kind="Internal").ap()

    NT2 = BLK // 128
    LAST = BLOCKS - 1

    def turns(engine, body):
        for r in range(4):
            body(0, r)
        with engine.Fori(1, BLOCKS // 4) as n:
            for r in range(4):
                body(n, r)
        for r in range(BLOCKS % 4):
            body(BLOCKS // 4, r)

    def follower(n, r):
        return (n, r + 1) if r < 3 else (n + 1, 0)

    def is_last(n, r):
        return isinstance(n, int) and 4 * n + r == LAST

    def expert_of(engine, j):
        return engine.value_load(block_expert[0:1, bass.ds(j, 1)], min_val=0, max_val=E_ - 1)

    with nc.Block() as block:
        @block.sync
        def _(sp):
            def body(n, r):
                j, i = 4 * n + r, r % 2
                e = expert_of(sp, j)
                at = sp.value_load(block_row[0:1, bass.ds(j, 1)], min_val=0, max_val=NULL_ROW + (SPARE - 1) * BLK)
                wait(sp, x_turned, j - 1)
                wait(sp, where_done, j - 1)
                sp.dma_start(xr[i][:], rows_dram[bass.ds(at, BLK)].rearrange("(a p) r -> p a r", p=128)).then_inc(x_in[i], 16)
                wait(sp, up_done, FC * (j - 1))
                sp.dma_start(w1[i][:], t["L0_xattn_e_w1"][bass.ds(e, 1)].rearrange("a d f -> d (a f)")).then_inc(w1_in[i], 16)

            turns(sp, body)

        @block.tensor
        def _(pe):
            pe.wait_ge(moe_in, 48)

            def turn(n, r):
                j, i = 4 * n + r, r % 2
                pe.wait_ge(x_in[i], 16 * (2 * n + r // 2 + 1))
                wait(pe, x_copied, j - 1)
                for a in range(NT2):
                    mm = nc.tensor.transpose(xb[i][:, a * 128:(a + 1) * 128], xr[i][:, a, 0:D], ident[:])
                mm.then_inc(x_turned, 1)

            def up(n, r):
                j, i = 4 * n + r, r % 2
                pe.wait_ge(w1_in[i], 16 * (2 * n + r // 2 + 1))
                pe.wait_ge(x_copied, j + 1)
                for c in range(FC):
                    if c % 2 == 0:
                        wait(pe, gelu_done, FC * (j - 2) + c + 2)
                    nc.tensor.matmul(hb[2 * i + c // 2][:, c % 2 * BLK:(c % 2 + 1) * BLK], w1[i][:, c * 128:(c + 1) * 128], xt[i][:],
                                     start=True, stop=True).then_inc(up_done, 1)

            def down(n, r):
                j, i = 4 * n + r, r % 2
                e = expert_of(pe, j)
                pe.wait_ge(gelu_done, FC * (j + 1))
                wait(pe, res_done, j - 1)
                for a in range(NT2):
                    for c in range(FC):
                        mm = nc.tensor.matmul(yb[i][:, a * D:(a + 1) * D], hid[i][:, c, a * 128:(a + 1) * 128],
                                              w2[:, bass.ds(e, 1), c, :].rearrange("p a d -> p (a d)"), start=c == 0, stop=c == FC - 1)
                mm.then_inc(down_done, 1)

            def body(n, r):
                if not is_last(n, r):
                    if not is_last(*follower(n, r)):
                        turn(*follower(*follower(n, r)))
                    up(*follower(n, r))
                down(n, r)

            turn(0, 0)
            turn(0, 1)
            up(0, 0)
            turns(pe, body)

        @block.scalar
        def _(act):
            act.wait_ge(moe_in, 48)

            def body(n, r):
                j, i = 4 * n + r, r % 2
                e = expert_of(act, j)
                for c in range(FC):
                    act.wait_ge(up_done, FC * j + c + 1 if c % 2 else FC * j + c + 2)
                    if c == 0:
                        wait(act, down_done, j - 1)
                    nc.scalar.activation(hid[i][:, c, :], hb[2 * i + c // 2][:, c % 2 * BLK:(c % 2 + 1) * BLK], ACT.Gelu,
                                         bias=b1[:, bass.ds(e, 1), c]).then_inc(gelu_done, 1)

            turns(act, body)

        @block.vector
        def _(dve):
            def copy_x(n, r):
                j, i = 4 * n + r, r % 2
                dve.wait_ge(x_turned, j + 1)
                wait(dve, up_done, FC * (j - 1))
                nc.vector.tensor_copy(xt[i][:], xb[i][:, 0:BLK]).then_inc(x_copied, 1)
                wait(dve, placed[r], 16 * NT2 * n)
                nc.vector.tensor_copy(where[r][:], xr[i][:, :, D].bitcast(i32)).then_inc(where_done, 1)

            def finish(n, r):
                j, i = 4 * n + r, r % 2
                e = expert_of(dve, j)
                dve.wait_ge(down_done, j + 1)
                nc.vector.tensor_tensor(res[r][:], yb[i][:, 0:NT2 * D].rearrange("p (a d) -> p a d", d=D),
                                        b2[:, bass.ds(e, 1), :].to_broadcast([128, NT2, D]), ALU.add).then_inc(res_done, 1)

            def body(n, r):
                if not (is_last(n, r) or is_last(*follower(n, r))):
                    copy_x(*follower(*follower(n, r)))
                finish(n, r)

            dve.wait_ge(moe_in, 48)
            copy_x(0, 0)
            copy_x(0, 1)
            turns(dve, body)

        @block.gpsimd
        def _(pool):
            def body(n, r):
                j = 4 * n + r
                wait_apart(pool, res_done, j + 1, passed)
                wait_apart(pool, where_done, j + 1, passed)
                for a in range(NT2):
                    nc.gpsimd.indirect_dma_start(result_dram, bass.IndirectOffsetOnAxis(ap=where[r][:, a:a + 1], axis=0),
                                                 res[r][:, a, :], None).then_inc(placed[r], 16)

            turns(pool, body)
            for r in range(4):
                pool.wait_ge(placed[r], 16 * NT2 * ((BLOCKS + 3 - r) // 4))

    BUFS = 4
    assert G % BUFS == 0
    with ExitStack() as c2:
        sb = lambda n, s, d=fp32: c2.enter_context(nc.sbuf_tensor(n, s, d))
        sem = lambda n: c2.enter_context(nc.semaphore(n))
        y = [sb(f"f_y{g}", [128, TOPK, GB, D]) for g in range(G)]
        part, summed, zt, zg, outt = ([sb(f"f_{n}{i}", [128, GB, D]) for i in range(BUFS)] for n in ("part", "summed", "z", "zg", "out"))
        st, mv = [sb(f"f_st{i}", [128, GB, 6]) for i in range(BUFS)], [sb(f"f_mv{i}", [128, GB, 2]) for i in range(BUFS)]
        ve, rs = [sb(f"f_ve{i}", [128, GB]) for i in range(BUFS)], [sb(f"f_rs{i}", [128, GB]) for i in range(BUFS)]
        g_rows, b_rows, mh = sb("f_g", [128, D]), sb("f_b", [128, D]), sb("f_mh", [128, GB])
        nb = [sb(f"f_nb{i}", [128, GB]) for i in range(BUFS)]
        f_in = [sem(f"f_in{i}") for i in range(BUFS)]
        nb_done, mh_done = sem("f_nb_done"), sem("f_mh_done")
        c_in, part_done, sum_done, st_done, mv_done, ve_done, rs_done, z_done, zg_done, o_done = (sem(f"f_{n}") for n in (
            "c_in", "part_done", "sum_done", "st_done", "mv_done", "ve_done", "rs_done", "z_done", "zg_done", "o_done"))
        stored = [sem(f"f_stored{i}") for i in range(BUFS)]
        out_v = out.rearrange("(g b) s d -> g s b d", b=GB)
        with nc.Block() as block:
            @block.sync
            def _(sp):
                for g in range(G):
                    wait(sp, sum_done, GB * (g - BUFS + 1))
                    if g == 2:
                        sp.dma_start(g_rows[:], t["L0_xattn_ln3_g"].partition_broadcast(128)).then_inc(c_in, 16)
                        sp.dma_start(b_rows[:], t["L0_xattn_ln3_b"].partition_broadcast(128)).then_inc(c_in, 16)
                    for k in range(TOPK):
                        src = result_dram[k * TOK:(k + 1) * TOK].rearrange("(g j p) d -> g p j d", j=GB, p=128)[g]
                        sp.dma_start(y[g][:, k], src).then_inc(f_in[g % BUFS], 16)

                for g in range(G):
                    sp.wait_ge(o_done, g + 1)
                    sp.dma_start(out_v[g], outt[g % BUFS][:]).then_inc(stored[g % BUFS], 16)
                for i in range(BUFS):
                    sp.wait_ge(stored[i], 16 * G // BUFS)

            @block.vector
            def _(dve):
                v = nc.vector

                def offset(g):
                    dve.wait_ge(rs_done, g + 1)
                    v.scalar_tensor_tensor(nb[g % BUFS][:], mv[g % BUFS][:, :, 0], -1.0, rs[g % BUFS][:], ALU.mult, ALU.mult).then_inc(nb_done, 1)

                for g in range(G):
                    i = g % BUFS
                    dve.wait_ge(f_in[i], 16 * TOPK * (g // BUFS + 1))
                    wait(dve, z_done, g - BUFS + 1)
                    for j in range(GB):
                        op = v.scalar_tensor_tensor(part[i][:, j], y[g][:, 0, j], weights[:, 0, GB * g + j:GB * g + j + 1],
                                                    x2_all[:, GB * g + j], ALU.mult, ALU.add).then_inc(part_done, 1)
                    for j in range(GB):
                        dve.wait_ge(part_done, GB * g + j + 1)
                        v.scalar_tensor_tensor(summed[i][:, j], y[g][:, 1, j], weights[:, 1, GB * g + j:GB * g + j + 1],
                                               part[i][:, j], ALU.mult, ALU.add).then_inc(sum_done, 1)
                    for j in range(GB):
                        dve.wait_ge(sum_done, GB * g + j + 1)
                        v.bn_stats(st[i][:, j], summed[i][:, j]).then_inc(st_done, 1)
                    for j in range(GB):
                        dve.wait_ge(st_done, GB * g + j + 1)
                        op = v.bn_aggr(mv[i][:, j], st[i][:, j])
                    op.then_inc(mv_done, 1)
                    dve.wait_ge(mv_done, g + 1)
                    v.tensor_scalar(ve[i][:], mv[i][:, :, 1], EPS, None, ALU.add).then_inc(ve_done, 1)
                    if g:
                        offset(g - 1)
                offset(G - 1)

            @block.scalar
            def _(act):
                for g in range(G):
                    i = g % BUFS
                    act.wait_ge(nb_done, g + 1)
                    wait(act, zg_done, g - BUFS + 1)
                    for j in range(GB):
                        op = nc.scalar.activation(zt[i][:, j], summed[i][:, j], ACT.Identity, bias=nb[i][:, j:j + 1], scale=rs[i][:, j:j + 1])
                    op.then_inc(z_done, 1)

            @block.gpsimd
            def _(pool):
                nc.gpsimd.memset(mh[:], -0.5).then_inc(mh_done, 1)
                pool.wait_ge(mh_done, 1)
                rr = lambda ap: ap[:].unsqueeze(1).to_broadcast([128, GB, D])

                def deviation(g):
                    i = g % BUFS
                    pool.wait_ge(ve_done, g + 1)
                    nc.gpsimd.tensor_tensor(rs[i][:], ve[i][:], mh[:], ALU.pow).then_inc(rs_done, 1)

                deviation(0)
                pool.wait_ge(c_in, 32)
                for g in range(G):
                    i = g % BUFS
                    if g + 1 < G:
                        deviation(g + 1)
                    pool.wait_ge(z_done, g + 1)
                    nc.gpsimd.tensor_tensor(zg[i][:], zt[i][:], rr(g_rows), ALU.mult).then_inc(zg_done, 1)
                    pool.wait_ge(zg_done, g + 1)
                    wait(pool, stored[i], 16 * (g // BUFS))
                    nc.gpsimd.tensor_tensor(outt[i][:], zg[i][:], rr(b_rows), ALU.add).then_inc(o_done, 1)


def decoder_layer(nc, t, out):
    with ExitStack() as ctx:
        banks = [ctx.enter_context(nc.psum_tensor(f"bank{i}", [128, 512], fp32)) for i in range(8)]
        x2_all = ctx.enter_context(nc.sbuf_tensor("x2_all", [128, NTILE, D], fp32))
        weights = ctx.enter_context(nc.sbuf_tensor("weights", [128, TOPK, NTILE], fp32))
        tables = [ctx.enter_context(nc.sbuf_tensor(n, [1, BLOCKS], mybir.dt.int32)) for n in ("block_expert", "block_row")]
        rows_dram = nc.dram_tensor("rows_dram", (NULL_ROW + SPARE * BLK, ROW), fp32, kind="Internal").ap()
        sb = lambda n, s, d=fp32: ctx.enter_context(nc.sbuf_tensor(n, s, d))
        constants = {"ident": sb("ident", [128, 128]), "rw": sb("rw", [D, E_]), "rb_rows": sb("rb_rows", [128, E_]),
                     "earlier": sb("earlier", [128, 128], bf16), "ones_b": sb("ones_b", [128, 128], bf16),
                     "first_weight": sb("first_weight", [128, E_]), "region": sb("region", [128, E_])}
        counts_early = sb("counts_early", [128, E_])
        q_diag_self = sb("q_diag_self", [128, NP, 2, NT], bf16)
        second_rows = sb("second_rows", [128, EARLY_TILES, ROW])
        early_slot = sb("early_slot", [128, TOPK, EARLY_TILES], mybir.dt.int32)
        sem = lambda n: ctx.enter_context(nc.semaphore(n))
        with ExitStack() as part:
            early = attention(nc, part, t, x2_all, banks, weights, constants, rows_dram, counts_early, q_diag_self,
                              second_rows, early_slot, sem)
        with ExitStack() as moe:
            sb = lambda n, s: moe.enter_context(nc.sbuf_tensor(n, s, fp32))
            shared = (sb("w2_all", [128, E_, FC, D]), sb("b1_all", [128, E_, FC]), sb("b2_all", [128, E_, D]),
                      moe.enter_context(nc.semaphore("moe_in")))
            with ExitStack() as part:
                routing(nc, part, t, x2_all, weights, tables, rows_dram, banks[0:4], shared, constants, counts_early, early)
            with ExitStack() as part:
                experts(nc, part, t, x2_all, weights, tables, rows_dram, out, (banks[0:2], banks[2:6], banks[6:8]), shared, constants)


def kernel(**inputs):
    import numpy as _np
    import concourse.bacc as _bacc
    from concourse import mybir as _mybir
    from concourse.bass_utils import run_bass_kernel_spmd as _run

    nc = _bacc.Bacc("TRN2", target_bir_lowering=False, num_devices=1)
    arrays, t = {}, {}
    for name, a in inputs.items():
        a = _np.ascontiguousarray(a)
        arrays[f"in_{name}"] = a
        t[name] = nc.dram_tensor(f"in_{name}", a.shape, _mybir.dt.from_np(a.dtype), kind="ExternalInput").ap()
    out = nc.dram_tensor("out", (B, SQ, D), _mybir.dt.float32, kind="ExternalOutput").ap()
    decoder_layer(nc, t, out)
    r = _run(nc, [arrays], core_ids=[0])
    return r.results[0]["out"]
```
